# Optimizing a Trainium2 kernel written in Bass

```python
import numpy as np
import jax
import jax.numpy as jnp

def _softmax(x, axis=-1):
    return jax.nn.softmax(x, axis=axis)
def _gelu(x):
    return jax.nn.gelu(x, approximate=True)
def _silu(x):
    return jax.nn.silu(x)
def _sigmoid(x):
    return jax.nn.sigmoid(x)
def _layernorm(x, axis=-1, eps=1e-5):
    m = jnp.mean(x, axis=axis, keepdims=True)
    v = jnp.var(x, axis=axis, keepdims=True)
    return (x - m) / jnp.sqrt(v + eps)
def _scatter_add(tgt, idx, src, axis=0):
    return tgt.at[idx].add(src)
def _segment_sum(src, seg, n):
    return jax.ops.segment_sum(src, seg, n)

kernel_name = 'mk_adj_resnorm_d2_adj_256_ad6de9'

def setup_inputs(seed: int = 0):
    np.random.seed(seed)
    _w = jnp.asarray
    def _rec_inputs():
        import jax
        import jax.numpy as jnp
        _gk = jax.random.key(seed)
        x = -8.015e-05 + 0.9999 * jax.random.normal(jax.random.fold_in(_gk, 1), (16, 1024, 256), jnp.float32)
        _w = (1.0 + jnp.arange(1024, dtype=jnp.float32)) ** -0.5
        _w = _w / _w.mean()
        _pij = jnp.clip(0.03125 * _w[:, None] * _w[None, :], 0.0, 1.0)
        _a = jax.random.uniform(jax.random.fold_in(_gk, 2), (16, 1024, 1024)) < _pij
        _a = jnp.logical_or(_a, jnp.swapaxes(_a, -1, -2))
        _a = jnp.logical_or(_a, jnp.eye(1024, dtype=bool))
        _af = _a.astype(jnp.float32)
        _af = _af * jax.random.uniform(jax.random.fold_in(_gk, 3), (16, 1024, 1024), jnp.float32, 0.05, 0.999837)
        adj = _af
        return x, adj
    x, adj = _rec_inputs()
    def _L0_gnn_setup():
        import jax, jax.numpy as jnp
        import numpy as np
        GROUPS = [list(range(25)), [0, 1, 2, 3, 4, 5, 6, 7, 8], [0, 9, 10, 11, 12, 13, 14], [6, 7, 8, 12, 13, 14], [3, 4, 5, 9, 10, 11]]
        B, N, D_IN, D_HID = (8192, 25, 256, 512)

        def _graph_conv(x, adj, W, b):
            n = adj.shape[-1]
            A = adj + jnp.eye(n, dtype=adj.dtype)
            deg = jnp.sum(A, axis=-1)
            deg_safe = jnp.where(deg == 0, 1.0, deg)
            dinv = jnp.where(deg == 0, 0.0, deg_safe ** (-0.5))
            norm_adj = dinv[:, :, None] * A * dinv[:, None, :]
            support = jnp.einsum('bnd,de->bne', x, W)
            out = jnp.einsum('bnm,bme->bne', norm_adj, support) + b
            return jax.nn.relu(out)
        key = jax.random.key(seed)
        ks = jax.random.split(key, 7)
        s1 = float(np.sqrt(6.0 / (D_IN + D_HID)))
        s2 = float(np.sqrt(6.0 / (D_HID + D_IN)))
        return {'x': jax.random.normal(ks[0], (B, N, D_IN), dtype=jnp.float32), 'adj': jax.random.uniform(ks[1], (B, N, N), dtype=jnp.float32), 'W1': jax.random.uniform(ks[2], (5, D_IN, D_HID), jnp.float32, -s1, s1), 'b1': jnp.zeros((5, D_HID), dtype=jnp.float32), 'W2': jax.random.uniform(ks[3], (5, D_HID, D_IN), jnp.float32, -s2, s2), 'b2': jnp.zeros((5, D_IN), dtype=jnp.float32), 'fusion_w': jnp.ones((5,), dtype=jnp.float32)}
    _L0_gnn_all = _L0_gnn_setup()
    _L0_gnn_in = {k: v for k, v in _L0_gnn_all.items() if k in ('W1', 'b1', 'W2', 'b2', 'fusion_w', )}
    del _L0_gnn_all

    def _L1_gnn_setup():
        import jax, jax.numpy as jnp
        import numpy as np
        from jax import lax
        DIM = 256
        EPS = 1e-05

        def _bn(h, g, b, m, v):
            scale = g / jnp.sqrt(v + EPS)
            return h * scale[None, :, None] + (b - m * scale)[None, :, None]

        def _conv1d(h, w, pad):
            return lax.conv_general_dilated(h, w, window_strides=(1,), padding=[(pad, pad)], dimension_numbers=('NCH', 'OIH', 'NCH'))
        key = jax.random.key(seed)
        ks = jax.random.split(key, 16)
        bs, n, d = (16, 2048, DIM)
        s = 0.05
        return {'x': jax.random.normal(ks[0], (bs, n, d), jnp.float32), 'mask': jnp.ones((bs, n, n), jnp.float32), 'w_se': jax.random.normal(ks[1], (3, d), jnp.float32) * s, 'b_se': jnp.zeros((3,), jnp.float32), 'conv1_w': jax.random.normal(ks[2], (d, d, 1), jnp.float32) * s, 'bn1_g': jnp.ones((d,), jnp.float32), 'bn1_b': jnp.zeros((d,), jnp.float32), 'bn1_m': jnp.zeros((d,), jnp.float32), 'bn1_v': jnp.ones((d,), jnp.float32), 'conv2_w': jax.random.normal(ks[3], (d, d, 17), jnp.float32) * s, 'bn2_g': jnp.ones((d,), jnp.float32), 'bn2_b': jnp.zeros((d,), jnp.float32), 'bn2_m': jnp.zeros((d,), jnp.float32), 'bn2_v': jnp.ones((d,), jnp.float32), 'w_msg': jax.random.normal(ks[4], (d, d), jnp.float32) * s, 'b_msg': jnp.zeros((d,), jnp.float32), 'w_ih': jax.random.normal(ks[5], (3 * d, 2 * d), jnp.float32) * s, 'b_ih': jnp.zeros((3 * d,), jnp.float32), 'w_hh': jax.random.normal(ks[6], (3 * d, d), jnp.float32) * s, 'b_hh': jnp.zeros((3 * d,), jnp.float32)}
    _L1_gnn_all = _L1_gnn_setup()
    _L1_gnn_in = {k: v for k, v in _L1_gnn_all.items() if k in ('w_se', 'b_se', 'conv1_w', 'bn1_g', 'bn1_b', 'bn1_m', 'bn1_v', 'conv2_w', 'bn2_g', 'bn2_b', 'bn2_m', 'bn2_v', 'w_msg', 'b_msg', 'w_ih', 'b_ih', 'w_hh', 'b_hh', )}
    del _L1_gnn_all

    return {
        "x": x,
        "adj": adj,
        "L0_gnn_W1": _L0_gnn_in["W1"],
        "L0_gnn_b1": _L0_gnn_in["b1"],
        "L0_gnn_W2": _L0_gnn_in["W2"],
        "L0_gnn_b2": _L0_gnn_in["b2"],
        "L0_gnn_fusion_w": _L0_gnn_in["fusion_w"],
        "L1_gnn_w_se": _L1_gnn_in["w_se"],
        "L1_gnn_b_se": _L1_gnn_in["b_se"],
        "L1_gnn_conv1_w": _L1_gnn_in["conv1_w"],
        "L1_gnn_bn1_g": _L1_gnn_in["bn1_g"],
        "L1_gnn_bn1_b": _L1_gnn_in["bn1_b"],
        "L1_gnn_bn1_m": _L1_gnn_in["bn1_m"],
        "L1_gnn_bn1_v": _L1_gnn_in["bn1_v"],
        "L1_gnn_conv2_w": _L1_gnn_in["conv2_w"],
        "L1_gnn_bn2_g": _L1_gnn_in["bn2_g"],
        "L1_gnn_bn2_b": _L1_gnn_in["bn2_b"],
        "L1_gnn_bn2_m": _L1_gnn_in["bn2_m"],
        "L1_gnn_bn2_v": _L1_gnn_in["bn2_v"],
        "L1_gnn_w_msg": _L1_gnn_in["w_msg"],
        "L1_gnn_b_msg": _L1_gnn_in["b_msg"],
        "L1_gnn_w_ih": _L1_gnn_in["w_ih"],
        "L1_gnn_b_ih": _L1_gnn_in["b_ih"],
        "L1_gnn_w_hh": _L1_gnn_in["w_hh"],
        "L1_gnn_b_hh": _L1_gnn_in["b_hh"],
    }

def reference(x, adj, L0_gnn_W1, L0_gnn_b1, L0_gnn_W2, L0_gnn_b2, L0_gnn_fusion_w, L1_gnn_w_se, L1_gnn_b_se, L1_gnn_conv1_w, L1_gnn_bn1_g, L1_gnn_bn1_b, L1_gnn_bn1_m, L1_gnn_bn1_v, L1_gnn_conv2_w, L1_gnn_bn2_g, L1_gnn_bn2_b, L1_gnn_bn2_m, L1_gnn_bn2_v, L1_gnn_w_msg, L1_gnn_b_msg, L1_gnn_w_ih, L1_gnn_b_ih, L1_gnn_w_hh, L1_gnn_b_hh):
    import jax
    import jax.numpy as jnp
    def _L0_gnn_ref(x, adj, W1, b1, W2, b2, fusion_w):
        import jax, jax.numpy as jnp
        import numpy as np
        GROUPS = [list(range(25)), [0, 1, 2, 3, 4, 5, 6, 7, 8], [0, 9, 10, 11, 12, 13, 14], [6, 7, 8, 12, 13, 14], [3, 4, 5, 9, 10, 11]]
        B, N, D_IN, D_HID = (8192, 25, 256, 512)

        def _graph_conv(x, adj, W, b):
            n = adj.shape[-1]
            A = adj + jnp.eye(n, dtype=adj.dtype)
            deg = jnp.sum(A, axis=-1)
            deg_safe = jnp.where(deg == 0, 1.0, deg)
            dinv = jnp.where(deg == 0, 0.0, deg_safe ** (-0.5))
            norm_adj = dinv[:, :, None] * A * dinv[:, None, :]
            support = jnp.einsum('bnd,de->bne', x, W)
            out = jnp.einsum('bnm,bme->bne', norm_adj, support) + b
            return jax.nn.relu(out)
        norm_w = jax.nn.softmax(fusion_w)
        fused = jnp.zeros_like(x)
        for g, idx_list in enumerate(GROUPS):
            idx = jnp.asarray(idx_list)
            x_g = x[:, idx, :]
            adj_g = adj[:, idx][:, :, idx]
            h = _graph_conv(x_g, adj_g, W1[g], b1[g])
            out_g = _graph_conv(h, adj_g, W2[g], b2[g])
            fused = fused.at[:, idx, :].add(norm_w[g] * out_g)
        return fused

    def _L1_gnn_ref(x, mask, w_se, b_se, conv1_w, bn1_g, bn1_b, bn1_m, bn1_v, conv2_w, bn2_g, bn2_b, bn2_m, bn2_v, w_msg, b_msg, w_ih, b_ih, w_hh, b_hh):
        import jax, jax.numpy as jnp
        import numpy as np
        from jax import lax
        DIM = 256
        EPS = 1e-05

        def _bn(h, g, b, m, v):
            scale = g / jnp.sqrt(v + EPS)
            return h * scale[None, :, None] + (b - m * scale)[None, :, None]

        def _conv1d(h, w, pad):
            return lax.conv_general_dilated(h, w, window_strides=(1,), padding=[(pad, pad)], dimension_numbers=('NCH', 'OIH', 'NCH'))
        d = x.shape[-1]
        xc = jnp.transpose(x, (0, 2, 1))
        h = _bn(_conv1d(xc, conv1_w, 0), bn1_g, bn1_b, bn1_m, bn1_v)
        h = jax.nn.relu(h)
        h = _bn(_conv1d(h, conv2_w, 8), bn2_g, bn2_b, bn2_m, bn2_v)
        x_conv = jnp.transpose(jax.nn.relu(h + xc), (0, 2, 1))
        s = x @ w_se.T + b_se
        sq = jnp.sum(s * s, axis=-1)
        dist = sq[:, :, None] + sq[:, None, :] - 2.0 * jnp.einsum('bnd,bmd->bnm', s, s)
        A = jnp.exp(-dist) * mask
        msg = jax.nn.relu(x @ w_msg.T + b_msg)
        x_nmp = jnp.einsum('bnm,bmd->bnd', A, msg)
        x_in = jnp.concatenate([x_conv, x_nmp], axis=-1)
        gi = x_in @ w_ih.T + b_ih
        gh = x @ w_hh.T + b_hh
        gi_r, gi_z, gi_n = (gi[..., :d], gi[..., d:2 * d], gi[..., 2 * d:])
        gh_r, gh_z, gh_n = (gh[..., :d], gh[..., d:2 * d], gh[..., 2 * d:])
        r = jax.nn.sigmoid(gi_r + gh_r)
        z = jax.nn.sigmoid(gi_z + gh_z)
        nn_ = jnp.tanh(gi_n + r * gh_n)
        return (1.0 - z) * nn_ + z * x

    x = _layernorm(x + _L0_gnn_ref(x, adj, L0_gnn_W1, L0_gnn_b1, L0_gnn_W2, L0_gnn_b2, L0_gnn_fusion_w), axis=-1)
    x = _layernorm(x + _L1_gnn_ref(x, adj, L1_gnn_w_se, L1_gnn_b_se, L1_gnn_conv1_w, L1_gnn_bn1_g, L1_gnn_bn1_b, L1_gnn_bn1_m, L1_gnn_bn1_v, L1_gnn_conv2_w, L1_gnn_bn2_g, L1_gnn_bn2_b, L1_gnn_bn2_m, L1_gnn_bn2_v, L1_gnn_w_msg, L1_gnn_b_msg, L1_gnn_w_ih, L1_gnn_b_ih, L1_gnn_w_hh, L1_gnn_b_hh), axis=-1)
    return x


_drawn_inputs = setup_inputs


def setup_inputs(seed=0):
    import zlib

    import numpy as np

    out = dict(_drawn_inputs(seed))
    spreads = {'L0_gnn_b1': (0.0, 0.8),
     'L0_gnn_b2': (0.0, 0.8),
     'L0_gnn_fusion_w': (1.0, 0.6),
     'L1_gnn_b_se': (0.0, 0.8),
     'L1_gnn_bn1_g': (1.0, 0.2),
     'L1_gnn_bn1_b': (0.0, 0.1),
     'L1_gnn_bn1_m': (0.0, 0.1),
     'L1_gnn_bn1_v': (1.0, 0.576),
     'L1_gnn_bn2_g': (1.0, 0.2),
     'L1_gnn_bn2_b': (0.0, 0.631),
     'L1_gnn_bn2_m': (0.0, 0.517),
     'L1_gnn_bn2_v': (1.0, 0.6),
     'L1_gnn_b_msg': (0.0, 0.1),
     'L1_gnn_b_ih': (0.0, 0.357),
     'L1_gnn_b_hh': (0.0, 0.445)}
    factors = {'L0_gnn_W1': 8.0, 'L0_gnn_W2': 8.0}
    for name, (base, spread) in spreads.items():
        noise = np.random.default_rng([zlib.crc32(name.encode()), seed]).standard_normal(out[name].shape)
        drawn = base * np.exp(spread * noise) if base else spread * noise
        out[name] = jnp.asarray(drawn.astype(out[name].dtype))
    for name, factor in factors.items():
        out[name] = (out[name] * factor).astype(out[name].dtype)
    return out
```

```python
from contextlib import ExitStack

import numpy as np

import concourse.bass as bass
from concourse import mybir

P = 128
B, N, D = 16, 1024, 256
DC = D // P
NT = N // P
H2 = N // 2
DH = 512
HC = DH // P
GROUPS = [list(range(25)), [0, 1, 2, 3, 4, 5, 6, 7, 8], [0, 9, 10, 11, 12, 13, 14],
          [6, 7, 8, 12, 13, 14], [3, 4, 5, 9, 10, 11]]
NG = len(GROUPS)
GN = 25
GP = 32
GB = P // GP
GT = B // GB
TAPS, PAD = 17, 8
HW = N + 2 * PAD
EPS = 1e-5
SELW = 64

F32 = mybir.dt.float32
F32R = mybir.dt.float32r
ALU = mybir.AluOpType
ACT = mybir.ActivationFunctionType
AX = mybir.AxisListType.X


class Space:

    def __init__(self, nc, ctx, tag):
        self.nc, self.ctx, self.tag = nc, ctx, tag

    def sb(self, name, shape, dt=F32):
        return self.ctx.enter_context(self.nc.sbuf_tensor(f"{self.tag}_{name}", shape, dt))

    def bank(self, name):
        return self.ctx.enter_context(self.nc.psum_tensor(f"{self.tag}_{name}", [P, 512], F32))

    def sem(self, name):
        return self.ctx.enter_context(self.nc.semaphore(f"{self.tag}_{name}"))


def products(nc, out, pairs, start=True, stop=True):
    last = None
    steps = [(a, b) for ah, al, bh, bl in pairs for a, b in ((ah, bh), (ah, bl), (al, bh))]
    for k, (a, b) in enumerate(steps):
        last = nc.tensor.matmul(out, a, b, start=start and k == 0, stop=stop and k == len(steps) - 1)
    return last


class Turn:

    def __init__(self, i, a=1, c=0):
        self.i, self.a, self.c = i, a, c

    def __add__(self, k):
        return Turn(self.i, self.a, self.c + k)

    def __sub__(self, k):
        return self + -k

    def __mul__(self, k):
        return Turn(self.i, self.a * k, self.c * k)

    __radd__, __rmul__ = __add__, __mul__


def val(n):
    return n.i * n.a + n.c if isinstance(n, Turn) else n


def groups_stage(nc, t):
    with ExitStack() as ctx:
        m = Space(nc, ctx, "g")
        x0 = m.sb("x0", [P, GT, D])
        adj0 = m.sb("adj0", [P, GT, P])
        gmask = m.sb("gmask", [P, NG, P])
        geye = m.sb("geye", [P, NG, P])
        member = m.sb("member", [P, NG])
        ident = m.sb("ident", [P, P])
        w1 = m.sb("w1", [P, NG, DC, DH])
        w2 = m.sb("w2", [P, NG, HC, D])
        b1 = m.sb("b1", [P, NG, HC])
        b2 = m.sb("b2", [P, NG, D])
        fw = m.sb("fw", [P, NG])
        A = m.sb("A", [P, NG, GT, P])
        nadjT = m.sb("nadjT", [P, NG, GT, P])
        deg = m.sb("deg", [P, NG * GT])
        deg0 = m.sb("deg0", [P, NG * GT])
        dsafe = m.sb("dsafe", [P, NG * GT])
        dpow = m.sb("dpow", [P, NG * GT])
        dhave = m.sb("dhave", [P, NG * GT])
        dinv = m.sb("dinv", [P, NG * GT])
        half = m.sb("half", [P, NG * GT])
        wmax = m.sb("wmax", [P, 1])
        wexp = m.sb("wexp", [P, NG])
        wsum = m.sb("wsum", [P, 1])
        wrec = m.sb("wrec", [P, 1])
        wsm = m.sb("wsm", [P, NG])
        wmem = m.sb("wmem", [P, NG])
        xaT = m.sb("xaT", [P, DC, 512])
        hT = m.sb("hT", [P, HC, 512])
        sup2 = m.sb("sup2", [P, GT, D])
        pre = m.sb("pre", [P, D])
        act2 = m.sb("act2", [P, D])
        fused = m.sb("fused", [P, GT, D])

        pT = [m.bank(f"pT{k}") for k in range(2)]
        pX = [m.bank(f"pX{k}") for k in range(2)]
        pH = [m.bank(f"pH{k}") for k in range(2)]
        pS = [m.bank(f"pS{k}") for k in range(2)]

        ld = m.sem("loaded")
        ldw = m.sem("weights_loaded")
        st = m.sem("fused_stored")
        dve = m.sem("dve_chain")
        halfs = m.sem("half_set")
        pw = m.sem("powered")
        an = m.sem("adj_normed_rows")
        tr = m.sem("adj_transposed")
        nt = m.sem("nadjT_ready")
        we = m.sem("weights_exp")
        wm = m.sem("weights_max")
        xm = m.sem("xa_multiplied")
        xr = m.sem("xaT_ready")
        hm = m.sem("h_multiplied")
        hr = m.sem("hT_ready")
        sm = m.sem("sup2_multiplied")
        sr = m.sem("sup2_ready")
        om = m.sem("out_multiplied")
        orr = m.sem("out_read")
        fr = m.sem("fused_ready")

        with nc.Block() as block:
            @block.sync
            def _(sp):
                for dst, src in ((adj0, t["l0_adj"]), (gmask, t["l0_gmask"]), (geye, t["l0_geye"]),
                                 (member, t["l0_member"]), (fw, t["l0_fw"]), (ident, t["ident"]), (x0, t["l0_x"])):
                    sp.dma_start(dst[:], src).then_inc(ld, 16)
                for dst, src in ((w1, t["l0_w1"]), (b1, t["l0_b1"]), (w2, t["l0_w2"]), (b2, t["l0_b2"])):
                    sp.dma_start(dst[:], src).then_inc(ldw, 16)
                for b in range(B):
                    k, q = divmod(b, GB)
                    sp.wait_ge(fr, k + 1)
                    sp.dma_start(t["fused"][val(b)], fused[GP * q:GP * q + GN, k, :]).then_inc(st, 16)
                sp.wait_ge(st, 16 * B)

            @block.gpsimd
            def _(pool):
                nc.gpsimd.memset(half[:, :], -0.5).then_inc(halfs, 1)
                pool.wait_ge(halfs, 1)
                pool.wait_ge(dve, 4)
                nc.gpsimd.tensor_tensor(dpow[:, :], dsafe[:, :], half[:, :], ALU.pow).then_inc(pw, 1)

            @block.scalar
            def _(act):
                act.wait_ge(wm, 1)
                nc.scalar.activation(wexp[:, :], fw[:, :], ACT.Exp, bias=wmax[:, :],
                                     accum_out=wsum[:, :]).then_inc(we, 1)
                for g in range(NG):
                    for c in range(DC):
                        act.wait_ge(xm, val(g * DC + c + 1))
                        if g:
                            act.wait_ge(hm, val(HC * g))
                        nc.scalar.copy(xaT[:, c, :], pX[c][:, :]).then_inc(xr, 1)
                    act.wait_ge(ldw, 64)
                    for e in range(HC):
                        act.wait_ge(hm, val(g * HC + e + 1))
                        if g:
                            act.wait_ge(sm, val(GT * g))
                        nc.scalar.activation(hT[:, e, :], pH[e % 2][:, :], ACT.Relu,
                                             bias=b1[:, g, e:e + 1]).then_inc(hr, 1)
                    for k in range(GT):
                        act.wait_ge(sm, val(g * GT + k + 1))
                        if g:
                            act.wait_ge(om, val(GT * (g - 1) + k + 1))
                        nc.scalar.copy(sup2[:, k, :], pS[k % 2][:, 0:D]).then_inc(sr, 1)

            @block.vector
            def _(v):
                n = [0]

                def link(ins):
                    n[0] += 1
                    ins.then_inc(dve, 1)
                    v.wait_ge(dve, val(n[0]))

                v.wait_ge(ld, 16 * 7)
                for g in range(NG):
                    Ag = A[:, g, :, :]
                    ins = nc.vector.tensor_tensor(Ag, adj0[:, :, :], gmask[:, g, :].unsqueeze(1).to_broadcast([P, GT, P]), ALU.mult)
                link(ins)
                for g in range(NG):
                    Ag = A[:, g, :, :]
                    ins = nc.vector.tensor_tensor(Ag, Ag, geye[:, g, :].unsqueeze(1).to_broadcast([P, GT, P]), ALU.add)
                link(ins)
                link(nc.vector.tensor_reduce(deg[:, :], A[:].rearrange("p g t n -> p (g t) n"), axis=AX, op=ALU.add))
                nc.vector.tensor_scalar(deg0[:, :], deg[:, :], 0.0, None, ALU.is_equal).then_inc(halfs, 1)
                v.wait_ge(halfs, 2)
                link(nc.vector.tensor_tensor(dsafe[:, :], deg[:, :], deg0[:, :], ALU.add))
                link(nc.vector.tensor_scalar(dhave[:, :], deg0[:, :], -1.0, 1.0, ALU.mult, ALU.add))
                v.wait_ge(pw, 1)
                link(nc.vector.tensor_tensor(dinv[:, :], dpow[:, :], dhave[:, :], ALU.mult))
                for g in range(NG):
                    for k in range(GT):
                        j = g * GT + k
                        nc.vector.tensor_scalar(A[:, g, k, :], A[:, g, k, :], dinv[:, j:j + 1], None, ALU.mult).then_inc(an, 1)
                link(nc.vector.tensor_reduce(wrec[:, :], fw[:, :], axis=AX, op=ALU.max))
                nc.vector.tensor_scalar(wmax[:, :], wrec[:, :], -1.0, None, ALU.mult).then_inc(wm, 1)
                v.wait_ge(wm, 1)
                for j in range(NG * GT):
                    g, k = divmod(j, GT)
                    v.wait_ge(tr, val(j + 1))
                    nc.vector.tensor_scalar(nadjT[:, g, k, :], pT[j % 2][:, 0:P], dinv[:, j:j + 1], None, ALU.mult).then_inc(nt, 1)
                v.wait_ge(we, 1)
                link(nc.vector.reciprocal(wrec[:, :], wsum[:, :]))
                link(nc.vector.tensor_scalar(wsm[:, :], wexp[:, :], wrec[:, :], None, ALU.mult))
                link(nc.vector.tensor_tensor(wmem[:, :], wsm[:, :], member[:, :], ALU.mult))
                v.wait_ge(ldw, 64)
                for g in range(NG):
                    for k in range(GT):
                        v.wait_ge(om, val(g * GT + k + 1))
                        ins = nc.vector.tensor_tensor(pre[:, :], pT[k % 2][:, 0:D], b2[:, g, :], ALU.add)
                        ins.then_inc(orr, 1)
                        v.wait_ge(orr, val(g * GT + k + 1))
                        link(nc.vector.tensor_scalar(act2[:, :], pre[:, :], 0.0, wmem[:, g:g + 1], ALU.max, ALU.mult))
                        if g == 0:
                            ins = nc.vector.tensor_copy(fused[:, k, :], act2[:, :])
                        else:
                            ins = nc.vector.tensor_tensor(fused[:, k, :], fused[:, k, :], act2[:, :], ALU.add)
                        if g == NG - 1:
                            ins.then_inc(fr, 1)
                            v.wait_ge(fr, k + 1)
                        else:
                            link(ins)

            @block.tensor
            def _(pe):
                pe.wait_ge(ld, 16 * 7)
                for j in range(NG * GT):
                    g, k = divmod(j, GT)
                    pe.wait_ge(an, val(j + 1))
                    if j >= 2:
                        pe.wait_ge(nt, val(j - 1))
                    nc.tensor.transpose(pT[j % 2][:, 0:P], A[:, g, k, :], ident[:, :]).then_inc(tr, 1)
                pe.wait_ge(nt, NG * GT)
                pe.wait_ge(ldw, 64)
                for g in range(NG):
                    for c in range(DC):
                        if g:
                            pe.wait_ge(xr, val((g - 1) * DC + c + 1))
                        for k in range(GT):
                            ins = nc.tensor.matmul(pX[c][:, k * P:(k + 1) * P], x0[:, k, c * P:(c + 1) * P],
                                                   nadjT[:, g, k, :], start=True, stop=True)
                        ins.then_inc(xm, 1)
                    pe.wait_ge(xr, val((g + 1) * DC))
                    for e in range(HC):
                        if g * HC + e >= 2:
                            pe.wait_ge(hr, val(g * HC + e - 1))
                        for c in range(DC):
                            ins = nc.tensor.matmul(pH[e % 2][:, :], w1[:, g, c, e * P:(e + 1) * P], xaT[:, c, :],
                                                   start=c == 0, stop=c == DC - 1)
                        ins.then_inc(hm, 1)
                    pe.wait_ge(hr, val((g + 1) * HC))
                    for k in range(GT):
                        if g * GT + k >= 2:
                            pe.wait_ge(sr, val(g * GT + k - 1))
                        for e in range(HC):
                            ins = nc.tensor.matmul(pS[k % 2][:, 0:D], hT[:, e, k * P:(k + 1) * P], w2[:, g, e, :],
                                                   start=e == 0, stop=e == HC - 1)
                        ins.then_inc(sm, 1)
                    for k in range(GT):
                        pe.wait_ge(sr, val(g * GT + k + 1))
                        if g * GT + k >= 2:
                            pe.wait_ge(orr, val(g * GT + k - 1))
                        nc.tensor.matmul(pT[k % 2][:, 0:D], nadjT[:, g, k, :], sup2[:, k, :],
                                         start=True, stop=True).then_inc(om, 1)


def conv_stage(nc, t):
    with ExitStack() as ctx:
        m = Space(nc, ctx, "c")
        ident = m.sb("ident", [P, P])
        wstage = m.sb("wstage", [P, 2, TAPS, P])
        w1stage = m.sb("w1stage", [P, DC, D])
        w2hi = m.sb("w2hi", [P, DC, TAPS, D], F32R)
        w2lo = m.sb("w2lo", [P, DC, TAPS, D], F32R)
        w1hi = m.sb("w1hi", [P, DC, D], F32R)
        w1lo = m.sb("w1lo", [P, DC, D], F32R)
        bn = m.sb("bn", [P, 2, 4, DC])
        bnp = m.sb("bnp", [P, 2, DC])
        scale = m.sb("scale", [P, 2, DC])
        shift = m.sb("shift", [P, 2, DC])
        half = m.sb("half", [P, NT])
        xin = m.sb("xin", [P, 2, NT, D])
        fus = m.sb("fus", [GN, 2, D])
        stats = m.sb("stats", [P, NT, 6])
        mv = m.sb("mv", [P, NT, 2])
        mark = m.sb("mark", [P, 1])
        veps = m.sb("veps", [P, NT])
        rstd = m.sb("rstd", [P, NT])
        xT = m.sb("xT", [P, 2, DC, N])
        xhi = m.sb("xhi", [P, DC, N], F32R)
        xlo = m.sb("xlo", [P, DC, N], F32R)
        h32 = m.sb("h32", [P, 2, H2])
        hhi = m.sb("hhi", [P, 2, DC, HW], F32R)
        hlo = m.sb("hlo", [P, 2, DC, HW], F32R)
        yt = m.sb("yt", [P, 2, H2])
        xc = m.sb("xc", [P, 2, H2])

        pT = [m.bank(f"pT{k}") for k in range(2)]
        pH = [m.bank(f"pH{k}") for k in range(2)]
        pY = [m.bank(f"pY{k}") for k in range(2)]

        ld = m.sem("constants_loaded")
        wl = [m.sem(f"tap_weights_loaded{k}") for k in range(2)]
        wh = m.sem("tap_weights_hi")
        wo = m.sem("tap_weights_lo")
        cw = m.sem("conv1_weights_split")
        chain = m.sem("dve_setup_chain")
        pows = m.sem("bn_powered")
        hset = m.sem("half_set")
        pads = m.sem("pads_zeroed")
        x_ld = [m.sem(f"x_loaded{k}") for k in range(2)]
        x_st = [m.sem(f"x1_stored{k}") for k in range(2)]
        xT_st = [m.sem(f"x1T_stored{k}") for k in range(2)]
        c_st = [m.sem(f"xc_stored{k}") for k in range(2)]
        fadd = m.sem("fused_added")
        bst = m.sem("bn_stats_done")
        bag = m.sem("mean_var_done")
        vep = m.sem("var_eps_done")
        rst = m.sem("rstd_done")
        x1r = m.sem("x1_ready")
        tr = m.sem("x1_transposed")
        xTr = m.sem("x1T_ready")
        xhr = m.sem("x1T_hi_ready")
        xlr = m.sem("x1T_lo_ready")
        c1 = m.sem("conv1_multiplied")
        h3 = m.sem("h_ready")
        hh = m.sem("h_hi_ready")
        hl = m.sem("h_lo_ready")
        c2 = m.sem("conv2_multiplied")
        yr = m.sem("conv2_read")
        xcr = m.sem("xc_ready")

        LAST = B - 1
        first = lambda j: isinstance(j, int) and j == 0

        def schedule(body, eng):
            body(0, 0, True)
            with eng.Fori(0, B // 2 - 1) as turn:
                i = Turn(turn)
                for k in range(2):
                    body(2 * i + k + 1, 1 - k, True)
            body(LAST, 1, False)

        QC = [(co, nh) for co in range(DC) for nh in range(2)]

        with nc.Block() as block:
            @block.sync
            def _(sp):
                sp.dma_start(ident[:], t["ident"]).then_inc(ld, 16)
                sp.dma_start(bn[:], t["bn"]).then_inc(ld, 16)
                sp.dma_start(w1stage[:], t["conv1_w"]).then_inc(ld, 16)

                def load(j, s):
                    if not (isinstance(j, int) and j < 2):
                        sp.wait_ge(x_st[s], val(8 * j - 8 * s))
                        sp.wait_ge(tr, val(4 * j - 4))
                    sp.dma_start(xin[:, s, :, :], t["x"][val(j)]).then_inc(x_ld[s], 16)
                    sp.dma_start(fus[:, s, :], t["fused"][val(j)]).then_inc(x_ld[s], 16)

                def store_prep(j, s):
                    sp.wait_ge(x1r, val(NT * j + NT))
                    sp.dma_start(t["x1"][val(j)], xin[:, s, :, :]).then_inc(x_st[s], 16)
                    sp.wait_ge(xTr, val(4 * j + 4))
                    sp.dma_start(t["x1T"][val(j)], xT[:, s, :, :]).then_inc(xT_st[s], 16)

                def store_conv(j):
                    for q, (co, nh) in enumerate(QC):
                        sp.wait_ge(xcr, val(4 * j + q + 1))
                        sp.dma_start(t["xcT"][val(j)][:, co, nh * H2:(nh + 1) * H2], xc[:, q % 2, :]).then_inc(c_st[q % 2], 16)

                load(0, 0)
                for k in range(4):
                    ci, co = divmod(k, 2)
                    if k >= 2:
                        sp.wait_ge(wo, k - 1)
                    sp.dma_start(wstage[:, k % 2], t["conv2_w"][:, ci, :, co * P:(co + 1) * P]).then_inc(wl[k % 2], 16)
                store_prep(0, 0)

                def body(b, s, nxt):
                    if nxt:
                        load(b + 1, 1 - s)
                        store_prep(b + 1, 1 - s)
                    store_conv(b)

                schedule(body, sp)
                for s in range(2):
                    sp.wait_ge(x_st[s], 8 * B)
                    sp.wait_ge(xT_st[s], 8 * B)
                    sp.wait_ge(c_st[s], 32 * B)

            @block.gpsimd
            def _(pool):
                nc.gpsimd.memset(half[:, :], -0.5).then_inc(hset, 1)
                for hx in (hhi, hlo):
                    for s in range(2):
                        for c in range(DC):
                            nc.gpsimd.memset(hx[:, s, c, 0:PAD].bitcast(F32), 0.0).then_inc(pads, 1)
                            nc.gpsimd.memset(hx[:, s, c, PAD + N:HW].bitcast(F32), 0.0).then_inc(pads, 1)
                pool.wait_ge(hset, 1)
                pool.wait_ge(chain, 1)
                nc.gpsimd.tensor_tensor(bnp[:].rearrange("p a c -> p (a c)"), scale[:].rearrange("p a c -> p (a c)"),
                                        half[:, 0:2 * DC], ALU.pow).then_inc(pows, 1)

                def prep(j, s):
                    pool.wait_ge(vep, val(j + 1))
                    if not (isinstance(j, int) and j == 0):
                        pool.wait_ge(x1r, val(NT * j))
                    nc.gpsimd.tensor_tensor(rstd[:, :], veps[:, :], half[:, :], ALU.pow).then_inc(rst, 1)
                    for q in range(4):
                        ci, nh = divmod(q, 2)
                        pool.wait_ge(xTr, val(4 * j + q + 1))
                        pool.wait_ge(xhr, val(4 * j + q + 1))
                        if not (isinstance(j, int) and j == 0):
                            pool.wait_ge(c1, val(4 * j))
                        sl = slice(nh * H2, (nh + 1) * H2)
                        nc.gpsimd.tensor_tensor(xlo[:, ci, sl], xT[:, s, ci, sl], xhi[:, ci, sl].bitcast(F32),
                                                ALU.subtract).then_inc(xlr, 1)

                prep(0, 0)
                schedule(lambda b, s, nxt: prep(b + 1, 1 - s) if nxt else None, pool)

            @block.scalar
            def _(act):
                for k in range(4):
                    ci, co = divmod(k, 2)
                    act.wait_ge(wl[k % 2], 16 * (k // 2) + 16)
                    nc.scalar.copy(w2hi[:, ci, :, co * P:(co + 1) * P], wstage[:, k % 2]).then_inc(wh, 1)
                act.wait_ge(ld, 48)
                nc.scalar.copy(w1hi[:], w1stage[:]).then_inc(cw, 1)
                act.wait_ge(chain, 4)

                def prep(j, s):
                    for q in range(4):
                        ci, nh = divmod(q, 2)
                        sl = slice(nh * H2, (nh + 1) * H2)
                        act.wait_ge(tr, val(4 * j + q + 1))
                        if not (isinstance(j, int) and j < 2) and q == 0:
                            act.wait_ge(xT_st[s], val(8 * j - 8 * s))
                            act.wait_ge(yr, val(4 * j - 4))
                        nc.scalar.copy(xT[:, s, ci, sl], pT[q % 2][:, :]).then_inc(xTr, 1)
                        if not (isinstance(j, int) and j == 0) and q == 0:
                            act.wait_ge(c1, val(4 * j))
                        nc.scalar.copy(xhi[:, ci, sl], pT[q % 2][:, :]).then_inc(xhr, 1)
                    for q, (co, nh) in enumerate(QC):
                        act.wait_ge(c1, val(4 * j + q + 1))
                        if not (isinstance(j, int) and j == 0 and q < 2):
                            act.wait_ge(hl, val(4 * j + q - 1))
                        nc.scalar.activation(h32[:, q % 2, :], pH[q % 2][:, :], ACT.Relu, scale=scale[:, 0, co:co + 1],
                                             bias=shift[:, 0, co:co + 1]).then_inc(h3, 1)
                        if not (isinstance(j, int) and j < 2) and q == 0:
                            act.wait_ge(c2, val(4 * j - 4))
                        act.wait_ge(h3, val(4 * j + q + 1))
                        nc.scalar.copy(hhi[:, s, co, PAD + nh * H2:PAD + (nh + 1) * H2], h32[:, q % 2, :]).then_inc(hh, 1)

                def finish(j, qs):
                    for q in qs:
                        co, nh = QC[q]
                        act.wait_ge(yr, val(4 * j + q + 1))
                        if not (isinstance(j, int) and j == 0 and q < 2):
                            act.wait_ge(c_st[q % 2], val(32 * j + 16 * (q // 2)))
                        nc.scalar.activation(xc[:, q % 2, :], yt[:, q % 2, :], ACT.Relu,
                                             bias=shift[:, 1, co:co + 1]).then_inc(xcr, 1)

                def body(b, s, nxt):
                    if nxt:
                        prep(b + 1, 1 - s)
                    finish(b, range(4))

                prep(0, 0)
                schedule(body, act)

            @block.vector
            def _(v):
                v.wait_ge(ld, 48)
                nc.vector.tensor_scalar(scale[:, :, :], bn[:, :, 3, :], EPS, None, ALU.add).then_inc(chain, 1)
                v.wait_ge(pows, 1)
                nc.vector.tensor_tensor(scale[:, :, :], bn[:, :, 0, :], bnp[:, :, :], ALU.mult).then_inc(chain, 1)
                v.wait_ge(chain, 2)
                nc.vector.tensor_tensor(shift[:, :, :], bn[:, :, 2, :], scale[:, :, :], ALU.mult).then_inc(chain, 1)
                v.wait_ge(chain, 3)
                nc.vector.tensor_tensor(shift[:, :, :], bn[:, :, 1, :], shift[:, :, :], ALU.subtract).then_inc(chain, 1)
                for k in range(4):
                    ci, co = divmod(k, 2)
                    v.wait_ge(wh, k + 1)
                    cs = slice(co * P, (co + 1) * P)
                    nc.vector.tensor_tensor(w2lo[:, ci, :, cs], wstage[:, k % 2], w2hi[:, ci, :, cs].bitcast(F32),
                                            ALU.subtract).then_inc(wo, 1)
                v.wait_ge(cw, 1)
                nc.vector.tensor_tensor(w1lo[:], w1stage[:], w1hi[:].bitcast(F32), ALU.subtract).then_inc(cw, 1)

                def norm(j, s):
                    v.wait_ge(x_ld[s], val(16 * j - 16 * s + 32))
                    nc.vector.tensor_tensor(xin[0:GN, s, 0, :], xin[0:GN, s, 0, :], fus[:, s, :], ALU.add).then_inc(fadd, 1)
                    v.wait_ge(fadd, val(j + 1))
                    for k in range(NT):
                        nc.vector.bn_stats(stats[:, k, :], xin[:, s, k, :]).then_inc(bst, 1)
                    v.wait_ge(bst, val(NT * j + NT))
                    nc.vector.memset(mark[:, :], 0.0)
                    for k in range(NT):
                        nc.vector.bn_aggr(mv[:, k, :], stats[:, k, :]).then_inc(bag, 1)
                    v.wait_ge(bag, val(NT * j + NT))
                    nc.vector.tensor_scalar(veps[:, :], mv[:, :, 1], EPS, None, ALU.add).then_inc(vep, 1)
                    v.wait_ge(rst, val(j + 1))
                    for k in range(NT):
                        nc.vector.tensor_scalar(xin[:, s, k, :], xin[:, s, k, :], mv[:, k, 0:1], rstd[:, k:k + 1],
                                                ALU.subtract, ALU.mult).then_inc(x1r, 1)

                def low(j, s, qs):
                    for q in qs:
                        co, nh = QC[q]
                        v.wait_ge(hh, val(4 * j + q + 1))
                        sl = slice(PAD + nh * H2, PAD + (nh + 1) * H2)
                        nc.vector.tensor_tensor(hlo[:, s, co, sl], h32[:, q % 2, :], hhi[:, s, co, sl].bitcast(F32),
                                                ALU.subtract).then_inc(hl, 1)

                def add(j, s, qs):
                    for q in qs:
                        co, nh = QC[q]
                        v.wait_ge(c2, val(4 * j + q + 1))
                        if not (isinstance(j, int) and j == 0 and q < 2):
                            v.wait_ge(xcr, val(4 * j + q - 1))
                        nc.vector.scalar_tensor_tensor(yt[:, q % 2, :], pY[q % 2][:, :], scale[:, 1, co:co + 1],
                                                       xT[:, s, co, nh * H2:(nh + 1) * H2], ALU.mult, ALU.add).then_inc(yr, 1)

                def body(b, s, nxt):
                    if nxt:
                        norm(b + 1, 1 - s)
                    add(b, s, [0])
                    if nxt:
                        low(b + 1, 1 - s, range(4))
                    add(b, s, [1, 2, 3])

                norm(0, 0)
                low(0, 0, range(4))
                schedule(body, v)

            @block.tensor
            def _(pe):
                pe.wait_ge(ld, 48)

                def transposes(j, s):
                    for q in range(4):
                        ci, nh = divmod(q, 2)
                        pe.wait_ge(x1r, val(NT * j + 4 * nh + 4))
                        if not (isinstance(j, int) and j == 0 and q < 2):
                            pe.wait_ge(xhr, val(4 * j + q - 1))
                        for k in range(4):
                            ins = nc.tensor.transpose(pT[q % 2][:, k * P:(k + 1) * P],
                                                      xin[:, s, 4 * nh + k, ci * P:(ci + 1) * P], ident[:, :])
                        ins.then_inc(tr, 1)

                def conv1(j):
                    pe.wait_ge(xlr, val(4 * j + 4))
                    for q, (co, nh) in enumerate(QC):
                        if not (isinstance(j, int) and j == 0 and q < 2):
                            pe.wait_ge(h3, val(4 * j + q - 1))
                        sl, cs = slice(nh * H2, (nh + 1) * H2), slice(co * P, (co + 1) * P)
                        products(nc, pH[q % 2][:, :], [(w1hi[:, c, cs], w1lo[:, c, cs], xhi[:, c, sl], xlo[:, c, sl])
                                                       for c in range(DC)]).then_inc(c1, 1)

                def conv2(j, s, q):
                    co, nh = QC[q]
                    if q == 0:
                        pe.wait_ge(hl, val(4 * j + 4))
                    if not (isinstance(j, int) and j == 0 and q < 2):
                        pe.wait_ge(yr, val(4 * j + q - 1))
                    cs = slice(co * P, (co + 1) * P)
                    products(nc, pY[q % 2][:, :], [
                        (w2hi[:, c, k, cs], w2lo[:, c, k, cs],
                         hhi[:, s, c, nh * H2 + k:nh * H2 + k + H2], hlo[:, s, c, nh * H2 + k:nh * H2 + k + H2])
                        for c in range(DC) for k in range(TAPS)]).then_inc(c2, 1)

                pe.wait_ge(cw, 2)
                transposes(0, 0)
                conv1(0)
                pe.wait_ge(wo, 4)
                pe.wait_ge(pads, 16)

                def body(b, s, nxt):
                    conv2(b, s, 0)
                    if nxt:
                        transposes(b + 1, 1 - s)
                    conv2(b, s, 1)
                    if nxt:
                        conv1(b + 1)
                    conv2(b, s, 2)
                    conv2(b, s, 3)

                schedule(body, pe)


def nodes_stage(nc, t):
    with ExitStack() as ctx:
        m = Space(nc, ctx, "n")
        SR = 12
        LR = 16
        XK = 2 * DC
        wst = m.sb("wst", [P, 3 * D])
        wihh = m.sb("wihh", [P, XK, 3 * D], F32R)
        wihl = m.sb("wihl", [P, XK, 3 * D], F32R)
        whhh = m.sb("whhh", [P, DC, 3 * D], F32R)
        whhl = m.sb("whhl", [P, DC, 3 * D], F32R)
        wmh = m.sb("wmh", [P, DC, D], F32R)
        wml = m.sb("wml", [P, DC, D], F32R)
        wseh = m.sb("wseh", [P, DC, SR], F32R)
        wsel = m.sb("wsel", [P, DC, SR], F32R)
        wse = m.sb("wse", [P, DC, SR])
        bse = m.sb("bse", [SR, 1])
        selA = m.sb("selA", [SR, SELW])
        selB = m.sb("selB", [SR, SELW])
        rows = m.sb("rows", [LR, 6])
        bih = m.sb("bih", [P, 3 * D])
        bn_ = m.sb("bn", [P, 2 * D])
        bmsg = m.sb("bmsg", [P, D])
        half = m.sb("half", [P, 1])

        xstg = m.sb("xstg", [P, DC, H2])
        cstg = m.sb("cstg", [P, DC, H2])
        xhi = m.sb("xhi", [P, 2, DC, N], F32R)
        xlo = m.sb("xlo", [P, 2, DC, N], F32R)
        chi = m.sb("chi", [P, 2, DC, H2], F32R)
        clo = m.sb("clo", [P, 2, DC, H2], F32R)
        mhi = m.sb("mhi", [P, 2, DC, H2], F32R)
        mlo = m.sb("mlo", [P, 2, DC, H2], F32R)
        s1 = m.sb("s1", [SR, 2, H2])
        s2 = m.sb("s2", [SR, 2, H2])
        vhi = m.sb("vhi", [LR, H2])
        vlo = m.sb("vlo", [LR, H2])
        vt = m.sb("vt", [LR, 2, H2])
        Lr = m.sb("Lr", [LR, N], F32R)
        Rr = m.sb("Rr", [LR, N], F32R)
        mt_ = m.sb("mt", [P, 2, D])
        msgh = m.sb("msgh", [P, NT, D], F32R)
        msgl = m.sb("msgl", [P, NT, D], F32R)
        adj = m.sb("adj", [P, 4, H2])
        E = m.sb("E", [P, 2, H2])
        A32 = m.sb("A32", [P, 2, H2])
        Ahi = m.sb("Ahi", [P, 2, H2], F32R)
        Alo = m.sb("Alo", [P, 2, H2], F32R)
        x1 = m.sb("x1", [P, 2, D])
        rz = m.sb("rz", [P, 2 * D])
        th = m.sb("th", [P, 2 * D])
        gn = m.sb("gn", [P, 2 * D])
        t1 = m.sb("t1", [P, D])
        t2 = m.sb("t2", [P, D])
        nn = m.sb("nn", [P, D])
        dd = m.sb("dd", [P, D])
        ee, ff = t1, t2
        res = m.sb("res", [P, D])
        stats = m.sb("stats", [P, 6])
        mv = m.sb("mv", [P, 2])
        mark = m.sb("mark", [P, 1])
        veps = m.sb("veps", [P, 1])
        rstd = m.sb("rstd", [P, 1])
        outt = m.sb("outt", [P, 2, D])

        pN = [m.bank(f"pN{k}") for k in range(2)]
        pD = [m.bank(f"pD{k}") for k in range(2)]
        pRZ = m.bank("pRZ")
        pG = m.bank("pG")
        pP = [m.bank(f"pP{k}") for k in range(2)]

        ld = m.sem("constants_loaded")
        wl = m.sem("weights_staged")
        wh = m.sem("weights_hi")
        wo = m.sem("weights_lo")
        bs = m.sem("biases_summed")
        hs = m.sem("half_set")
        xl = m.sem("x1T_loaded")
        cl = m.sem("xcT_loaded")
        xh_r = m.sem("x1T_hi_ready")
        xl_r = m.sem("x1T_lo_ready")
        ch_r = m.sem("xcT_hi_ready")
        cl_r = m.sem("xcT_lo_ready")
        s_m = m.sem("s_multiplied")
        s_r = m.sem("s_ready")
        s2_r = m.sem("s_squared")
        v_m = m.sem("rows_multiplied")
        vh_r = m.sem("rows_hi")
        vl_r = m.sem("rows_lo")
        vt_r = m.sem("rows_partial")
        lr_r = m.sem("LR_ready")
        mg_m = m.sem("msg_multiplied")
        mg_t = m.sem("msg_biased")
        mg_h = m.sem("msg_hi_ready")
        mg_l = m.sem("msg_lo_ready")
        al = [m.sem(f"adj_loaded{k}") for k in range(4)]
        d_m = m.sem("dist_multiplied")
        e_r = m.sem("E_ready")
        a_r = m.sem("A_ready")
        ah_r = m.sem("A_hi_ready")
        alo_r = m.sem("A_lo_ready")
        av = m.sem("A_multiplied")
        nh_r = m.sem("nmp_hi_ready")
        nl_r = m.sem("nmp_lo_ready")
        x1l = [m.sem(f"x1_loaded{k}") for k in range(2)]
        rz_m = m.sem("rz_multiplied")
        gn_m = m.sem("n_multiplied")
        rz_r = m.sem("rz_biased")
        gn_r = m.sem("n_biased")
        th_r = m.sem("rz_tanh")
        tt1 = m.sem("r_gh_n")
        tt2 = m.sem("n_arg")
        n_r = m.sem("n_ready")
        g_d = m.sem("x_minus_n")
        g_e = m.sem("z_scaled")
        g_f = m.sem("update_ready")
        g_r = m.sem("residual_ready")
        g_s = m.sem("stats_ready")
        g_a = m.sem("mean_var_ready")
        g_v = m.sem("var_eps_ready")
        g_p = m.sem("rstd_ready")
        o_r = m.sem("out_ready")
        o_st = [m.sem(f"out_stored{k}") for k in range(2)]

        WTS = ([(t["w_ih"][:, k, :], wihh[:, k, :], wihl[:, k, :], 3 * D) for k in range(XK)]
               + [(t["w_hh"][:, k, :], whhh[:, k, :], whhl[:, k, :], 3 * D) for k in range(DC)]
               + [(t["w_msg"][:, k, :], wmh[:, k, :], wml[:, k, :], D) for k in range(DC)])
        NW = len(WTS)
        first = lambda j: isinstance(j, int) and j == 0

        def schedule(prep, body, eng):
            prep(0, 0)
            body(0, 0, False, True)
            with eng.Fori(0, B // 2 - 1) as turn:
                i = Turn(turn)
                for k in range(2):
                    body(2 * i + k + 1, 1 - k, True, True)
            body(B - 1, 1, True, False)

        with nc.Block() as block:
            @block.sync
            def _(sp):
                for dst, src in ((wse, t["w_se"]), (bse, t["b_se"]), (selA, t["selA"]), (selB, t["selB"]),
                                 (rows, t["rows"]), (bih, t["b_ih"]), (wst, t["b_hh"]), (bmsg, t["b_msg"])):
                    sp.dma_start(dst[:], src).then_inc(ld, 16)
                sp.wait_ge(bs, 3)
                for n, (src, _h, _l, w) in enumerate(WTS):
                    if n:
                        sp.wait_ge(wo, val(n))
                    sp.dma_start(wst[:, 0:w], src).then_inc(wl, 16)

                def load_xT(b, h):
                    if True:
                        if not (first(b) and h == 0):
                            sp.wait_ge(xl_r, val(2 * b + h))
                        sp.dma_start(xstg[:], t["x1T"][val(b)][:, :, h * H2:(h + 1) * H2]).then_inc(xl, 16)

                def load_xc(b, h):
                    if not (first(b) and h == 0):
                        sp.wait_ge(cl_r, val(2 * b + h))
                    sp.dma_start(cstg[:], t["xcT"][val(b)][:, :, h * H2:(h + 1) * H2]).then_inc(cl, 16)

                def load_adj(b, h, k):
                    n = 16 * b + 8 * h + k
                    if not (first(b) and h == 0 and k < 4):
                        sp.wait_ge(a_r, val(n - 3))
                    sp.dma_start(adj[:, k % 4, :], t["adjT"][val(b)][:, k, h * H2:(h + 1) * H2]).then_inc(al[k % 4], 16)

                def load_x1(g_b, g_k):
                    g = 8 * g_b + g_k
                    if not (first(g_b) and g_k < 2):
                        sp.wait_ge(g_r, val(g - 1))
                    sp.dma_start(x1[:, g_k % 2, :], t["x1"][val(g_b)][:, g_k, :]).then_inc(x1l[g_k % 2], 16)

                def store(g_b, g_k):
                    g = 8 * g_b + g_k
                    sp.wait_ge(o_r, val(g + 1))
                    sp.dma_start(t["out"][val(g_b)][:, g_k, :], outt[:, g_k % 2, :]).then_inc(o_st[g_k % 2], 16)

                def prep(b, s):
                    for h in range(2):
                        load_xT(b, h)

                def body(b, s, gates, nxt):
                    for h in range(2):
                        load_xc(b, h)
                        for k in range(NT):
                            load_adj(b, h, k)
                            if h == 1 and nxt and k in (1, 4):
                                load_xT(b + 1, k // 4)
                            if h == 0 and gates and k % 2 == 0:
                                load_x1(b - 1, 4 + k // 2)
                            if h == 0 and gates and k % 2 == 1:
                                store_lag(b - 1, 4 + k // 2)
                            if h == 1 and k % 2 == 0:
                                load_x1(b, k // 2)
                            if h == 1 and k % 2 == 1:
                                store_lag(b, k // 2)

                def store_lag(b, k):
                    if k > 0:
                        store(b, k - 1)
                    elif not first(b):
                        store(b - 1, NT - 1)

                schedule(prep, body, sp)
                for k in range(4):
                    load_x1(B - 1, 4 + k)
                    store_lag(B - 1, 4 + k)
                store(B - 1, NT - 1)
                for k in range(2):
                    sp.wait_ge(o_st[k], 16 * B * NT // 2)

            @block.gpsimd
            def _(pool):
                nc.gpsimd.memset(half[:, :], -0.5).then_inc(hs, 1)
                pool.wait_ge(hs, 1)

                def split_x(b, s, h):
                    pool.wait_ge(xh_r, val(2 * b + h + 1))
                    nc.gpsimd.tensor_tensor(xlo[:, s, :, h * H2:(h + 1) * H2], xstg[:],
                                            xhi[:, s, :, h * H2:(h + 1) * H2].bitcast(F32), ALU.subtract).then_inc(xl_r, 1)

                def split_c(b, h):
                    pool.wait_ge(ch_r, val(2 * b + h + 1))
                    nc.gpsimd.tensor_tensor(clo[:, h], cstg[:], chi[:, h].bitcast(F32), ALU.subtract).then_inc(cl_r, 1)

                def low_A(b, h, k):
                    n = 16 * b + 8 * h + k
                    pool.wait_ge(ah_r, val(n + 1))
                    nc.gpsimd.tensor_tensor(Alo[:, k % 2], A32[:, k % 2], Ahi[:, k % 2].bitcast(F32),
                                            ALU.subtract).then_inc(alo_r, 1)

                def rstd_of(g_b, g_k):
                    pool.wait_ge(g_v, val(8 * g_b + g_k + 1))
                    nc.gpsimd.tensor_tensor(rstd[:, :], veps[:, :], half[:, :], ALU.pow).then_inc(g_p, 1)

                def prep(b, s):
                    for h in range(2):
                        split_x(b, s, h)

                def body(b, s, gates, nxt):
                    for h in range(2):
                        for k in range(NT):
                            low_A(b, h, k)
                            if k == 1:
                                split_c(b, h)
                            if h == 1 and nxt and k in (3, 5):
                                split_x(b + 1, 1 - s, (k - 3) // 2)
                            if k % 2 == 1 and h == 0 and gates:
                                rstd_of(b - 1, 4 + k // 2)
                            if k % 2 == 1 and h == 1:
                                rstd_of(b, k // 2)

                schedule(prep, body, pool)
                for k in range(4):
                    rstd_of(B - 1, 4 + k)

            @block.scalar
            def _(act):
                act.wait_ge(ld, 128)
                for n, (_s, hi, _l, w) in enumerate(WTS):
                    act.wait_ge(wl, val(16 * n + 16))
                    nc.scalar.copy(hi, wst[:, 0:w]).then_inc(wh, 1)
                nc.scalar.copy(wseh[:], wse[:]).then_inc(wh, 1)

                def split_x(b, s, h):
                    act.wait_ge(xl, val(32 * b + 16 * h + 16))
                    if h == 0 and not (isinstance(b, int) and b < 2):
                        act.wait_ge(gn_m, val(8 * b - 8))
                    nc.scalar.copy(xhi[:, s, :, h * H2:(h + 1) * H2], xstg[:]).then_inc(xh_r, 1)

                def prep(b, s):
                    for h in range(2):
                        act.wait_ge(s_m, val(2 * b + h + 1))
                        if not first(b):
                            act.wait_ge(v_m, val(2 * b - 1 + h))
                        nc.scalar.activation(s1[:, h, :], pP[h][0:SR, :], ACT.Identity, bias=bse[:, :]).then_inc(s_r, 1)
                    for k in range(NT):
                        act.wait_ge(mg_t, val(8 * b + k + 1))
                        nc.scalar.activation(msgh[:, k, :], mt_[:, k % 2, :], ACT.Relu).then_inc(mg_h, 1)
                        if k in (1, 3):
                            h = k // 2
                            act.wait_ge(v_m, val(2 * b + h + 1))
                            if not (first(b) and h == 0):
                                act.wait_ge(lr_r, val(4 * b + 2 * h))
                            nc.scalar.copy(vhi[:, :].bitcast(F32R), pD[h][0:LR, :]).then_inc(vh_r, 1)

                def exp_hi(b, h, k):
                    n = 16 * b + 8 * h + k
                    act.wait_ge(d_m, val(n + 1))
                    if not (first(b) and h == 0 and k < 2):
                        act.wait_ge(a_r, val(n - 1))
                    nc.scalar.activation(E[:, k % 2], pD[k % 2][:, :], ACT.Exp).then_inc(e_r, 1)

                def hi_A(b, h, k):
                    n = 16 * b + 8 * h + k
                    act.wait_ge(a_r, val(n + 1))
                    if not (first(b) and h == 0 and k < 2):
                        act.wait_ge(av, val(n - 1))
                    nc.scalar.copy(Ahi[:, k % 2], A32[:, k % 2]).then_inc(ah_r, 1)

                def hi_c(b, h):
                    act.wait_ge(cl, val(32 * b + 16 * h + 16))
                    if not first(b):
                        act.wait_ge(gn_m, val(8 * b - 8 + 4 * h + 4))
                    nc.scalar.copy(chi[:, h], cstg[:]).then_inc(ch_r, 1)

                def hi_n(b, h):
                    act.wait_ge(av, val(16 * b + 8 * h + 8))
                    if not first(b):
                        act.wait_ge(gn_m, val(8 * b - 8 + 4 * h + 4))
                    for c in range(DC):
                        nc.scalar.copy(mhi[:, h, c, :], pN[c][:, :]).then_inc(nh_r, 1)

                def tanhs(g_b, g_k):
                    g = 8 * g_b + g_k
                    act.wait_ge(rz_r, val(g + 1))
                    if not (first(g_b) and g_k == 0):
                        act.wait_ge(g_e, val(g))
                    nc.scalar.activation(th[:, :], rz[:, :], ACT.Tanh, scale=0.5).then_inc(th_r, 1)
                    act.wait_ge(tt2, val(g + 1))
                    if not (first(g_b) and g_k == 0):
                        act.wait_ge(g_f, val(g))
                    nc.scalar.activation(nn[:, :], t2[:, :], ACT.Tanh).then_inc(n_r, 1)

                def body(b, s, gates, nxt):
                    for h in range(2):
                        for k in range(NT):
                            exp_hi(b, h, k)
                            if k:
                                hi_A(b, h, k - 1)
                            if k == 1 and not (h == 0 and not gates):
                                tanhs(*((b - 1, 4) if h == 0 else (b, 0)))
                            if k == 2:
                                hi_c(b, h)
                            if h == 1 and nxt and k in (4, 6):
                                split_x(b + 1, 1 - s, (k - 4) // 2)
                            if k % 2 == 1 and k > 1 and not (h == 0 and not gates):
                                tanhs(*((b - 1, 4 + k // 2) if h == 0 else (b, k // 2)))
                        hi_A(b, h, NT - 1)
                        hi_n(b, h)
                    if nxt:
                        prep(b + 1, 1 - s)

                for h in range(2):
                    split_x(0, 0, h)
                schedule(prep, body, act)
                for k in range(4):
                    tanhs(B - 1, 4 + k)

            @block.vector
            def _(v):
                v.wait_ge(ld, 128)
                nc.vector.tensor_tensor(bih[:, 0:2 * D], bih[:, 0:2 * D], wst[:, 0:2 * D], ALU.add).then_inc(bs, 1)
                nc.vector.tensor_copy(bn_[:, D:2 * D], wst[:, 2 * D:3 * D]).then_inc(bs, 1)
                nc.vector.tensor_copy(bn_[:, 0:D], bih[:, 2 * D:3 * D]).then_inc(bs, 1)
                v.wait_ge(bs, 3)
                for n, (_s, hi, lo, w) in enumerate(WTS):
                    v.wait_ge(wh, val(n + 1))
                    nc.vector.tensor_tensor(lo, wst[:, 0:w], hi.bitcast(F32), ALU.subtract).then_inc(wo, 1)
                v.wait_ge(wh, NW + 1)
                nc.vector.tensor_tensor(wsel[:], wse[:], wseh[:].bitcast(F32), ALU.subtract).then_inc(wo, 1)

                def operands(b, h):
                    sl = slice(h * H2, (h + 1) * H2)
                    v.wait_ge(vh_r, val(2 * b + h + 1))
                    nc.vector.tensor_tensor(vlo[:, :], pD[h][0:LR, :], vhi[:, :], ALU.subtract).then_inc(vl_r, 1)
                    nc.vector.tensor_scalar(vt[:, 0, :], vhi[:, :], rows[:, 0:1], rows[:, 2:3], ALU.mult, ALU.add).then_inc(vt_r, 1)
                    nc.vector.tensor_scalar(vt[:, 1, :], vhi[:, :], rows[:, 3:4], rows[:, 5:6], ALU.mult, ALU.add).then_inc(vt_r, 1)
                    v.wait_ge(vl_r, val(2 * b + h + 1))
                    v.wait_ge(vt_r, val(4 * b + 2 * h + 2))
                    if not first(b):
                        v.wait_ge(d_m, val(16 * b))
                    nc.vector.scalar_tensor_tensor(Lr[:, sl], vlo[:, :], rows[:, 1:2], vt[:, 0, :], ALU.mult, ALU.add).then_inc(lr_r, 1)
                    nc.vector.scalar_tensor_tensor(Rr[:, sl], vlo[:, :], rows[:, 4:5], vt[:, 1, :], ALU.mult, ALU.add).then_inc(lr_r, 1)
                    v.wait_ge(lr_r, val(4 * b + 2 * h + 2))

                def prep(b, s):
                    for h in range(2):
                        v.wait_ge(s_r, val(2 * b + h + 1))
                        if not first(b):
                            v.wait_ge(v_m, val(2 * b - 1 + h))
                        nc.vector.tensor_tensor(s2[:, h, :], s1[:, h, :], s1[:, h, :], ALU.mult).then_inc(s2_r, 1)
                    for k in range(NT + 1):
                        if k < NT:
                            v.wait_ge(mg_m, val(8 * b + k + 1))
                            if not (first(b) and k < 2):
                                v.wait_ge(mg_l, val(8 * b + k - 1))
                            nc.vector.tensor_tensor(mt_[:, k % 2, :], pP[k % 2][:, 0:D], bmsg[:, :], ALU.add).then_inc(mg_t, 1)
                        if k:
                            v.wait_ge(mg_h, val(8 * b + k))
                            nc.vector.scalar_tensor_tensor(msgl[:, k - 1, :], mt_[:, (k - 1) % 2, :], 0.0,
                                                           msgh[:, k - 1, :].bitcast(F32), ALU.max, ALU.subtract).then_inc(mg_l, 1)
                        if k in (2, 4):
                            operands(b, k // 2 - 1)

                def mask(b, h, k):
                    n = 16 * b + 8 * h + k
                    v.wait_ge(e_r, val(n + 1))
                    v.wait_ge(al[k % 4], val(64 * b + 32 * h + 16 * (k // 4) + 16))
                    if not (first(b) and h == 0 and k < 2):
                        v.wait_ge(alo_r, val(n - 1))
                    nc.vector.tensor_tensor(A32[:, k % 2], E[:, k % 2], adj[:, k % 4], ALU.mult).then_inc(a_r, 1)

                def low_n(b, h):
                    for c in range(DC):
                        v.wait_ge(nh_r, val(4 * b + 2 * h + c + 1))
                        nc.vector.tensor_tensor(mlo[:, h, c, :], pN[c][:, :], mhi[:, h, c, :].bitcast(F32), ALU.subtract).then_inc(nl_r, 1)

                def gate(g_b, g_k):
                    g = 8 * g_b + g_k
                    n0 = first(g_b) and g_k == 0
                    v.wait_ge(rz_m, val(g + 1))
                    if not n0:
                        v.wait_ge(th_r, val(g))
                    nc.vector.tensor_tensor(rz[:, :], pRZ[:, :], bih[:, 0:2 * D], ALU.add).then_inc(rz_r, 1)
                    v.wait_ge(gn_m, val(g + 1))
                    nc.vector.tensor_tensor(gn[:, :], pG[:, :], bn_[:, :], ALU.add).then_inc(gn_r, 1)
                    v.wait_ge(gn_r, val(g + 1))
                    v.wait_ge(th_r, val(g + 1))
                    nc.vector.scalar_tensor_tensor(t1[:, :], th[:, 0:D], 1.0, gn[:, D:2 * D], ALU.add, ALU.mult).then_inc(tt1, 1)
                    v.wait_ge(tt1, val(g + 1))
                    nc.vector.scalar_tensor_tensor(t2[:, :], t1[:, :], 0.5, gn[:, 0:D], ALU.mult, ALU.add).then_inc(tt2, 1)

                def update(g_b, g_k):
                    g = 8 * g_b + g_k
                    v.wait_ge(n_r, val(g + 1))
                    v.wait_ge(x1l[g_k % 2], val(64 * g_b + 16 * (g_k // 2) + 16))
                    nc.vector.tensor_tensor(dd[:, :], x1[:, g_k % 2, :], nn[:, :], ALU.subtract).then_inc(g_d, 1)
                    v.wait_ge(g_d, val(g + 1))
                    nc.vector.scalar_tensor_tensor(ee[:, :], th[:, D:2 * D], 1.0, dd[:, :], ALU.add, ALU.mult).then_inc(g_e, 1)
                    v.wait_ge(g_e, val(g + 1))
                    nc.vector.scalar_tensor_tensor(ff[:, :], ee[:, :], 0.5, nn[:, :], ALU.mult, ALU.add).then_inc(g_f, 1)
                    v.wait_ge(g_f, val(g + 1))
                    nc.vector.tensor_tensor(res[:, :], ff[:, :], x1[:, g_k % 2, :], ALU.add).then_inc(g_r, 1)
                    v.wait_ge(g_r, val(g + 1))
                    nc.vector.bn_stats(stats[:, :], res[:, :]).then_inc(g_s, 1)
                    v.wait_ge(g_s, val(g + 1))
                    nc.vector.memset(mark[:, :], 0.0)
                    nc.vector.bn_aggr(mv[:, :], stats[:, :]).then_inc(g_a, 1)
                    v.wait_ge(g_a, val(g + 1))
                    nc.vector.tensor_scalar(veps[:, :], mv[:, 1:2], EPS, None, ALU.add).then_inc(g_v, 1)

                def norm(g_b, g_k):
                    g = 8 * g_b + g_k
                    v.wait_ge(g_p, val(g + 1))
                    if not (first(g_b) and g_k < 2):
                        v.wait_ge(o_st[g_k % 2], val(64 * g_b + 16 * (g_k // 2)))
                    nc.vector.tensor_scalar(outt[:, g_k % 2, :], res[:, :], mv[:, 0:1], rstd[:, :],
                                            ALU.subtract, ALU.mult).then_inc(o_r, 1)

                def body(b, s, gates, nxt):
                    for h in range(2):
                        for k in range(NT):
                            on = not (h == 0 and not gates)
                            at = (b - 1, 4 + k // 2) if h == 0 else (b, k // 2)
                            mask(b, h, k)
                            if k % 2 == 0 and on:
                                gate(*at)
                            if k % 2 == 1 and on:
                                update(*at)
                                if k < NT - 1:
                                    norm(*at)
                        low_n(b, h)
                        if on:
                            norm(*at)
                    if nxt:
                        prep(b + 1, 1 - s)

                schedule(prep, body, v)
                for k in range(4):
                    gate(B - 1, 4 + k)
                    update(B - 1, 4 + k)
                    norm(B - 1, 4 + k)

            @block.tensor
            def _(pe):
                pe.wait_ge(wo, NW + 1)
                pe.wait_ge(ld, 128)

                def prep(b, s):
                    for h in range(2):
                        sl = slice(h * H2, (h + 1) * H2)
                        pe.wait_ge(xl_r, val(2 * b + h + 1))
                        if h == 0 and not first(b):
                            pe.wait_ge(mg_t, val(8 * b))
                        products(nc, pP[h][0:SR, :], [(wseh[:, c, :], wsel[:, c, :], xhi[:, s, c, sl], xlo[:, s, c, sl])
                                                      for c in range(DC)]).then_inc(s_m, 1)
                    for k in range(NT):
                        if k < 2:
                            pe.wait_ge(s_r, val(2 * b + k + 1))
                        else:
                            pe.wait_ge(mg_t, val(8 * b + k - 1))
                        products(nc, pP[k % 2][:, 0:D], [(xhi[:, s, c, k * P:(k + 1) * P], xlo[:, s, c, k * P:(k + 1) * P],
                                                          wmh[:, c, :], wml[:, c, :]) for c in range(DC)]).then_inc(mg_m, 1)
                        if k in (1, 3):
                            h = k // 2
                            pe.wait_ge(s_r, val(2 * b + h + 1))
                            pe.wait_ge(s2_r, val(2 * b + h + 1))
                            if h == 0 and not first(b):
                                pe.wait_ge(e_r, val(16 * b))
                            nc.tensor.matmul(pD[h][0:SELW, :], selA[:, :], s1[:, h, :], start=True, stop=False)
                            nc.tensor.matmul(pD[h][0:SELW, :], selB[:, :], s2[:, h, :], start=False, stop=True).then_inc(v_m, 1)

                def dist(b, s, h, k):
                    n = 16 * b + 8 * h + k
                    if h == 0 and k == 0:
                        pe.wait_ge(lr_r, val(4 * b + 4))
                    if not (first(b) and h == 0 and k < 2):
                        pe.wait_ge(e_r, val(n - 1))
                    nc.tensor.matmul(pD[k % 2][:, :], Lr[:, k * P:(k + 1) * P], Rr[:, h * H2:(h + 1) * H2],
                                     start=True, stop=True).then_inc(d_m, 1)

                def gather(b, h, k):
                    n = 16 * b + 8 * h + k
                    pe.wait_ge(alo_r, val(n + 1))
                    if h == 0:
                        pe.wait_ge(mg_l, val(8 * b + k + 1))
                    if k == 0 and not (first(b) and h == 0):
                        pe.wait_ge(nl_r, val(4 * b + 2 * h))
                    for c in range(DC):
                        cs = slice(c * P, (c + 1) * P)
                        ins = products(nc, pN[c][:, :], [(msgh[:, k, cs], msgl[:, k, cs], Ahi[:, k % 2], Alo[:, k % 2])],
                                       start=k == 0, stop=k == NT - 1)
                    ins.then_inc(av, 1)

                def gates_of(g_b, s, g_k):
                    g = 8 * g_b + g_k
                    h, k = divmod(g_k, 4)
                    cs, ns = slice(k * P, (k + 1) * P), slice(g_k * P, (g_k + 1) * P)
                    if k == 0:
                        pe.wait_ge(cl_r, val(2 * g_b + h + 1))
                    xin = ([(chi[:, h, c, cs], clo[:, h, c, cs]) for c in range(DC)]
                           + [(mhi[:, h, c, cs], mlo[:, h, c, cs]) for c in range(DC)])
                    xs = [(xhi[:, s, c, ns], xlo[:, s, c, ns]) for c in range(DC)]
                    rzs, ns_ = slice(0, 2 * D), slice(2 * D, 3 * D)
                    if not (first(g_b) and g_k == 0):
                        pe.wait_ge(rz_r, val(g))
                    rz = ([(a, l, whhh[:, c, rzs], whhl[:, c, rzs]) for c, (a, l) in enumerate(xs)]
                          + [(a, l, wihh[:, c, rzs], wihl[:, c, rzs]) for c, (a, l) in enumerate(xin)])
                    products(nc, pRZ[:, :], rz[:2 * DC], stop=False)
                    if k == 0:
                        pe.wait_ge(nl_r, val(4 * g_b + 2 * h + 2))
                    products(nc, pRZ[:, :], rz[2 * DC:], start=False).then_inc(rz_m, 1)
                    if not (first(g_b) and g_k == 0):
                        pe.wait_ge(gn_r, val(g))
                    products(nc, pG[:, 0:D], [(a, l, wihh[:, c, ns_], wihl[:, c, ns_]) for c, (a, l) in enumerate(xin)])
                    products(nc, pG[:, D:2 * D], [(a, l, whhh[:, c, ns_], whhl[:, c, ns_]) for c, (a, l) in enumerate(xs)]).then_inc(gn_m, 1)

                def body(b, s, gates, nxt):
                    for h in range(2):
                        dist(b, s, h, 0)
                        for k in range(NT):
                            on = not (h == 0 and not gates)
                            if k + 1 < NT:
                                dist(b, s, h, k + 1)
                            if k % 2 == 0 and on:
                                if h == 0:
                                    gates_of(b - 1, 1 - s, 4 + k // 2)
                                else:
                                    gates_of(b, s, k // 2)
                            gather(b, h, k)
                    if nxt:
                        prep(b + 1, 1 - s)

                schedule(prep, body, pe)
                for k in range(4):
                    gates_of(B - 1, 1, 4 + k)


INPUTS = ["x", "adjT", "l0_x", "l0_adj", "l0_gmask", "l0_geye", "l0_member", "l0_fw", "ident", "l0_w1", "l0_b1",
          "l0_w2", "l0_b2", "conv1_w", "conv2_w", "bn", "w_ih", "w_hh", "w_msg", "w_se", "b_se", "selA", "selB",
          "rows", "b_ih", "b_hh", "b_msg"]


def build(nc, t):
    t["fused"] = nc.dram_tensor("fused_scratch", (B, GN, D), F32, kind="Internal").ap()
    t["x1"] = nc.dram_tensor("x1_scratch", (B, P, NT, D), F32, kind="Internal").ap()
    t["x1T"] = nc.dram_tensor("x1T_scratch", (B, P, DC, N), F32, kind="Internal").ap()
    t["xcT"] = nc.dram_tensor("xcT_scratch", (B, P, DC, N), F32, kind="Internal").ap()
    groups_stage(nc, t)
    conv_stage(nc, t)
    nodes_stage(nc, t)


def constants():
    gmask = np.zeros((P, NG, P), np.float32)
    geye = np.zeros((P, NG, P), np.float32)
    member = np.zeros((P, NG), np.float32)
    for g, idx in enumerate(GROUPS):
        for q in range(GB):
            rows = GP * q + np.array(idx)
            gmask[np.ix_(rows, [g], rows)] = 1
            geye[rows, g, rows] = 1
            member[rows, g] = 1
    selA = np.zeros((12, SELW), np.float32)
    selB = np.zeros((12, SELW), np.float32)
    selA[np.arange(12), np.arange(12)] = 1
    selB[0:3, 12:16] = -1
    rows = np.zeros((16, 6), np.float32)
    rows[0:6, 0] = 1
    rows[6:12, 1] = 1
    rows[12:14, 2] = 1
    rows[14, 0] = rows[15, 1] = 1
    rows[[0, 1, 2, 6, 7, 8], 3] = 2
    rows[[3, 4, 5, 9, 10, 11], 4] = 2
    rows[12, 3] = rows[13, 4] = 1
    rows[14:16, 5] = 1
    return {"l0_gmask": gmask, "l0_geye": geye, "l0_member": member, "ident": np.eye(P, dtype=np.float32),
            "selA": selA, "selB": selB, "rows": rows}


def layout(i):
    def parts(w):
        return np.ascontiguousarray(w.reshape(-1, P, w.shape[-1]).transpose(1, 0, 2))

    def rep(v):
        return np.ascontiguousarray(np.broadcast_to(v, (P,) + v.shape))

    x, adj = i["x"], i["adj"]
    l0_x = np.zeros((GT, GB, GP, D), np.float32)
    l0_x[:, :, :GN] = x[:, :GN].reshape(GT, GB, GN, D)
    l0_adj = np.zeros((GT, GB, GP, GB, GP), np.float32)
    for q in range(GB):
        l0_adj[:, q, :GN, q, :GN] = adj[:, :GN, :GN].reshape(GT, GB, GN, GN)[:, q]
    bn = np.stack([np.stack([i[f"L1_gnn_bn{k}_{f}"].reshape(DC, P) for f in "gbmv"]) for k in (1, 2)])
    w_se = np.concatenate([i["L1_gnn_w_se"].T] * 4, axis=1)
    b_se = np.concatenate([i["L1_gnn_b_se"]] * 4)
    return {
        "x": np.ascontiguousarray(x.reshape(B, NT, P, D).transpose(0, 2, 1, 3)),
        "adjT": np.ascontiguousarray(adj.transpose(0, 2, 1).reshape(B, NT, P, N).transpose(0, 2, 1, 3)),
        "l0_x": np.ascontiguousarray(l0_x.reshape(GT, P, D).transpose(1, 0, 2)),
        "l0_adj": np.ascontiguousarray(l0_adj.reshape(GT, P, P).transpose(1, 0, 2)),
        "l0_fw": rep(i["L0_gnn_fusion_w"]),
        "l0_w1": np.ascontiguousarray(i["L0_gnn_W1"].reshape(NG, DC, P, DH).transpose(2, 0, 1, 3)),
        "l0_w2": np.ascontiguousarray(i["L0_gnn_W2"].reshape(NG, HC, P, D).transpose(2, 0, 1, 3)),
        "l0_b1": np.ascontiguousarray(i["L0_gnn_b1"].reshape(NG, HC, P).transpose(2, 0, 1)),
        "l0_b2": rep(i["L0_gnn_b2"]),
        "conv1_w": parts(i["L1_gnn_conv1_w"][:, :, 0].T),
        "conv2_w": np.ascontiguousarray(i["L1_gnn_conv2_w"].transpose(1, 2, 0).reshape(DC, P, TAPS, D).transpose(1, 0, 2, 3)),
        "bn": np.ascontiguousarray(bn.transpose(3, 0, 1, 2)),
        "w_ih": parts(i["L1_gnn_w_ih"].T), "w_hh": parts(i["L1_gnn_w_hh"].T), "w_msg": parts(i["L1_gnn_w_msg"].T),
        "w_se": parts(w_se), "b_se": b_se.reshape(-1, 1),
        "b_ih": rep(i["L1_gnn_b_ih"]), "b_hh": rep(i["L1_gnn_b_hh"]), "b_msg": rep(i["L1_gnn_b_msg"]),
    }


def kernel(**inputs):
    import concourse.bacc as bacc
    from concourse.bass_utils import run_bass_kernel_spmd

    inputs = {k: np.asarray(v) for k, v in inputs.items()}
    arrays = {**layout(inputs), **constants()}
    arrays = {f"in_{k}": np.ascontiguousarray(arrays[k]) for k in INPUTS}
    nc = bacc.Bacc("TRN2", target_bir_lowering=False, num_devices=1)
    t = {k: nc.dram_tensor(f"in_{k}", arrays[f"in_{k}"].shape, F32, kind="ExternalInput").ap() for k in INPUTS}
    t["out"] = nc.dram_tensor("out", (B, P, NT, D), F32, kind="ExternalOutput").ap()
    build(nc, t)
    r = run_bass_kernel_spmd(nc, [arrays], core_ids=[0])
    out = r.results[0]["out"]
    return np.ascontiguousarray(out.transpose(0, 2, 1, 3).reshape(B, N, D))
```

```python
from contextlib import ExitStack

import numpy as np

import concourse.bass as bass
from concourse import mybir

P = 128
B, N, D = 16, 1024, 256
DC = D // P
NT = N // P
H2 = N // 2
DH = 512
HC = DH // P
GROUPS = [list(range(25)), [0, 1, 2, 3, 4, 5, 6, 7, 8], [0, 9, 10, 11, 12, 13, 14],
          [6, 7, 8, 12, 13, 14], [3, 4, 5, 9, 10, 11]]
NG = len(GROUPS)
GN = 25
GP = 32
GB = P // GP
GT = B // GB
TAPS, PAD = 17, 8
PQ = (N + 2 * PAD) // 4
HQ = PQ + 2
EPS = 1e-5
SELW = 64

F32 = mybir.dt.float32
F32R = mybir.dt.float32r
ALU = mybir.AluOpType
ACT = mybir.ActivationFunctionType
AX = mybir.AxisListType.X


class Space:

    def __init__(self, nc, ctx, tag):
        self.nc, self.ctx, self.tag = nc, ctx, tag

    def sb(self, name, shape, dt=F32):
        return self.ctx.enter_context(self.nc.sbuf_tensor(f"{self.tag}_{name}", shape, dt))

    def bank(self, name):
        return self.ctx.enter_context(self.nc.psum_tensor(f"{self.tag}_{name}", [P, 512], F32))

    def sem(self, name):
        return self.ctx.enter_context(self.nc.semaphore(f"{self.tag}_{name}"))


def products(nc, out, pairs, start=True, stop=True):
    last = None
    steps = [(a, b) for ah, al, bh, bl in pairs for a, b in ((ah, bh), (ah, bl), (al, bh))]
    for k, (a, b) in enumerate(steps):
        last = nc.tensor.matmul(out, a, b, start=start and k == 0, stop=stop and k == len(steps) - 1)
    return last


class Turn:

    def __init__(self, i, a=1, c=0):
        self.i, self.a, self.c = i, a, c

    def __add__(self, k):
        return Turn(self.i, self.a, self.c + k)

    def __sub__(self, k):
        return self + -k

    def __mul__(self, k):
        return Turn(self.i, self.a * k, self.c * k)

    __radd__, __rmul__ = __add__, __mul__


def val(n):
    return n.i * n.a + n.c if isinstance(n, Turn) else n


def groups_stage(nc, t):
    with ExitStack() as ctx:
        m = Space(nc, ctx, "g")
        x0 = m.sb("x0", [P, GT, D])
        adj0 = m.sb("adj0", [P, GT, P])
        gmask = m.sb("gmask", [P, NG, P])
        geye = m.sb("geye", [P, NG, P])
        member = m.sb("member", [P, NG])
        ident = m.sb("ident", [P, P])
        w1 = m.sb("w1", [P, NG, DC, DH])
        w2 = m.sb("w2", [P, NG, HC, D])
        b1 = m.sb("b1", [P, NG, HC])
        b2 = m.sb("b2", [P, NG, D])
        fw = m.sb("fw", [P, NG])
        A = m.sb("A", [P, NG, GT, P])
        nadjT = m.sb("nadjT", [P, NG, GT, P])
        deg = m.sb("deg", [P, NG * GT])
        deg0 = m.sb("deg0", [P, NG * GT])
        dsafe = m.sb("dsafe", [P, NG * GT])
        dpow = m.sb("dpow", [P, NG * GT])
        dhave = m.sb("dhave", [P, NG * GT])
        dinv = m.sb("dinv", [P, NG * GT])
        half = m.sb("half", [P, NG * GT])
        wmax = m.sb("wmax", [P, 1])
        wexp = m.sb("wexp", [P, NG])
        wsum = m.sb("wsum", [P, 1])
        wrec = m.sb("wrec", [P, 1])
        wsm = m.sb("wsm", [P, NG])
        wmem = m.sb("wmem", [P, NG])
        xaT = m.sb("xaT", [P, DC, 512])
        hT = m.sb("hT", [P, HC, 512])
        sup2 = m.sb("sup2", [P, GT, D])
        pre = m.sb("pre", [P, D])
        act2 = m.sb("act2", [P, D])
        fused = m.sb("fused", [P, GT, D])

        pT = [m.bank(f"pT{k}") for k in range(2)]
        pX = [m.bank(f"pX{k}") for k in range(2)]
        pH = [m.bank(f"pH{k}") for k in range(2)]
        pS = [m.bank(f"pS{k}") for k in range(2)]

        ld = m.sem("loaded")
        ldw = m.sem("weights_loaded")
        st = m.sem("fused_stored")
        dve = m.sem("dve_chain")
        halfs = m.sem("half_set")
        pw = m.sem("powered")
        an = m.sem("adj_normed_rows")
        tr = m.sem("adj_transposed")
        nt = m.sem("nadjT_ready")
        we = m.sem("weights_exp")
        wm = m.sem("weights_max")
        xm = m.sem("xa_multiplied")
        xr = m.sem("xaT_ready")
        hm = m.sem("h_multiplied")
        hr = m.sem("hT_ready")
        sm = m.sem("sup2_multiplied")
        sr = m.sem("sup2_ready")
        om = m.sem("out_multiplied")
        orr = m.sem("out_read")
        fr = m.sem("fused_ready")

        with nc.Block() as block:
            @block.sync
            def _(sp):
                for dst, src in ((adj0, t["l0_adj"]), (gmask, t["l0_gmask"]), (geye, t["l0_geye"]),
                                 (member, t["l0_member"]), (fw, t["l0_fw"]), (ident, t["ident"]), (x0, t["l0_x"])):
                    sp.dma_start(dst[:], src).then_inc(ld, 16)
                for dst, src in ((w1, t["l0_w1"]), (b1, t["l0_b1"]), (w2, t["l0_w2"]), (b2, t["l0_b2"])):
                    sp.dma_start(dst[:], src).then_inc(ldw, 16)
                for b in range(B):
                    k, q = divmod(b, GB)
                    sp.wait_ge(fr, k + 1)
                    sp.dma_start(t["fused"][val(b)], fused[GP * q:GP * q + GN, k, :]).then_inc(st, 16)
                sp.wait_ge(st, 16 * B)

            @block.gpsimd
            def _(pool):
                nc.gpsimd.memset(half[:, :], -0.5).then_inc(halfs, 1)
                pool.wait_ge(halfs, 1)
                pool.wait_ge(dve, 4)
                nc.gpsimd.tensor_tensor(dpow[:, :], dsafe[:, :], half[:, :], ALU.pow).then_inc(pw, 1)

            @block.scalar
            def _(act):
                act.wait_ge(wm, 1)
                nc.scalar.activation(wexp[:, :], fw[:, :], ACT.Exp, bias=wmax[:, :],
                                     accum_out=wsum[:, :]).then_inc(we, 1)
                for g in range(NG):
                    for c in range(DC):
                        act.wait_ge(xm, val(g * DC + c + 1))
                        if g:
                            act.wait_ge(hm, val(HC * g))
                        nc.scalar.copy(xaT[:, c, :], pX[c][:, :]).then_inc(xr, 1)
                    act.wait_ge(ldw, 64)
                    for e in range(HC):
                        act.wait_ge(hm, val(g * HC + e + 1))
                        if g:
                            act.wait_ge(sm, val(GT * g))
                        nc.scalar.activation(hT[:, e, :], pH[e % 2][:, :], ACT.Relu,
                                             bias=b1[:, g, e:e + 1]).then_inc(hr, 1)
                    for k in range(GT):
                        act.wait_ge(sm, val(g * GT + k + 1))
                        if g:
                            act.wait_ge(om, val(GT * (g - 1) + k + 1))
                        nc.scalar.copy(sup2[:, k, :], pS[k % 2][:, 0:D]).then_inc(sr, 1)

            @block.vector
            def _(v):
                n = [0]

                def link(ins):
                    n[0] += 1
                    ins.then_inc(dve, 1)
                    v.wait_ge(dve, val(n[0]))

                v.wait_ge(ld, 16 * 7)
                for g in range(NG):
                    Ag = A[:, g, :, :]
                    ins = nc.vector.tensor_tensor(Ag, adj0[:, :, :], gmask[:, g, :].unsqueeze(1).to_broadcast([P, GT, P]), ALU.mult)
                link(ins)
                for g in range(NG):
                    Ag = A[:, g, :, :]
                    ins = nc.vector.tensor_tensor(Ag, Ag, geye[:, g, :].unsqueeze(1).to_broadcast([P, GT, P]), ALU.add)
                link(ins)
                link(nc.vector.tensor_reduce(deg[:, :], A[:].rearrange("p g t n -> p (g t) n"), axis=AX, op=ALU.add))
                nc.vector.tensor_scalar(deg0[:, :], deg[:, :], 0.0, None, ALU.is_equal).then_inc(halfs, 1)
                v.wait_ge(halfs, 2)
                link(nc.vector.tensor_tensor(dsafe[:, :], deg[:, :], deg0[:, :], ALU.add))
                link(nc.vector.tensor_scalar(dhave[:, :], deg0[:, :], -1.0, 1.0, ALU.mult, ALU.add))
                v.wait_ge(pw, 1)
                link(nc.vector.tensor_tensor(dinv[:, :], dpow[:, :], dhave[:, :], ALU.mult))
                for g in range(NG):
                    for k in range(GT):
                        j = g * GT + k
                        nc.vector.tensor_scalar(A[:, g, k, :], A[:, g, k, :], dinv[:, j:j + 1], None, ALU.mult).then_inc(an, 1)
                link(nc.vector.tensor_reduce(wrec[:, :], fw[:, :], axis=AX, op=ALU.max))
                nc.vector.tensor_scalar(wmax[:, :], wrec[:, :], -1.0, None, ALU.mult).then_inc(wm, 1)
                v.wait_ge(wm, 1)
                for j in range(NG * GT):
                    g, k = divmod(j, GT)
                    v.wait_ge(tr, val(j + 1))
                    nc.vector.tensor_scalar(nadjT[:, g, k, :], pT[j % 2][:, 0:P], dinv[:, j:j + 1], None, ALU.mult).then_inc(nt, 1)
                v.wait_ge(we, 1)
                link(nc.vector.reciprocal(wrec[:, :], wsum[:, :]))
                link(nc.vector.tensor_scalar(wsm[:, :], wexp[:, :], wrec[:, :], None, ALU.mult))
                link(nc.vector.tensor_tensor(wmem[:, :], wsm[:, :], member[:, :], ALU.mult))
                v.wait_ge(ldw, 64)
                for g in range(NG):
                    for k in range(GT):
                        v.wait_ge(om, val(g * GT + k + 1))
                        ins = nc.vector.tensor_tensor(pre[:, :], pT[k % 2][:, 0:D], b2[:, g, :], ALU.add)
                        ins.then_inc(orr, 1)
                        v.wait_ge(orr, val(g * GT + k + 1))
                        link(nc.vector.tensor_scalar(act2[:, :], pre[:, :], 0.0, wmem[:, g:g + 1], ALU.max, ALU.mult))
                        if g == 0:
                            ins = nc.vector.tensor_copy(fused[:, k, :], act2[:, :])
                        else:
                            ins = nc.vector.tensor_tensor(fused[:, k, :], fused[:, k, :], act2[:, :], ALU.add)
                        if g == NG - 1:
                            ins.then_inc(fr, 1)
                            v.wait_ge(fr, k + 1)
                        else:
                            link(ins)

            @block.tensor
            def _(pe):
                pe.wait_ge(ld, 16 * 7)
                for j in range(NG * GT):
                    g, k = divmod(j, GT)
                    pe.wait_ge(an, val(j + 1))
                    if j >= 2:
                        pe.wait_ge(nt, val(j - 1))
                    nc.tensor.transpose(pT[j % 2][:, 0:P], A[:, g, k, :], ident[:, :]).then_inc(tr, 1)
                pe.wait_ge(nt, NG * GT)
                pe.wait_ge(ldw, 64)
                for g in range(NG):
                    for c in range(DC):
                        if g:
                            pe.wait_ge(xr, val((g - 1) * DC + c + 1))
                        for k in range(GT):
                            ins = nc.tensor.matmul(pX[c][:, k * P:(k + 1) * P], x0[:, k, c * P:(c + 1) * P],
                                                   nadjT[:, g, k, :], start=True, stop=True)
                        ins.then_inc(xm, 1)
                    pe.wait_ge(xr, val((g + 1) * DC))
                    for e in range(HC):
                        if g * HC + e >= 2:
                            pe.wait_ge(hr, val(g * HC + e - 1))
                        for c in range(DC):
                            ins = nc.tensor.matmul(pH[e % 2][:, :], w1[:, g, c, e * P:(e + 1) * P], xaT[:, c, :],
                                                   start=c == 0, stop=c == DC - 1)
                        ins.then_inc(hm, 1)
                    pe.wait_ge(hr, val((g + 1) * HC))
                    for k in range(GT):
                        if g * GT + k >= 2:
                            pe.wait_ge(sr, val(g * GT + k - 1))
                        for e in range(HC):
                            ins = nc.tensor.matmul(pS[k % 2][:, 0:D], hT[:, e, k * P:(k + 1) * P], w2[:, g, e, :],
                                                   start=e == 0, stop=e == HC - 1)
                        ins.then_inc(sm, 1)
                    for k in range(GT):
                        pe.wait_ge(sr, val(g * GT + k + 1))
                        if g * GT + k >= 2:
                            pe.wait_ge(orr, val(g * GT + k - 1))
                        nc.tensor.matmul(pT[k % 2][:, 0:D], nadjT[:, g, k, :], sup2[:, k, :],
                                         start=True, stop=True).then_inc(om, 1)


def conv_stage(nc, t, co):
    with ExitStack() as ctx:
        m = Space(nc, ctx, f"c{co}")
        prepares = co == 0
        PAIRS = B // 2
        whi = m.sb("whi", [P, DC, 3, 4, 3, P], F32R)
        wlo = m.sb("wlo", [P, DC, 3, 4, 3, P], F32R)
        h4 = m.sb("h4", [P, 2, 2 * DC, 4, HQ])
        bn = m.sb("bn", [P, 2, 4, DC])
        bnp = m.sb("bnp", [P, 2, DC])
        scale = m.sb("scale", [P, 2, DC])
        shift = m.sb("shift", [P, 2, DC])
        half = m.sb("half", [P, NT])
        M0 = m.sb("M0", [P, 2, H2])
        Y0 = m.sb("Y0", [P, 2, H2])
        y = m.sb("y", [P, 2, N])
        with ExitStack() as staging:
            ms = Space(nc, staging, f"c{co}")
            kept = ms if prepares else m
            raw = kept.sb("raw", [P, DC, 18, P])
            tap = kept.sb("tap", [P, 2, DC, 3, P])
            pairs = ms.sb("pairs", [P, DC, 9, P])
            if prepares:
                w1stage = ms.sb("w1stage", [P, DC, D])
        Pt = m.sb("Pt", [P, 2 * DC, 2, PQ])
        Dt = m.sb("Dt", [P, 2, 2 * DC, 2, PQ])
        Dhi = m.sb("Dhi", [P, 2, 2 * DC, 2, PQ], F32R)
        Dlo = m.sb("Dlo", [P, 2, 2 * DC, 2, PQ], F32R)
        if prepares:
            ident = m.sb("ident", [P, P])
            w1hi = m.sb("w1hi", [P, DC, D], F32R)
            w1lo = m.sb("w1lo", [P, DC, D], F32R)
            xin = m.sb("xin", [P, NT, D])
            fus = m.sb("fus", [GN, D])
            stats = m.sb("stats", [P, NT, 6])
            mv = m.sb("mv", [P, NT, 2])
            mark = m.sb("mark", [P, 1])
            veps = m.sb("veps", [P, NT])
            rstd = m.sb("rstd", [P, NT])
            negmean = m.sb("negmean", [P, NT])
            offset = m.sb("offset", [P, NT])
            xT = m.sb("xT", [P, DC, H2])
            xhi = m.sb("xhi", [P, DC, H2], F32R)
            xlo = m.sb("xlo", [P, DC, H2], F32R)

        pY = [m.bank(f"pY{k}") for k in range(4)]
        pT = [m.bank(f"pT{k}") for k in range(2)]
        pH = [m.bank(f"pH{k}") for k in range(2)]

        bnl = m.sem("bn_loaded")
        wl = m.sem("taps_loaded")
        gs = m.sem("pairs_summed")
        ts = m.sem("tap_sums")
        tr_ = m.sem("taps_ready")
        wh = m.sem("tap_hi_ready")
        wo = m.sem("tap_lo_ready")
        chain = m.sem("dve_setup_chain")
        pows = m.sem("bn_powered")
        hset = m.sem("half_set")
        pads = m.sem("pads_zeroed")
        y_ld = m.sem("y_loaded")
        y_st = m.sem("y_stored")
        pr = m.sem("P_ready")
        dr = m.sem("D_ready")
        dh = m.sem("D_hi_ready")
        dl = m.sem("D_lo_ready")
        c2_0 = m.sem("conv2_chunk0_multiplied")
        c2 = m.sem("conv2_multiplied")
        mr0 = m.sem("M_first_ready")
        sr = m.sem("sums_ready")
        fr = m.sem("y_added")
        yr = m.sem("y_ready")

        if prepares:
            ld = m.sem("constants_loaded")
            cw = m.sem("conv1_weights_split")
            x_ld = m.sem("x_loaded")
            x_st = m.sem("x1_stored")
            xT_st = m.sem("x1T_stored")
            h_st = [m.sem(f"h_stored{k}") for k in range(2)]
            fadd = m.sem("fused_added")
            bst = m.sem("bn_stats_done")
            bag = m.sem("mean_var_done")
            vep = m.sem("var_eps_done")
            rst = m.sem("rstd_done")
            x1r = m.sem("x1_ready")
            tr = m.sem("x1_transposed")
            xTr = m.sem("x1T_ready")
            xhr = m.sem("x1T_hi_ready")
            xlr = m.sem("x1T_lo_ready")
            c1 = m.sem("conv1_multiplied")
            hr = m.sem("h_ready")
        else:
            h_ld = [m.sem(f"h_loaded{k}") for k in range(2)]

        first = lambda j: isinstance(j, int) and j == 0

        PS = (1, 0, 2)
        SUMS = [(c, j, 3 * a + max(0, k - 1), k) for a, c in enumerate(PS) for k, j in enumerate((0, 3, 1, 2))]
        NS, ND = len(SUMS), 9
        ADDS = {0: (0,), 3: (1,), 1: (0, 1), 2: (0, 1)}
        OPS = [(n, odd) for n, sm in enumerate(SUMS) if n > 1 for odd in ADDS[sm[1]]]
        SOPS = len(OPS)
        SUM_END = [sum(o[0] <= n for o in OPS) for n in range(NS)]
        START = {j: [(0, 0), (1, 1), (0, 3)] for j in (0, 1, 2)} | {3: [(1, 0), (0, 2), (1, 3)]}
        LAST_USE = [max(n for n, sm in enumerate(SUMS) if sm[2] == k) for k in range(ND)]
        DW = PQ - 1

        def schedule(body, eng):
            body(0, 0, True)
            with eng.Fori(0, PAIRS // 2 - 1) as turn:
                i = Turn(turn)
                for k in range(2):
                    body(2 * i + k + 1, 1 - k, True)
            body(PAIRS - 1, 1, False)

        def units(u):
            return [(e, e // 2, e % 2, 4 * u + e) for e in range(4)]

        def multiplied(u, k):
            return NS * (u if k >= 0 else u - 1) + LAST_USE[k % ND] + 1

        with nc.Block() as block:
            @block.sync
            def _(sp):
                def load_x(j):
                    if not first(j):
                        sp.wait_ge(x_st, val(16 * j))
                        sp.wait_ge(tr, val(4 * j))
                    sp.dma_start(xin[:, :, :], t["x"][val(j)]).then_inc(x_ld, 16)
                    sp.dma_start(fus[:, :], t["fused"][val(j)]).then_inc(x_ld, 16)

                def store_x1(j):
                    sp.wait_ge(x1r, val(NT * j + NT))
                    sp.dma_start(t["x1"][val(j)], xin[:, :, :]).then_inc(x_st, 16)

                def store_x1T(j, nh):
                    sp.wait_ge(xTr, val(2 * (2 * j + nh) + 2))
                    sp.dma_start(t["x1T"][val(j)][:, :, nh * H2:(nh + 1) * H2], xT[:]).then_inc(xT_st, 16)

                def store_h(u, s):
                    sp.wait_ge(hr, val(8 * u + 8))
                    sp.dma_start(t["h4"][val(u)], h4[:, s]).then_inc(h_st[s], 16)

                def load_h(u, s):
                    if not (isinstance(u, int) and u < 2):
                        sp.wait_ge(dr, val(ND * u - ND))
                    sp.dma_start(h4[:, s], t["h4"][val(u)]).then_inc(h_ld[s], 16)

                def x1T_in_dram(u, nxt):
                    if prepares:
                        sp.wait_ge(xT_st, val(64 * u + 64 + 32 * nxt))

                def store_y(u, q):
                    sp.dma_start(t["xcT"][val(2 * u + q)][:, co, :], y[:, q, :]).then_inc(y_st, 16)

                def turn_y(u, nxt):
                    if first(u):
                        x1T_in_dram(u, nxt)
                    else:
                        sp.wait_ge(yr, val(u))
                        store_y(u - 1, 0)
                        x1T_in_dram(u, nxt)
                        store_y(u - 1, 1)
                        sp.wait_ge(y_st, val(32 * u))
                    for q in range(2):
                        sp.dma_start(y[:, q, :], t["x1T"][val(2 * u + q)][:, co, :]).then_inc(y_ld, 16)

                def body(u, s, nxt):
                    if not (nxt and prepares):
                        if nxt:
                            load_h(u + 1, 1 - s)
                        turn_y(u, nxt)
                        return
                    j = 2 * (u + 1)
                    load_x(j)
                    store_x1(j)
                    store_x1T(j, 0)
                    store_x1T(j, 1)
                    load_x(j + 1)
                    turn_y(u, nxt)
                    store_x1(j + 1)
                    store_x1T(j + 1, 0)
                    store_x1T(j + 1, 1)
                    store_h(u + 1, 1 - s)

                def load_taps():
                    for i in range(DC):
                        sp.dma_start(raw[:, i, 0:TAPS, :], t["conv2_w"][:, i, :, co * P:(co + 1) * P]).then_inc(wl, 16)

                if prepares:
                    load_x(0)
                    sp.dma_start(bn[:], t["bn"]).then_inc(bnl, 16)
                    sp.dma_start(ident[:], t["ident"]).then_inc(ld, 16)
                    sp.dma_start(w1stage[:], t["conv1_w"]).then_inc(ld, 16)
                    load_taps()
                    for j in range(2):
                        if j:
                            load_x(j)
                        store_x1(j)
                        store_x1T(j, 0)
                        store_x1T(j, 1)
                    store_h(0, 0)
                else:
                    load_taps()
                    sp.dma_start(bn[:], t["bn"]).then_inc(bnl, 16)
                    load_h(0, 0)
                schedule(body, sp)
                sp.wait_ge(yr, PAIRS)
                for q in range(2):
                    store_y(PAIRS - 1, q)
                sp.wait_ge(y_st, 32 * PAIRS)
                if prepares:
                    sp.wait_ge(x_st, 16 * B)
                    sp.wait_ge(xT_st, 32 * B)
                    for s in range(2):
                        sp.wait_ge(h_st[s], 8 * PAIRS)

            @block.gpsimd
            def _(pool):
                nc.gpsimd.memset(half[:, :], -0.5).then_inc(hset, 1)
                nc.gpsimd.memset(raw[:, :, TAPS, :], 0.0).then_inc(pads, 1)
                if prepares:
                    for s in range(2):
                        nc.gpsimd.memset(h4[:, s, :, :, 0:PAD // 4], 0.0).then_inc(pads, 1)
                        nc.gpsimd.memset(h4[:, s, :, :, (PAD + N) // 4:HQ], 0.0).then_inc(pads, 1)
                pool.wait_ge(hset, 1)

                def rstd_of(j):
                    pool.wait_ge(vep, val(2 * j + 2))
                    nc.gpsimd.tensor_tensor(rstd[:, :], veps[:, :], half[:, :], ALU.pow).then_inc(rst, 1)
                    pool.wait_ge(rst, val(2 * j + 1))
                    nc.gpsimd.tensor_tensor(offset[:, :], negmean[:, :], rstd[:, :], ALU.mult).then_inc(rst, 1)

                def low_d(u, s, k):
                    a = (s + k) % 2
                    for i in range(DC):
                        pool.wait_ge(dh, val(DC * (ND * u + k) + i + 1))
                        ch = slice(2 * i, 2 * i + 2)
                        nc.gpsimd.tensor_tensor(Dlo[:, a, ch, :, 0:DW], Dt[:, a, ch, :, 0:DW],
                                                Dhi[:, a, ch, :, 0:DW].bitcast(F32), ALU.subtract).then_inc(dl, 1)

                def body(u, s, nxt):
                    for k in range(ND):
                        if nxt and prepares and k in (0, 5):
                            rstd_of(2 * (u + 1) + k // 5)
                        low_d(u, s, k)

                if prepares:
                    rstd_of(0)
                pool.wait_ge(chain, 1)
                nc.gpsimd.tensor_tensor(bnp[:].rearrange("p a c -> p (a c)"), scale[:].rearrange("p a c -> p (a c)"),
                                        half[:, 0:2 * DC], ALU.pow).then_inc(pows, 1)
                if prepares:
                    rstd_of(1)
                schedule(body, pool)

            @block.scalar
            def _(act):
                def taps_high(a):
                    for k, w in enumerate(taps_of(raw, pairs, tap, PS[a])):
                        if a == 0 and k == 0:
                            act.wait_ge(gs, 1)
                        if k == 2:
                            act.wait_ge(tr_, a + 1)
                        nc.scalar.copy(whi[:, :, PS[a], SUMS[k][1]], w).then_inc(wh, 1)

                def scale_x(j):
                    act.wait_ge(rst, val(2 * j + 2))
                    for k in range(NT):
                        nc.scalar.activation(xin[:, k, :], xin[:, k, :], ACT.Identity, scale=rstd[:, k:k + 1],
                                             bias=offset[:, k:k + 1]).then_inc(x1r, 1)

                def parts_x(u, e, q, nh, n):
                    for ci in range(DC):
                        act.wait_ge(tr, val(2 * n + ci + 1))
                        if ci == 0 and not first(n):
                            act.wait_ge(xT_st, val(16 * n))
                            act.wait_ge(xlr, val(n))
                            act.wait_ge(c1, val(2 * n))
                        nc.scalar.copy(xT[:, ci, :], pT[ci][:, :]).then_inc(xTr, 1)
                        nc.scalar.copy(xhi[:, ci, :], pT[ci][:, :]).then_inc(xhr, 1)

                def relu_h(u, s, e, q, nh, n):
                    for c in range(DC):
                        act.wait_ge(c1, val(2 * n + c + 1))
                        if e == 0 and c == 0 and not (isinstance(u, int) and u < 2):
                            act.wait_ge(dr, val(ND * u - ND))
                            act.wait_ge(h_st[s], val(8 * u - 8 * s))
                        at = PAD // 4 + nh * (H2 // 4)
                        nc.scalar.activation(h4[:, s, 2 * c + q, :, at:at + H2 // 4],
                                             pH[c][:, :].rearrange("p (w r) -> p r w", r=4), ACT.Relu,
                                             scale=scale[:, 0, c:c + 1], bias=shift[:, 0, c:c + 1]).then_inc(hr, 1)

                def high_d(u, s, k):
                    a = (s + k) % 2
                    act.wait_ge(dr, val(ND * u + k + 1))
                    for i in range(DC):
                        if not (first(u) and k < 2):
                            act.wait_ge(c2_0 if i == 0 else c2, val(multiplied(u, k - 2)))
                        ch = slice(2 * i, 2 * i + 2)
                        nc.scalar.copy(Dhi[:, a, ch, :, 0:DW], Dt[:, a, ch, :, 0:DW]).then_inc(dh, 1)

                def first_sums(u):
                    for k in range(2):
                        act.wait_ge(c2, val(NS * u + k + 1))
                        if not first(u) and k == 0:
                            act.wait_ge(fr, val(4 * u))
                        nc.scalar.activation(M0[:, k, :], pY[k][:, :], ACT.Copy, scale=1.0 - 2 * k).then_inc(mr0, 1)

                def finish(u):
                    act.wait_ge(fr, val(4 * u + 4))
                    nc.scalar.activation(y[:], y[:], ACT.Relu, bias=shift[:, 1, co:co + 1]).then_inc(yr, 1)

                def body(u, s, nxt):
                    unit = lambda e: units(u + 1)[e]
                    more = nxt and prepares
                    for k in range(ND):
                        high_d(u, s, k)
                        if k < 2 and first(u) and not prepares:
                            taps_high(k + 1)
                        if k == 1 and more:
                            scale_x(2 * (u + 1))
                        if k == 2:
                            first_sums(u)
                            if more:
                                parts_x(u + 1, *unit(0))
                        if k == 3 and more:
                            relu_h(u + 1, 1 - s, *unit(0))
                            parts_x(u + 1, *unit(1))
                        if k == 4:
                            if not first(u):
                                finish(u - 1)
                            if more:
                                relu_h(u + 1, 1 - s, *unit(1))
                        if k == 5 and more:
                            scale_x(2 * (u + 1) + 1)
                        if k == 6 and more:
                            parts_x(u + 1, *unit(2))
                        if k == 7 and more:
                            relu_h(u + 1, 1 - s, *unit(2))
                            parts_x(u + 1, *unit(3))
                            relu_h(u + 1, 1 - s, *unit(3))

                if prepares:
                    scale_x(0)
                    act.wait_ge(ld, 32)
                    nc.scalar.copy(w1hi[:], w1stage[:]).then_inc(cw, 1)
                    act.wait_ge(chain, 4)
                    for e, q, nh, n in units(0):
                        if e:
                            taps_high(e - 1)
                        parts_x(0, e, q, nh, n)
                        relu_h(0, 0, e, q, nh, n)
                        if e == 1:
                            scale_x(1)
                else:
                    taps_high(0)
                    act.wait_ge(chain, 4)
                schedule(body, act)
                finish(PAIRS - 1)

            @block.vector
            def _(v):
                def bn_coefficients():
                    v.wait_ge(bnl, 16)
                    nc.vector.tensor_scalar(scale[:, :, :], bn[:, :, 3, :], EPS, None, ALU.add).then_inc(chain, 1)
                    v.wait_ge(pows, 1)
                    nc.vector.tensor_tensor(scale[:, :, :], bn[:, :, 0, :], bnp[:, :, :], ALU.mult).then_inc(chain, 1)
                    v.wait_ge(chain, 2)
                    nc.vector.tensor_tensor(shift[:, :, :], bn[:, :, 2, :], scale[:, :, :], ALU.mult).then_inc(chain, 1)
                    v.wait_ge(chain, 3)
                    nc.vector.tensor_tensor(shift[:, :, :], bn[:, :, 1, :], shift[:, :, :], ALU.subtract).then_inc(chain, 1)

                def norm(j):
                    v.wait_ge(x_ld, val(32 * j + 32))
                    nc.vector.tensor_tensor(xin[0:GN, 0, :], xin[0:GN, 0, :], fus[:, :], ALU.add).then_inc(fadd, 1)
                    v.wait_ge(fadd, val(j + 1))
                    for k in range(NT):
                        nc.vector.bn_stats(stats[:, k, :], xin[:, k, :]).then_inc(bst, 1)
                    v.wait_ge(bst, val(NT * j + NT))
                    nc.vector.memset(mark[:, :], 0.0)
                    for k in range(NT):
                        nc.vector.bn_aggr(mv[:, k, :], stats[:, k, :]).then_inc(bag, 1)
                    v.wait_ge(bag, val(NT * j + NT))
                    nc.vector.tensor_scalar(veps[:, :], mv[:, :, 1], EPS, None, ALU.add).then_inc(vep, 1)
                    nc.vector.tensor_scalar(negmean[:, :], mv[:, :, 0], -1.0, None, ALU.mult).then_inc(vep, 1)

                def low_x(n):
                    v.wait_ge(xhr, val(2 * n + 2))
                    if not first(n):
                        v.wait_ge(c1, val(2 * n))
                    nc.vector.tensor_tensor(xlo[:], xT[:], xhi[:].bitcast(F32), ALU.subtract).then_inc(xlr, 1)

                def pair_taps():
                    v.wait_ge(wl, 16 * DC)
                    v.wait_ge(pads, 1)
                    nc.vector.tensor_tensor(pairs[:], raw[:, :, 0:18:2, :], raw[:, :, 1:18:2, :], ALU.add).then_inc(gs, 1)
                    v.wait_ge(gs, 1)

                def taps_low(a):
                    g = blocks_of(raw, pairs, PS[a])
                    if a:
                        v.wait_ge(wo, 4 * a)
                    nc.vector.tensor_tensor(tap[:, 0], g[:, :, :, 0], g[:, :, :, 2], ALU.add).then_inc(ts, 1)
                    outer, total = [tap[:, j].rearrange("p c l n -> p (c l) n") for j in range(2)]
                    middle = pairs[:].rearrange("p c k n -> p (c k) n")[:, 1::3, :] if PS[a] == 1 else \
                        raw[:].rearrange("p c k n -> p (c k) n")[:, PS[a] // 2 + 2::6, :]
                    nc.vector.tensor_scalar(middle, middle, 0.5, None, ALU.mult).then_inc(ts, 1)
                    v.wait_ge(ts, 3 * a + 2)
                    nc.vector.scalar_tensor_tensor(total, outer, 0.5, middle, ALU.mult, ALU.add).then_inc(ts, 1)
                    v.wait_ge(ts, 3 * a + 3)
                    nc.vector.scalar_tensor_tensor(outer, outer, 0.5, middle, ALU.mult, ALU.subtract).then_inc(tr_, 1)
                    v.wait_ge(tr_, a + 1)
                    for k, w in enumerate(taps_of(raw, pairs, tap, PS[a])):
                        v.wait_ge(wh, 4 * a + k + 1)
                        nc.vector.tensor_tensor(wlo[:, :, PS[a], SUMS[k][1]], w, whi[:, :, PS[a], SUMS[k][1]].bitcast(F32),
                                                ALU.subtract).then_inc(wo, 1)

                def stream(u, s, k):
                    c, j, a = PS[k // 3], k % 3, (s + k) % 2
                    X, to = h4[:, s], Dt[:, a]
                    if k == 0:
                        if prepares:
                            v.wait_ge(hr, val(8 * u + 8))
                            if first(u):
                                v.wait_ge(pads, 5)
                        else:
                            v.wait_ge(h_ld[s], val(8 * u - 8 * s + 16))
                    if j == 0 and c == 0:
                        nc.vector.tensor_tensor(Pt[:, :, :, :], X[:, :, 0::2, 0:PQ], X[:, :, 1::2, 0:PQ], ALU.subtract).then_inc(pr, 1)
                        v.wait_ge(pr, val(3 * u + 1))
                    if j == 0 and c == 2:
                        v.wait_ge(dr, val(ND * u + 6))
                        nc.vector.tensor_tensor(Pt[:, :, 0, :], X[:, :, 2, 0:PQ], X[:, :, 1, 0:PQ], ALU.subtract).then_inc(pr, 1)
                        nc.vector.tensor_tensor(Pt[:, :, 1, :], X[:, :, 0, 1:PQ + 1], X[:, :, 3, 0:PQ], ALU.subtract).then_inc(pr, 1)
                        v.wait_ge(pr, val(3 * u + 3))
                    S = X[:, :, 1::2, :] if c == 1 else Pt[:, :, :, :]
                    lo, hi = slice(0, DW), slice(1, DW + 1)
                    if not (first(u) and k < 2):
                        v.wait_ge(dl, val(DC * (ND * u + k - 1)))
                    if j == 0:
                        nc.vector.tensor_tensor(to[:, :, :, lo], S[:, :, :, lo], S[:, :, :, hi], ALU.subtract).then_inc(dr, 1)
                    elif j == 1:
                        nc.vector.tensor_tensor(to[:, :, 0, lo], S[:, :, 1, lo], S[:, :, 0, hi], ALU.add)
                        nc.vector.tensor_tensor(to[:, :, 1, lo], S[:, :, 0, hi], S[:, :, 1, hi], ALU.add).then_inc(dr, 1)
                    else:
                        nc.vector.tensor_tensor(to[:, :, 0, lo], S[:, :, 0, hi], S[:, :, 1, lo], ALU.subtract)
                        nc.vector.tensor_tensor(to[:, :, 1, lo], S[:, :, 1, hi], S[:, :, 0, hi], ALU.subtract).then_inc(dr, 1)

                def sums(u, n):
                    c, j, _k, _o = SUMS[n]
                    if n == 2:
                        v.wait_ge(mr0, val(2 * u + 2))
                    v.wait_ge(c2, val(NS * u + n + 1))
                    to = Y0 if c == 0 else M0
                    for odd in ADDS[j]:
                        op = ALU.subtract if (j == 3 or (j == 2 and odd)) else ALU.add
                        so_far = M0 if c == 0 and j in (0, 3) else to
                        v.wait_ge(sr, val(SOPS * u + OPS.index((n, odd))))
                        nc.vector.tensor_tensor(to[:, odd, :], so_far[:, odd, :], pY[n % 4][:, :], op).then_inc(sr, 1)

                def add_up(u):
                    v.wait_ge(y_ld, val(32 * u + 32))
                    v.wait_ge(sr, val(SOPS * u + SOPS))
                    for p, src in enumerate((Y0, M0)):
                        for odd in range(2):
                            view = y[:].rearrange("p b (w r) -> p b w r", r=4)[:, :, :, 2 * odd + p]
                            nc.vector.scalar_tensor_tensor(view, src[:, odd, :].rearrange("p (b w) -> p b w", b=2),
                                                           scale[:, 1, co:co + 1], view, ALU.mult, ALU.add).then_inc(fr, 1)

                def body(u, s, nxt):
                    more = nxt and prepares
                    if more:
                        norm(2 * (u + 1))
                    for k in range(ND):
                        stream(u, s, k)
                        if k < 2 and first(u) and not prepares:
                            taps_low(k + 1)
                        if k < 4 and not first(u):
                            sums(u - 1, 8 + k)
                        if k == 3 and not first(u):
                            add_up(u - 1)
                        if k == 4 and more:
                            low_x(4 * (u + 1))
                        if k == 5:
                            sums(u, 2)
                            if more:
                                low_x(4 * (u + 1) + 1)
                                norm(2 * (u + 1) + 1)
                        if k == 6:
                            sums(u, 3)
                            sums(u, 4)
                        if k == 7:
                            sums(u, 5)
                            sums(u, 6)
                            if more:
                                low_x(4 * (u + 1) + 2)
                        if k == 8:
                            sums(u, 7)
                            if more:
                                low_x(4 * (u + 1) + 3)

                if prepares:
                    norm(0)
                    bn_coefficients()
                    v.wait_ge(cw, 1)
                    nc.vector.tensor_tensor(w1lo[:], w1stage[:], w1hi[:].bitcast(F32), ALU.subtract).then_inc(cw, 1)
                    pair_taps()
                    for e in range(4):
                        if e:
                            taps_low(e - 1)
                        low_x(e)
                        if e == 1:
                            norm(1)
                    v.wait_ge(wo, 12)
                    v.wait_ge(cw, 2)
                else:
                    pair_taps()
                    taps_low(0)
                    bn_coefficients()
                schedule(body, v)
                for n in range(8, NS):
                    sums(PAIRS - 1, n)
                add_up(PAIRS - 1)

            @block.tensor
            def _(pe):
                def transposes(u, e, q, nh, n):
                    for ci in range(DC):
                        pe.wait_ge(x1r, val(NT * (2 * u + q) + 4 * nh + 4))
                        if not first(n):
                            pe.wait_ge(xhr, val(2 * n + ci - 1))
                        for k in range(4):
                            ins = nc.tensor.transpose(pT[ci][:, k * P:(k + 1) * P],
                                                      xin[:, 4 * nh + k, ci * P:(ci + 1) * P], ident[:, :])
                        ins.then_inc(tr, 1)

                def conv1(u, e, q, nh, n):
                    pe.wait_ge(xlr, val(n + 1))
                    for c in range(DC):
                        if not first(n):
                            pe.wait_ge(hr, val(2 * n + c - 1))
                        cs = slice(c * P, (c + 1) * P)
                        products(nc, pH[c][:, :], [(w1hi[:, i, cs], w1lo[:, i, cs], xhi[:, i, :], xlo[:, i, :])
                                                   for i in range(DC)]).then_inc(c1, 1)

                def conv2(u, s, n):
                    c, j, k, o = SUMS[n]
                    a = (s + k) % 2
                    if first(u):
                        pe.wait_ge(wo, n + 1)
                    if n in (4, 5):
                        pe.wait_ge(mr0, val(2 * u + n - 3))
                    elif not (first(u) and n < 4):
                        pe.wait_ge(sr, val(SOPS * (u if n >= 4 else u - 1) + SUM_END[(n - 4) % NS]))
                    for ci in range(DC):
                        pe.wait_ge(dl, val(DC * (ND * u + k) + ci + 1))
                        steps = []
                        for L in range(3):
                            if (c, j, L) == (2, 3, 2):
                                continue
                            par, at = START[j][L]
                            cols = [d[:, a, 2 * ci:2 * ci + 2, par, at:at + H2 // 2] for d in (Dhi, Dlo)]
                            steps.append((whi[:, ci, c, j, L, :], wlo[:, ci, c, j, L, :], cols[0], cols[1]))
                        products(nc, pY[n % 4][:, :].rearrange("p (b w) -> p b w", b=2), steps,
                                 start=ci == 0, stop=ci == DC - 1).then_inc(c2_0 if ci == 0 else c2, 1)

                def body(u, s, nxt):
                    turned, convolved = {1: 0, 2: 1, 6: 2, 7: 3}, {2: 0, 4: 1, 7: 2, 8: 3}
                    for n in range(NS):
                        conv2(u, s, n)
                        if nxt and prepares and n in turned:
                            transposes(u + 1, *units(u + 1)[turned[n]])
                        if nxt and prepares and n in convolved:
                            conv1(u + 1, *units(u + 1)[convolved[n]])

                if prepares:
                    pe.wait_ge(ld, 32)
                    for unit in units(0):
                        transposes(0, *unit)
                        if unit[0] == 0:
                            pe.wait_ge(cw, 2)
                        conv1(0, *unit)
                schedule(body, pe)


def blocks_of(raw, pairs, c):
    g = pairs[:] if c == 1 else raw[:, :, c // 2:18:2, :]
    return g.rearrange("p c (l i) n -> p c l i n", i=3)


def taps_of(raw, pairs, tap, c):
    g = blocks_of(raw, pairs, c)
    return g[:, :, :, 0], g[:, :, :, 2], tap[:, 1], tap[:, 0]


def nodes_stage(nc, t):
    with ExitStack() as ctx:
        m = Space(nc, ctx, "n")
        SR = 12
        LR = 16
        XK = 2 * DC
        wst = m.sb("wst", [P, 3 * D])
        wihh = m.sb("wihh", [P, XK, 3 * D], F32R)
        wihl = m.sb("wihl", [P, XK, 3 * D], F32R)
        whhh = m.sb("whhh", [P, DC, 3 * D], F32R)
        whhl = m.sb("whhl", [P, DC, 3 * D], F32R)
        wmh = m.sb("wmh", [P, DC, D], F32R)
        wml = m.sb("wml", [P, DC, D], F32R)
        wseh = m.sb("wseh", [P, DC, SR], F32R)
        wsel = m.sb("wsel", [P, DC, SR], F32R)
        wse = m.sb("wse", [P, DC, SR])
        bse = m.sb("bse", [SR, 1])
        selA = m.sb("selA", [SR, SELW])
        selB = m.sb("selB", [SR, SELW])
        rows = m.sb("rows", [LR, 6])
        bih = m.sb("bih", [P, 3 * D])
        bn_ = m.sb("bn", [P, 2 * D])
        bmsg = m.sb("bmsg", [P, D])
        half = m.sb("half", [P, 1])

        xstg = m.sb("xstg", [P, DC, H2])
        cstg = m.sb("cstg", [P, DC, H2])
        xhi = m.sb("xhi", [P, 2, DC, N], F32R)
        xlo = m.sb("xlo", [P, 2, DC, N], F32R)
        chi = m.sb("chi", [P, 2, DC, H2], F32R)
        clo = m.sb("clo", [P, 2, DC, H2], F32R)
        mhi = m.sb("mhi", [P, 2, DC, H2], F32R)
        mlo = m.sb("mlo", [P, 2, DC, H2], F32R)
        s1 = m.sb("s1", [SR, 2, H2])
        s2 = m.sb("s2", [SR, 2, H2])
        vhi = m.sb("vhi", [LR, H2])
        vlo = m.sb("vlo", [LR, H2])
        vt = m.sb("vt", [LR, 2, H2])
        Lr = m.sb("Lr", [LR, N], F32R)
        Rr = m.sb("Rr", [LR, N], F32R)
        mt_ = m.sb("mt", [P, 2, D])
        msgh = m.sb("msgh", [P, NT, D], F32R)
        msgl = m.sb("msgl", [P, NT, D], F32R)
        adj = m.sb("adj", [P, 4, H2])
        E = m.sb("E", [P, 2, H2])
        A32 = m.sb("A32", [P, 2, H2])
        Ahi = m.sb("Ahi", [P, 3, H2], F32R)
        Alo = m.sb("Alo", [P, 3, H2], F32R)
        x1 = m.sb("x1", [P, 2, D])
        rz = m.sb("rz", [P, 2 * D])
        th = m.sb("th", [P, 2 * D])
        gn = m.sb("gn", [P, 2 * D])
        t1 = m.sb("t1", [P, D])
        t2 = m.sb("t2", [P, D])
        nn = m.sb("nn", [P, D])
        dd = m.sb("dd", [P, D])
        ee, ff = t1, t2
        res = m.sb("res", [P, D])
        stats = m.sb("stats", [P, 6])
        mv = m.sb("mv", [P, 2])
        mark = m.sb("mark", [P, 1])
        veps = m.sb("veps", [P, 1])
        rstd = m.sb("rstd", [P, 1])
        outt = m.sb("outt", [P, 2, D])

        pN = [m.bank(f"pN{k}") for k in range(2)]
        pD = [m.bank(f"pD{k}") for k in range(2)]
        pRZ = m.bank("pRZ")
        pG = m.bank("pG")
        pP = [m.bank(f"pP{k}") for k in range(2)]

        ld = m.sem("constants_loaded")
        wl = m.sem("weights_staged")
        wh = m.sem("weights_hi")
        wo = m.sem("weights_lo")
        bs = m.sem("biases_summed")
        hs = m.sem("half_set")
        xl = m.sem("x1T_loaded")
        cl = m.sem("xcT_loaded")
        xh_r = m.sem("x1T_hi_ready")
        xl_r = m.sem("x1T_lo_ready")
        ch_r = m.sem("xcT_hi_ready")
        cl_r = m.sem("xcT_lo_ready")
        s_m = m.sem("s_multiplied")
        s_r = m.sem("s_ready")
        s2_r = m.sem("s_squared")
        v_m = m.sem("rows_multiplied")
        vh_r = m.sem("rows_hi")
        vl_r = m.sem("rows_lo")
        vt_r = m.sem("rows_partial")
        lr_r = m.sem("LR_ready")
        mg_m = m.sem("msg_multiplied")
        mg_t = m.sem("msg_biased")
        mg_h = m.sem("msg_hi_ready")
        mg_l = m.sem("msg_lo_ready")
        al = [m.sem(f"adj_loaded{k}") for k in range(4)]
        d_m = m.sem("dist_multiplied")
        e_r = m.sem("E_ready")
        a_r = m.sem("A_ready")
        ah_r = m.sem("A_hi_ready")
        alo_r = m.sem("A_lo_ready")
        av = m.sem("A_multiplied")
        nh_r = m.sem("nmp_hi_ready")
        nl_r = m.sem("nmp_lo_ready")
        x1l = [m.sem(f"x1_loaded{k}") for k in range(2)]
        rz_m = m.sem("rz_multiplied")
        gn_m = m.sem("n_multiplied")
        rz_r = m.sem("rz_biased")
        gn_r = m.sem("n_biased")
        th_r = m.sem("rz_tanh")
        tt1 = m.sem("r_gh_n")
        tt2 = m.sem("n_arg")
        n_r = m.sem("n_ready")
        g_d = m.sem("x_minus_n")
        g_e = m.sem("z_scaled")
        g_f = m.sem("update_ready")
        g_r = m.sem("residual_ready")
        g_s = m.sem("stats_ready")
        g_a = m.sem("mean_var_ready")
        g_v = m.sem("var_eps_ready")
        g_p = m.sem("rstd_ready")
        o_r = m.sem("out_ready")
        o_st = [m.sem(f"out_stored{k}") for k in range(2)]

        WTS = ([(t["w_ih"][:, k, :], wihh[:, k, :], wihl[:, k, :], 3 * D) for k in range(XK)]
               + [(t["w_hh"][:, k, :], whhh[:, k, :], whhl[:, k, :], 3 * D) for k in range(DC)]
               + [(t["w_msg"][:, k, :], wmh[:, k, :], wml[:, k, :], D) for k in range(DC)])
        NW = len(WTS)
        first = lambda j: isinstance(j, int) and j == 0

        STEPS = 2 * NT

        def schedule(prep, body, eng):
            prep(0, 0)
            body(0, 0, False, True)
            with eng.Fori(0, B // 2 - 1) as turn:
                i = Turn(turn)
                for k in range(2):
                    body(2 * i + k + 1, 1 - k, True, True)
            body(B - 1, 1, True, False)

        def gate_tile(b, p, back=0):
            k = p - back - DC * 2
            return (b, k) if k >= 0 else (b - 1, k + NT)

        def has_gates(gates, p):
            return gates or p >= NT // 2

        with nc.Block() as block:
            @block.sync
            def _(sp):
                for dst, src in ((wse, t["w_se"]), (bse, t["b_se"]), (selA, t["selA"]), (selB, t["selB"]),
                                 (rows, t["rows"]), (bih, t["b_ih"]), (wst, t["b_hh"]), (bmsg, t["b_msg"])):
                    sp.dma_start(dst[:], src).then_inc(ld, 16)
                sp.wait_ge(bs, 3)
                for n, (src, _h, _l, w) in enumerate(WTS):
                    if n:
                        sp.wait_ge(wo, val(n))
                    sp.dma_start(wst[:, 0:w], src).then_inc(wl, 16)

                def load_xT(b, h):
                    if not (first(b) and h == 0):
                        sp.wait_ge(xl_r, val(2 * b + h))
                    sp.dma_start(xstg[:], t["x1T"][val(b)][:, :, h * H2:(h + 1) * H2]).then_inc(xl, 16)

                def load_xc(b, h):
                    if not (first(b) and h == 0):
                        sp.wait_ge(cl_r, val(2 * b + h))
                    sp.dma_start(cstg[:], t["xcT"][val(b)][:, :, h * H2:(h + 1) * H2]).then_inc(cl, 16)

                def load_adj(b, n):
                    h, k = divmod(n, NT)
                    if not (first(b) and n < 4):
                        sp.wait_ge(a_r, val(STEPS * b + n - 3))
                    sp.dma_start(adj[:, n % 4, :], t["adjT"][val(b)][:, k, h * H2:(h + 1) * H2]).then_inc(al[n % 4], 16)

                def load_x1(g_b, g_k):
                    if not (first(g_b) and g_k < 2):
                        sp.wait_ge(g_r, val(NT * g_b + g_k - 1))
                    sp.dma_start(x1[:, g_k % 2, :], t["x1"][val(g_b)][:, g_k, :]).then_inc(x1l[g_k % 2], 16)

                def store(g_b, g_k):
                    sp.wait_ge(o_r, val(NT * g_b + g_k + 1))
                    sp.dma_start(t["out"][val(g_b)][:, g_k, :], outt[:, g_k % 2, :]).then_inc(o_st[g_k % 2], 16)

                def prep(b, s):
                    for h in range(2):
                        load_xT(b, h)
                    for n in range(2):
                        load_adj(b, n)

                def body(b, s, gates, nxt):
                    for n in range(STEPS):
                        p = n // 2
                        if n + 2 < STEPS:
                            load_adj(b, n + 2)
                        elif nxt:
                            load_adj(b + 1, n + 2 - STEPS)
                        if n % NT == 0:
                            load_xc(b, n // NT)
                        if nxt and n in (8, 11):
                            load_xT(b + 1, (n - 8) // 3)
                        if n % 2 == 0 and has_gates(gates, p):
                            load_x1(*gate_tile(b, p))
                        if n % 2 == 1 and (gates or p >= NT // 2 + 2):
                            store(*gate_tile(b, p, 2))

                schedule(prep, body, sp)
                for k in range(2, NT):
                    if k >= 4:
                        load_x1(B - 1, k)
                    store(B - 1, k)
                for k in range(2):
                    sp.wait_ge(o_st[k], 16 * B * NT // 2)

            @block.gpsimd
            def _(pool):
                nc.gpsimd.memset(half[:, :], -0.5).then_inc(hs, 1)
                pool.wait_ge(hs, 1)

                def split_x(b, s, h):
                    pool.wait_ge(xh_r, val(2 * b + h + 1))
                    nc.gpsimd.tensor_tensor(xlo[:, s, :, h * H2:(h + 1) * H2], xstg[:],
                                            xhi[:, s, :, h * H2:(h + 1) * H2].bitcast(F32), ALU.subtract).then_inc(xl_r, 1)

                def split_c(b, h):
                    pool.wait_ge(ch_r, val(2 * b + h + 1))
                    nc.gpsimd.tensor_tensor(clo[:, h], cstg[:], chi[:, h].bitcast(F32), ALU.subtract).then_inc(cl_r, 1)

                def low_A(b, n):
                    pool.wait_ge(ah_r, val(STEPS * b + n + 1))
                    a = n % 3
                    nc.gpsimd.tensor_tensor(Alo[:, a], A32[:, n % 2], Ahi[:, a].bitcast(F32),
                                            ALU.subtract).then_inc(alo_r, 1)

                def rstd_of(g_b, g_k):
                    pool.wait_ge(g_v, val(NT * g_b + g_k + 1))
                    nc.gpsimd.tensor_tensor(rstd[:, :], veps[:, :], half[:, :], ALU.pow).then_inc(g_p, 1)

                def prep(b, s):
                    for h in range(2):
                        split_x(b, s, h)

                def body(b, s, gates, nxt):
                    for n in range(STEPS):
                        p = n // 2
                        low_A(b, n)
                        if n % NT == 3:
                            split_c(b, n // NT)
                        if nxt and n in (10, 13):
                            split_x(b + 1, 1 - s, (n - 10) // 3)
                        if n % 2 == 1 and p and has_gates(gates, p - 1):
                            rstd_of(*gate_tile(b, p, 1))
                    rstd_of(*gate_tile(b, NT - 1))

                schedule(prep, body, pool)
                for k in range(4):
                    rstd_of(B - 1, 4 + k)

            @block.scalar
            def _(act):
                act.wait_ge(ld, 128)
                for n, (_s, hi, _l, w) in enumerate(WTS):
                    act.wait_ge(wl, val(16 * n + 16))
                    nc.scalar.copy(hi, wst[:, 0:w]).then_inc(wh, 1)
                nc.scalar.copy(wseh[:], wse[:]).then_inc(wh, 1)

                def split_x(b, s, h):
                    act.wait_ge(xl, val(32 * b + 16 * h + 16))
                    if h == 0 and not (isinstance(b, int) and b < 2):
                        act.wait_ge(gn_m, val(8 * b - 8))
                    nc.scalar.copy(xhi[:, s, :, h * H2:(h + 1) * H2], xstg[:]).then_inc(xh_r, 1)

                def prep(b, s):
                    for h in range(2):
                        act.wait_ge(s_m, val(2 * b + h + 1))
                        if not first(b):
                            act.wait_ge(v_m, val(2 * b - 1 + h))
                        nc.scalar.activation(s1[:, h, :], pP[h][0:SR, :], ACT.Identity, bias=bse[:, :]).then_inc(s_r, 1)
                    for k in range(NT):
                        act.wait_ge(mg_t, val(8 * b + k + 1))
                        nc.scalar.activation(msgh[:, k, :], mt_[:, k % 2, :], ACT.Relu).then_inc(mg_h, 1)
                        if k in (1, 3):
                            h = k // 2
                            act.wait_ge(v_m, val(2 * b + h + 1))
                            if not (first(b) and h == 0):
                                act.wait_ge(lr_r, val(4 * b + 2 * h))
                            nc.scalar.copy(vhi[:, :].bitcast(F32R), pD[h][0:LR, :]).then_inc(vh_r, 1)

                def exps(b, n):
                    act.wait_ge(d_m, val(STEPS * b + n + 1))
                    if not (first(b) and n < 2):
                        act.wait_ge(a_r, val(STEPS * b + n - 1))
                    nc.scalar.activation(E[:, n % 2], pD[n % 2][:, :], ACT.Exp).then_inc(e_r, 1)

                def hi_A(b, n):
                    act.wait_ge(a_r, val(STEPS * b + n + 1))
                    if n >= 3:
                        act.wait_ge(av, val(STEPS * b + n - 2))
                    elif not first(b):
                        act.wait_ge(av, val(STEPS * b))
                    nc.scalar.copy(Ahi[:, n % 3], A32[:, n % 2]).then_inc(ah_r, 1)

                def hi_c(b, h):
                    act.wait_ge(cl, val(32 * b + 16 * h + 16))
                    if not first(b):
                        act.wait_ge(gn_m, val(8 * b - 8 + 4 * h + 4))
                    nc.scalar.copy(chi[:, h], cstg[:]).then_inc(ch_r, 1)

                def hi_n(b, h):
                    act.wait_ge(av, val(16 * b + 8 * h + 8))
                    if not first(b):
                        act.wait_ge(gn_m, val(8 * b - 8 + 4 * h + 4))
                    for c in range(DC):
                        nc.scalar.copy(mhi[:, h, c, :], pN[c][:, :]).then_inc(nh_r, 1)

                def tanh_rz(g_b, g_k):
                    g = NT * g_b + g_k
                    act.wait_ge(rz_r, val(g + 1))
                    if not (first(g_b) and g_k == 0):
                        act.wait_ge(g_e, val(g))
                    nc.scalar.activation(th[:, :], rz[:, :], ACT.Tanh, scale=0.5).then_inc(th_r, 1)

                def tanh_n(g_b, g_k):
                    g = NT * g_b + g_k
                    act.wait_ge(tt2, val(g + 1))
                    if not (first(g_b) and g_k == 0):
                        act.wait_ge(g_f, val(g))
                    nc.scalar.activation(nn[:, :], t2[:, :], ACT.Tanh).then_inc(n_r, 1)

                def body(b, s, gates, nxt):
                    exps(b, 0)
                    exps(b, 1)
                    hi_A(b, 0)
                    for n in range(STEPS):
                        p = n // 2
                        if n == NT:
                            hi_n(b, 0)
                        if n + 2 < STEPS:
                            exps(b, n + 2)
                        if n + 1 < STEPS:
                            hi_A(b, n + 1)
                        if n % NT == 2:
                            hi_c(b, n // NT)
                        if nxt and n in (9, 12):
                            split_x(b + 1, 1 - s, (n - 9) // 3)
                        if has_gates(gates, p):
                            (tanh_n if n % 2 else tanh_rz)(*gate_tile(b, p))
                    hi_n(b, 1)
                    if nxt:
                        prep(b + 1, 1 - s)

                for h in range(2):
                    split_x(0, 0, h)
                schedule(prep, body, act)
                for k in range(4, NT):
                    tanh_rz(B - 1, k)
                    tanh_n(B - 1, k)

            @block.vector
            def _(v):
                v.wait_ge(ld, 128)
                nc.vector.tensor_tensor(bih[:, 0:2 * D], bih[:, 0:2 * D], wst[:, 0:2 * D], ALU.add).then_inc(bs, 1)
                nc.vector.tensor_copy(bn_[:, D:2 * D], wst[:, 2 * D:3 * D]).then_inc(bs, 1)
                nc.vector.tensor_copy(bn_[:, 0:D], bih[:, 2 * D:3 * D]).then_inc(bs, 1)
                v.wait_ge(bs, 3)
                for n, (_s, hi, lo, w) in enumerate(WTS):
                    v.wait_ge(wh, val(n + 1))
                    nc.vector.tensor_tensor(lo, wst[:, 0:w], hi.bitcast(F32), ALU.subtract).then_inc(wo, 1)
                v.wait_ge(wh, NW + 1)
                nc.vector.tensor_tensor(wsel[:], wse[:], wseh[:].bitcast(F32), ALU.subtract).then_inc(wo, 1)

                def operands(b, h):
                    sl = slice(h * H2, (h + 1) * H2)
                    v.wait_ge(vh_r, val(2 * b + h + 1))
                    nc.vector.tensor_tensor(vlo[:, :], pD[h][0:LR, :], vhi[:, :], ALU.subtract).then_inc(vl_r, 1)
                    nc.vector.tensor_scalar(vt[:, 0, :], vhi[:, :], rows[:, 0:1], rows[:, 2:3], ALU.mult, ALU.add).then_inc(vt_r, 1)
                    nc.vector.tensor_scalar(vt[:, 1, :], vhi[:, :], rows[:, 3:4], rows[:, 5:6], ALU.mult, ALU.add).then_inc(vt_r, 1)
                    v.wait_ge(vl_r, val(2 * b + h + 1))
                    v.wait_ge(vt_r, val(4 * b + 2 * h + 2))
                    if not first(b):
                        v.wait_ge(d_m, val(16 * b))
                    nc.vector.scalar_tensor_tensor(Lr[:, sl], vlo[:, :], rows[:, 1:2], vt[:, 0, :], ALU.mult, ALU.add).then_inc(lr_r, 1)
                    nc.vector.scalar_tensor_tensor(Rr[:, sl], vlo[:, :], rows[:, 4:5], vt[:, 1, :], ALU.mult, ALU.add).then_inc(lr_r, 1)
                    v.wait_ge(lr_r, val(4 * b + 2 * h + 2))

                def prep(b, s):
                    for h in range(2):
                        v.wait_ge(s_r, val(2 * b + h + 1))
                        if not first(b):
                            v.wait_ge(v_m, val(2 * b - 1 + h))
                        nc.vector.tensor_tensor(s2[:, h, :], s1[:, h, :], s1[:, h, :], ALU.mult).then_inc(s2_r, 1)
                    for k in range(NT + 1):
                        if k < NT:
                            v.wait_ge(mg_m, val(8 * b + k + 1))
                            if not (first(b) and k < 2):
                                v.wait_ge(mg_l, val(8 * b + k - 1))
                            nc.vector.tensor_tensor(mt_[:, k % 2, :], pP[k % 2][:, 0:D], bmsg[:, :], ALU.add).then_inc(mg_t, 1)
                        if k:
                            v.wait_ge(mg_h, val(8 * b + k))
                            nc.vector.scalar_tensor_tensor(msgl[:, k - 1, :], mt_[:, (k - 1) % 2, :], 0.0,
                                                           msgh[:, k - 1, :].bitcast(F32), ALU.max, ALU.subtract).then_inc(mg_l, 1)
                        if k in (2, 4):
                            operands(b, k // 2 - 1)

                def mask(b, n):
                    v.wait_ge(e_r, val(STEPS * b + n + 1))
                    v.wait_ge(al[n % 4], val(64 * b + 16 * (n // 4) + 16))
                    if not (first(b) and n < 2):
                        v.wait_ge(alo_r, val(STEPS * b + n - 1))
                    nc.vector.tensor_tensor(A32[:, n % 2], E[:, n % 2], adj[:, n % 4], ALU.mult).then_inc(a_r, 1)

                def low_n(b, h):
                    for c in range(DC):
                        v.wait_ge(nh_r, val(4 * b + 2 * h + c + 1))
                        nc.vector.tensor_tensor(mlo[:, h, c, :], pN[c][:, :], mhi[:, h, c, :].bitcast(F32), ALU.subtract).then_inc(nl_r, 1)

                def bias_rz(g_b, g_k):
                    g = NT * g_b + g_k
                    v.wait_ge(rz_m, val(g + 1))
                    if not (first(g_b) and g_k == 0):
                        v.wait_ge(th_r, val(g))
                    nc.vector.tensor_tensor(rz[:, :], pRZ[:, :], bih[:, 0:2 * D], ALU.add).then_inc(rz_r, 1)

                def n_arg(g_b, g_k):
                    g = NT * g_b + g_k
                    v.wait_ge(gn_m, val(g + 1))
                    nc.vector.tensor_tensor(gn[:, :], pG[:, :], bn_[:, :], ALU.add).then_inc(gn_r, 1)
                    v.wait_ge(gn_r, val(g + 1))
                    v.wait_ge(th_r, val(g + 1))
                    nc.vector.scalar_tensor_tensor(t1[:, :], th[:, 0:D], 1.0, gn[:, D:2 * D], ALU.add, ALU.mult).then_inc(tt1, 1)
                    v.wait_ge(tt1, val(g + 1))
                    nc.vector.scalar_tensor_tensor(t2[:, :], t1[:, :], 0.5, gn[:, 0:D], ALU.mult, ALU.add).then_inc(tt2, 1)

                def update(g_b, g_k):
                    g = 8 * g_b + g_k
                    v.wait_ge(n_r, val(g + 1))
                    v.wait_ge(x1l[g_k % 2], val(64 * g_b + 16 * (g_k // 2) + 16))
                    nc.vector.tensor_tensor(dd[:, :], x1[:, g_k % 2, :], nn[:, :], ALU.subtract).then_inc(g_d, 1)
                    v.wait_ge(g_d, val(g + 1))
                    nc.vector.scalar_tensor_tensor(ee[:, :], th[:, D:2 * D], 1.0, dd[:, :], ALU.add, ALU.mult).then_inc(g_e, 1)
                    v.wait_ge(g_e, val(g + 1))
                    nc.vector.scalar_tensor_tensor(ff[:, :], ee[:, :], 0.5, nn[:, :], ALU.mult, ALU.add).then_inc(g_f, 1)
                    v.wait_ge(g_f, val(g + 1))
                    nc.vector.tensor_tensor(res[:, :], ff[:, :], x1[:, g_k % 2, :], ALU.add).then_inc(g_r, 1)
                    v.wait_ge(g_r, val(g + 1))
                    nc.vector.bn_stats(stats[:, :], res[:, :]).then_inc(g_s, 1)
                    v.wait_ge(g_s, val(g + 1))
                    nc.vector.memset(mark[:, :], 0.0)
                    nc.vector.bn_aggr(mv[:, :], stats[:, :]).then_inc(g_a, 1)
                    v.wait_ge(g_a, val(g + 1))
                    nc.vector.tensor_scalar(veps[:, :], mv[:, 1:2], EPS, None, ALU.add).then_inc(g_v, 1)

                def norm(g_b, g_k):
                    g = 8 * g_b + g_k
                    v.wait_ge(g_p, val(g + 1))
                    if not (first(g_b) and g_k < 2):
                        v.wait_ge(o_st[g_k % 2], val(64 * g_b + 16 * (g_k // 2)))
                    nc.vector.tensor_scalar(outt[:, g_k % 2, :], res[:, :], mv[:, 0:1], rstd[:, :],
                                            ALU.subtract, ALU.mult).then_inc(o_r, 1)

                def body(b, s, gates, nxt):
                    mask(b, 0)
                    mask(b, 1)
                    for n in range(STEPS):
                        p = n // 2
                        if n == NT:
                            low_n(b, 0)
                        if n + 2 < STEPS:
                            mask(b, n + 2)
                        if p and has_gates(gates, p - 1):
                            (norm if n % 2 else update)(*gate_tile(b, p, 1))
                        if has_gates(gates, p):
                            (n_arg if n % 2 else bias_rz)(*gate_tile(b, p))
                    low_n(b, 1)
                    update(*gate_tile(b, NT - 1))
                    norm(*gate_tile(b, NT - 1))
                    if nxt:
                        prep(b + 1, 1 - s)

                schedule(prep, body, v)
                for k in range(4, NT):
                    bias_rz(B - 1, k)
                    n_arg(B - 1, k)
                    update(B - 1, k)
                    norm(B - 1, k)

            @block.tensor
            def _(pe):
                pe.wait_ge(wo, NW + 1)
                pe.wait_ge(ld, 128)

                def prep(b, s):
                    for h in range(2):
                        sl = slice(h * H2, (h + 1) * H2)
                        pe.wait_ge(xl_r, val(2 * b + h + 1))
                        if h == 0 and not first(b):
                            pe.wait_ge(mg_t, val(8 * b))
                        products(nc, pP[h][0:SR, :], [(wseh[:, c, :], wsel[:, c, :], xhi[:, s, c, sl], xlo[:, s, c, sl])
                                                      for c in range(DC)]).then_inc(s_m, 1)
                    for k in range(NT):
                        if k < 2:
                            pe.wait_ge(s_r, val(2 * b + k + 1))
                        else:
                            pe.wait_ge(mg_t, val(8 * b + k - 1))
                        products(nc, pP[k % 2][:, 0:D], [(xhi[:, s, c, k * P:(k + 1) * P], xlo[:, s, c, k * P:(k + 1) * P],
                                                          wmh[:, c, :], wml[:, c, :]) for c in range(DC)]).then_inc(mg_m, 1)
                        if k in (1, 3):
                            h = k // 2
                            pe.wait_ge(s_r, val(2 * b + h + 1))
                            pe.wait_ge(s2_r, val(2 * b + h + 1))
                            if h == 0 and not first(b):
                                pe.wait_ge(e_r, val(16 * b))
                            nc.tensor.matmul(pD[h][0:SELW, :], selA[:, :], s1[:, h, :], start=True, stop=False)
                            nc.tensor.matmul(pD[h][0:SELW, :], selB[:, :], s2[:, h, :], start=False, stop=True).then_inc(v_m, 1)
                        if k >= NT - 2:
                            dist(b, k - NT + 2)

                def dist(b, n):
                    h, k = divmod(n, NT)
                    if n == 0:
                        pe.wait_ge(lr_r, val(4 * b + 4))
                    if not (first(b) and n < 2):
                        pe.wait_ge(e_r, val(STEPS * b + n - 1))
                    nc.tensor.matmul(pD[n % 2][:, :], Lr[:, k * P:(k + 1) * P], Rr[:, h * H2:(h + 1) * H2],
                                     start=True, stop=True).then_inc(d_m, 1)

                def gather(b, n):
                    h, k = divmod(n, NT)
                    pe.wait_ge(alo_r, val(STEPS * b + n + 1))
                    if h == 0:
                        pe.wait_ge(mg_l, val(8 * b + k + 1))
                    if k == 0 and not (first(b) and h == 0):
                        pe.wait_ge(nl_r, val(4 * b + 2 * h))
                    a = n % 3
                    for c in range(DC):
                        cs = slice(c * P, (c + 1) * P)
                        ins = products(nc, pN[c][:, :], [(msgh[:, k, cs], msgl[:, k, cs], Ahi[:, a], Alo[:, a])],
                                       start=k == 0, stop=k == NT - 1)
                    ins.then_inc(av, 1)

                def operands(g_b, s, g_k):
                    h, k = divmod(g_k, NT // 2)
                    cs, ns = slice(k * P, (k + 1) * P), slice(g_k * P, (g_k + 1) * P)
                    return ([(xhi[:, s, c, ns], xlo[:, s, c, ns]) for c in range(DC)],
                            [(chi[:, h, c, cs], clo[:, h, c, cs]) for c in range(DC)]
                            + [(mhi[:, h, c, cs], mlo[:, h, c, cs]) for c in range(DC)])

                def gate_rz(g_b, s, g_k):
                    h, k = divmod(g_k, NT // 2)
                    xs, xin = operands(g_b, s, g_k)
                    cols = slice(0, 2 * D)
                    if k == 0:
                        pe.wait_ge(cl_r, val(2 * g_b + h + 1))
                    if not (first(g_b) and g_k == 0):
                        pe.wait_ge(rz_r, val(NT * g_b + g_k))
                    parts = ([(a, l, whhh[:, c, cols], whhl[:, c, cols]) for c, (a, l) in enumerate(xs)]
                             + [(a, l, wihh[:, c, cols], wihl[:, c, cols]) for c, (a, l) in enumerate(xin)])
                    products(nc, pRZ[:, :], parts[:2 * DC], stop=False)
                    if k == 0:
                        pe.wait_ge(nl_r, val(4 * g_b + 2 * h + 2))
                    products(nc, pRZ[:, :], parts[2 * DC:], start=False).then_inc(rz_m, 1)

                def gate_n(g_b, s, g_k):
                    xs, xin = operands(g_b, s, g_k)
                    cols = slice(2 * D, 3 * D)
                    if not (first(g_b) and g_k == 0):
                        pe.wait_ge(gn_r, val(NT * g_b + g_k))
                    products(nc, pG[:, 0:D], [(a, l, wihh[:, c, cols], wihl[:, c, cols]) for c, (a, l) in enumerate(xin)])
                    products(nc, pG[:, D:2 * D], [(a, l, whhh[:, c, cols], whhl[:, c, cols])
                                                  for c, (a, l) in enumerate(xs)]).then_inc(gn_m, 1)

                def body(b, s, gates, nxt):
                    for n in range(STEPS):
                        p = n // 2
                        if n + 2 < STEPS:
                            dist(b, n + 2)
                        if has_gates(gates, p):
                            g_b, g_k = gate_tile(b, p)
                            (gate_n if n % 2 else gate_rz)(g_b, s if p >= NT // 2 else 1 - s, g_k)
                        gather(b, n)
                    if nxt:
                        prep(b + 1, 1 - s)

                schedule(prep, body, pe)
                for k in range(4, NT):
                    gate_rz(B - 1, 1, k)
                    gate_n(B - 1, 1, k)


INPUTS = ["x", "adjT", "l0_x", "l0_adj", "l0_gmask", "l0_geye", "l0_member", "l0_fw", "ident", "l0_w1", "l0_b1",
          "l0_w2", "l0_b2", "conv1_w", "conv2_w", "bn", "w_ih", "w_hh", "w_msg", "w_se", "b_se", "selA", "selB",
          "rows", "b_ih", "b_hh", "b_msg"]


def build(nc, t):
    t["fused"] = nc.dram_tensor("fused_scratch", (B, GN, D), F32, kind="Internal").ap()
    t["x1"] = nc.dram_tensor("x1_scratch", (B, P, NT, D), F32, kind="Internal").ap()
    t["x1T"] = nc.dram_tensor("x1T_scratch", (B, P, DC, N), F32, kind="Internal").ap()
    t["h4"] = nc.dram_tensor("h_scratch", (B // 2, P, 2 * DC, 4, HQ), F32, kind="Internal").ap()
    t["xcT"] = nc.dram_tensor("xcT_scratch", (B, P, DC, N), F32, kind="Internal").ap()
    groups_stage(nc, t)
    for co in range(DC):
        conv_stage(nc, t, co)
    nodes_stage(nc, t)


def constants():
    gmask = np.zeros((P, NG, P), np.float32)
    geye = np.zeros((P, NG, P), np.float32)
    member = np.zeros((P, NG), np.float32)
    for g, idx in enumerate(GROUPS):
        for q in range(GB):
            rows = GP * q + np.array(idx)
            gmask[np.ix_(rows, [g], rows)] = 1
            geye[rows, g, rows] = 1
            member[rows, g] = 1
    selA = np.zeros((12, SELW), np.float32)
    selB = np.zeros((12, SELW), np.float32)
    selA[np.arange(12), np.arange(12)] = 1
    selB[0:3, 12:16] = -1
    rows = np.zeros((16, 6), np.float32)
    rows[0:6, 0] = 1
    rows[6:12, 1] = 1
    rows[12:14, 2] = 1
    rows[14, 0] = rows[15, 1] = 1
    rows[[0, 1, 2, 6, 7, 8], 3] = 2
    rows[[3, 4, 5, 9, 10, 11], 4] = 2
    rows[12, 3] = rows[13, 4] = 1
    rows[14:16, 5] = 1
    return {"l0_gmask": gmask, "l0_geye": geye, "l0_member": member, "ident": np.eye(P, dtype=np.float32),
            "selA": selA, "selB": selB, "rows": rows}


def layout(i):
    def parts(w):
        return np.ascontiguousarray(w.reshape(-1, P, w.shape[-1]).transpose(1, 0, 2))

    def rep(v):
        return np.ascontiguousarray(np.broadcast_to(v, (P,) + v.shape))

    x, adj = i["x"], i["adj"]
    l0_x = np.zeros((GT, GB, GP, D), np.float32)
    l0_x[:, :, :GN] = x[:, :GN].reshape(GT, GB, GN, D)
    l0_adj = np.zeros((GT, GB, GP, GB, GP), np.float32)
    for q in range(GB):
        l0_adj[:, q, :GN, q, :GN] = adj[:, :GN, :GN].reshape(GT, GB, GN, GN)[:, q]
    bn = np.stack([np.stack([i[f"L1_gnn_bn{k}_{f}"].reshape(DC, P) for f in "gbmv"]) for k in (1, 2)])
    w_se = np.concatenate([i["L1_gnn_w_se"].T] * 4, axis=1)
    b_se = np.concatenate([i["L1_gnn_b_se"]] * 4)
    return {
        "x": np.ascontiguousarray(x.reshape(B, NT, P, D).transpose(0, 2, 1, 3)),
        "adjT": np.ascontiguousarray(adj.transpose(0, 2, 1).reshape(B, NT, P, N).transpose(0, 2, 1, 3)),
        "l0_x": np.ascontiguousarray(l0_x.reshape(GT, P, D).transpose(1, 0, 2)),
        "l0_adj": np.ascontiguousarray(l0_adj.reshape(GT, P, P).transpose(1, 0, 2)),
        "l0_fw": rep(i["L0_gnn_fusion_w"]),
        "l0_w1": np.ascontiguousarray(i["L0_gnn_W1"].reshape(NG, DC, P, DH).transpose(2, 0, 1, 3)),
        "l0_w2": np.ascontiguousarray(i["L0_gnn_W2"].reshape(NG, HC, P, D).transpose(2, 0, 1, 3)),
        "l0_b1": np.ascontiguousarray(i["L0_gnn_b1"].reshape(NG, HC, P).transpose(2, 0, 1)),
        "l0_b2": rep(i["L0_gnn_b2"]),
        "conv1_w": parts(i["L1_gnn_conv1_w"][:, :, 0].T),
        "conv2_w": np.ascontiguousarray(i["L1_gnn_conv2_w"].transpose(1, 2, 0).reshape(DC, P, TAPS, D).transpose(1, 0, 2, 3)),
        "bn": np.ascontiguousarray(bn.transpose(3, 0, 1, 2)),
        "w_ih": parts(i["L1_gnn_w_ih"].T), "w_hh": parts(i["L1_gnn_w_hh"].T), "w_msg": parts(i["L1_gnn_w_msg"].T),
        "w_se": parts(w_se), "b_se": b_se.reshape(-1, 1),
        "b_ih": rep(i["L1_gnn_b_ih"]), "b_hh": rep(i["L1_gnn_b_hh"]), "b_msg": rep(i["L1_gnn_b_msg"]),
    }


def kernel(**inputs):
    import concourse.bacc as bacc
    from concourse.bass_utils import run_bass_kernel_spmd

    inputs = {k: np.asarray(v) for k, v in inputs.items()}
    arrays = {**layout(inputs), **constants()}
    arrays = {f"in_{k}": np.ascontiguousarray(arrays[k]) for k in INPUTS}
    nc = bacc.Bacc("TRN2", target_bir_lowering=False, num_devices=1)
    t = {k: nc.dram_tensor(f"in_{k}", arrays[f"in_{k}"].shape, F32, kind="ExternalInput").ap() for k in INPUTS}
    t["out"] = nc.dram_tensor("out", (B, P, NT, D), F32, kind="ExternalOutput").ap()
    build(nc, t)
    r = run_bass_kernel_spmd(nc, [arrays], core_ids=[0])
    out = r.results[0]["out"]
    return np.ascontiguousarray(out.transpose(0, 2, 1, 3).reshape(B, N, D))
```

```python
from contextlib import ExitStack

import numpy as np

import concourse.bass as bass
from concourse import mybir

P = 128
B, N, D = 16, 1024, 256
DC = D // P
NT = N // P
H2 = N // 2
DH = 512
HC = DH // P
GROUPS = [list(range(25)), [0, 1, 2, 3, 4, 5, 6, 7, 8], [0, 9, 10, 11, 12, 13, 14],
          [6, 7, 8, 12, 13, 14], [3, 4, 5, 9, 10, 11]]
NG = len(GROUPS)
GN = 25
GP = 32
GB = P // GP
GT = B // GB
TAPS, PAD = 17, 8
PQ = (N + 2 * PAD) // 4
HQ = PQ + 2
EPS = 1e-5
SQ = 32
SK = 2 * SQ

F32 = mybir.dt.float32
F32R = mybir.dt.float32r
ALU = mybir.AluOpType
ACT = mybir.ActivationFunctionType
AX = mybir.AxisListType.X


class Space:

    def __init__(self, nc, ctx, tag):
        self.nc, self.ctx, self.tag = nc, ctx, tag

    def sb(self, name, shape, dt=F32):
        return self.ctx.enter_context(self.nc.sbuf_tensor(f"{self.tag}_{name}", shape, dt))

    def bank(self, name):
        return self.ctx.enter_context(self.nc.psum_tensor(f"{self.tag}_{name}", [P, 512], F32))

    def sem(self, name):
        return self.ctx.enter_context(self.nc.semaphore(f"{self.tag}_{name}"))


def products(nc, out, pairs, start=True, stop=True):
    last = None
    steps = [(a, b) for ah, al, bh, bl in pairs for a, b in ((ah, bh), (ah, bl), (al, bh))]
    for k, (a, b) in enumerate(steps):
        last = nc.tensor.matmul(out, a, b, start=start and k == 0, stop=stop and k == len(steps) - 1)
    return last


class Turn:

    def __init__(self, i, a=1, c=0):
        self.i, self.a, self.c = i, a, c

    def __add__(self, k):
        return Turn(self.i, self.a, self.c + k)

    def __sub__(self, k):
        return self + -k

    def __mul__(self, k):
        return Turn(self.i, self.a * k, self.c * k)

    __radd__, __rmul__ = __add__, __mul__


def val(n):
    return n.i * n.a + n.c if isinstance(n, Turn) else n


def groups_stage(nc, t):
    with ExitStack() as ctx:
        m = Space(nc, ctx, "g")
        x0 = m.sb("x0", [P, GT, D])
        adj0 = m.sb("adj0", [P, GT, P])
        gmask = m.sb("gmask", [P, NG, P])
        geye = m.sb("geye", [P, NG, P])
        member = m.sb("member", [P, NG])
        ident = m.sb("ident", [P, P])
        w1 = m.sb("w1", [P, NG, DC, DH])
        w2 = m.sb("w2", [P, NG, HC, D])
        b1 = m.sb("b1", [P, NG, HC])
        b2 = m.sb("b2", [P, NG, D])
        fw = m.sb("fw", [P, NG])
        A = m.sb("A", [P, NG, GT, P])
        nadjT = m.sb("nadjT", [P, NG, GT, P])
        deg = m.sb("deg", [P, NG * GT])
        deg0 = m.sb("deg0", [P, NG * GT])
        dsafe = m.sb("dsafe", [P, NG * GT])
        dpow = m.sb("dpow", [P, NG * GT])
        dhave = m.sb("dhave", [P, NG * GT])
        dinv = m.sb("dinv", [P, NG * GT])
        half = m.sb("half", [P, NG * GT])
        wmax = m.sb("wmax", [P, 1])
        wexp = m.sb("wexp", [P, NG])
        wsum = m.sb("wsum", [P, 1])
        wrec = m.sb("wrec", [P, 1])
        wsm = m.sb("wsm", [P, NG])
        wmem = m.sb("wmem", [P, NG])
        xaT = m.sb("xaT", [P, DC, 512])
        hT = m.sb("hT", [P, HC, 512])
        sup2 = m.sb("sup2", [P, GT, D])
        pre = m.sb("pre", [P, D])
        act2 = m.sb("act2", [P, D])
        fused = m.sb("fused", [P, GT, D])

        pT = [m.bank(f"pT{k}") for k in range(2)]
        pX = [m.bank(f"pX{k}") for k in range(2)]
        pH = [m.bank(f"pH{k}") for k in range(2)]
        pS = [m.bank(f"pS{k}") for k in range(2)]

        loaded = m.sem("loaded")
        weights_loaded = m.sem("weights_loaded")
        fused_stored = m.sem("fused_stored")
        dve_chain = m.sem("dve_chain")
        half_set = m.sem("half_set")
        powered = m.sem("powered")
        adj_normed_rows = m.sem("adj_normed_rows")
        adj_transposed = m.sem("adj_transposed")
        nadjT_ready = m.sem("nadjT_ready")
        weights_exp = m.sem("weights_exp")
        weights_max = m.sem("weights_max")
        xa_multiplied = m.sem("xa_multiplied")
        xaT_ready = m.sem("xaT_ready")
        h_multiplied = m.sem("h_multiplied")
        hT_ready = m.sem("hT_ready")
        sup2_multiplied = m.sem("sup2_multiplied")
        sup2_ready = m.sem("sup2_ready")
        out_multiplied = m.sem("out_multiplied")
        out_read = m.sem("out_read")
        fused_ready = m.sem("fused_ready")

        def runs(g):
            if g == 0:
                return [(0, GP, 0)]
            out = []
            for at, node in enumerate(GROUPS[g]):
                if out and node == out[-1][1]:
                    out[-1] = (out[-1][0], node + 1, out[-1][2])
                else:
                    out.append((node, node + 1, at))
            return out

        def width(g):
            return len(GROUPS[g]) if g else GP

        def padded(x):
            return x[:, :].rearrange("p (b i) -> p b i", i=GP)

        def kept(x, g):
            return x[:, 0:B * width(g)].rearrange("p (b i) -> p b i", i=width(g))

        with nc.Block() as block:
            @block.sync
            def _(sp):
                for dst, src in ((adj0, t["l0_adj"]), (gmask, t["l0_gmask"]), (geye, t["l0_geye"]),
                                 (member, t["l0_member"]), (fw, t["l0_fw"]), (ident, t["ident"])):
                    sp.dma_start(dst[:], src).then_inc(loaded, 16)
                for dst, src in ((x0, t["l0_x"]), (w1, t["l0_w1"]), (b1, t["l0_b1"]), (w2, t["l0_w2"]), (b2, t["l0_b2"])):
                    sp.dma_start(dst[:], src).then_inc(weights_loaded, 16)
                for b in range(B):
                    k, q = divmod(b, GB)
                    sp.wait_ge(fused_ready, k + 1)
                    sp.dma_start(t["fused"][val(b)], fused[GP * q:GP * q + GN, k, :]).then_inc(fused_stored, 16)
                sp.wait_ge(fused_stored, 16 * B)

            @block.gpsimd
            def _(pool):
                nc.gpsimd.memset(half[:, :], -0.5).then_inc(half_set, 1)
                pool.wait_ge(half_set, 1)
                pool.wait_ge(dve_chain, 4)
                nc.gpsimd.tensor_tensor(dpow[:, :], dsafe[:, :], half[:, :], ALU.pow).then_inc(powered, 1)

            @block.scalar
            def _(act):
                act.wait_ge(weights_max, 1)
                nc.scalar.activation(wexp[:, :], fw[:, :], ACT.Exp, bias=wmax[:, :],
                                     accum_out=wsum[:, :]).then_inc(weights_exp, 1)
                for g in range(NG):
                    for c in range(DC):
                        act.wait_ge(xa_multiplied, val(g * DC + c + 1))
                        if g:
                            act.wait_ge(h_multiplied, val(HC * g))
                        for start, stop, at in runs(g):
                            ins = nc.scalar.copy(kept(xaT[:, c], g)[:, :, at:at + stop - start],
                                                 padded(pX[c])[:, :, start:stop])
                        ins.then_inc(xaT_ready, 1)
                    act.wait_ge(weights_loaded, 80)
                    for e in range(HC):
                        act.wait_ge(h_multiplied, val(g * HC + e + 1))
                        if g:
                            act.wait_ge(sup2_multiplied, val(GT * g))
                        for start, stop, at in runs(g):
                            ins = nc.scalar.activation(padded(hT[:, e])[:, :, start:stop],
                                                       kept(pH[e % 2], g)[:, :, at:at + stop - start],
                                                       ACT.Relu, bias=b1[:, g, e:e + 1])
                        ins.then_inc(hT_ready, 1)
                    for k in range(GT):
                        act.wait_ge(sup2_multiplied, val(g * GT + k + 1))
                        if g:
                            act.wait_ge(out_multiplied, val(GT * (g - 1) + k + 1))
                        nc.scalar.copy(sup2[:, k, :], pS[k % 2][:, 0:D]).then_inc(sup2_ready, 1)

            @block.vector
            def _(v):
                n = [0]

                def link(ins):
                    n[0] += 1
                    ins.then_inc(dve_chain, 1)
                    v.wait_ge(dve_chain, val(n[0]))

                v.wait_ge(loaded, 16 * 6)
                for g in range(NG):
                    Ag = A[:, g, :, :]
                    ins = nc.vector.tensor_tensor(Ag, adj0[:, :, :], gmask[:, g, :].unsqueeze(1).to_broadcast([P, GT, P]), ALU.mult)
                link(ins)
                for g in range(NG):
                    Ag = A[:, g, :, :]
                    ins = nc.vector.tensor_tensor(Ag, Ag, geye[:, g, :].unsqueeze(1).to_broadcast([P, GT, P]), ALU.add)
                link(ins)
                link(nc.vector.tensor_reduce(deg[:, :], A[:].rearrange("p g t n -> p (g t) n"), axis=AX, op=ALU.add))
                nc.vector.tensor_scalar(deg0[:, :], deg[:, :], 0.0, None, ALU.is_equal).then_inc(half_set, 1)
                v.wait_ge(half_set, 2)
                link(nc.vector.tensor_tensor(dsafe[:, :], deg[:, :], deg0[:, :], ALU.add))
                link(nc.vector.tensor_scalar(dhave[:, :], deg0[:, :], -1.0, 1.0, ALU.mult, ALU.add))
                v.wait_ge(powered, 1)
                link(nc.vector.tensor_tensor(dinv[:, :], dpow[:, :], dhave[:, :], ALU.mult))
                for g in range(NG):
                    for k in range(GT):
                        j = g * GT + k
                        nc.vector.tensor_scalar(A[:, g, k, :], A[:, g, k, :], dinv[:, j:j + 1], None, ALU.mult).then_inc(adj_normed_rows, 1)
                link(nc.vector.tensor_reduce(wrec[:, :], fw[:, :], axis=AX, op=ALU.max))
                nc.vector.tensor_scalar(wmax[:, :], wrec[:, :], -1.0, None, ALU.mult).then_inc(weights_max, 1)
                v.wait_ge(weights_max, 1)
                for j in range(NG * GT):
                    g, k = divmod(j, GT)
                    v.wait_ge(adj_transposed, val(j + 1))
                    nc.vector.tensor_scalar(nadjT[:, g, k, :], pT[j % 2][:, 0:P], dinv[:, j:j + 1], None, ALU.mult).then_inc(nadjT_ready, 1)
                v.wait_ge(weights_exp, 1)
                link(nc.vector.reciprocal(wrec[:, :], wsum[:, :]))
                link(nc.vector.tensor_scalar(wsm[:, :], wexp[:, :], wrec[:, :], None, ALU.mult))
                link(nc.vector.tensor_tensor(wmem[:, :], wsm[:, :], member[:, :], ALU.mult))
                v.wait_ge(weights_loaded, 80)
                for g in range(NG):
                    for k in range(GT):
                        v.wait_ge(out_multiplied, val(g * GT + k + 1))
                        ins = nc.vector.tensor_tensor(pre[:, :], pT[k % 2][:, 0:D], b2[:, g, :], ALU.add)
                        ins.then_inc(out_read, 1)
                        v.wait_ge(out_read, val(g * GT + k + 1))
                        link(nc.vector.tensor_scalar(act2[:, :], pre[:, :], 0.0, wmem[:, g:g + 1], ALU.max, ALU.mult))
                        if g == 0:
                            ins = nc.vector.tensor_copy(fused[:, k, :], act2[:, :])
                        else:
                            ins = nc.vector.tensor_tensor(fused[:, k, :], fused[:, k, :], act2[:, :], ALU.add)
                        if g == NG - 1:
                            ins.then_inc(fused_ready, 1)
                            v.wait_ge(fused_ready, k + 1)
                        else:
                            link(ins)

            @block.tensor
            def _(pe):
                pe.wait_ge(loaded, 16 * 6)
                for j in range(NG * GT):
                    g, k = divmod(j, GT)
                    pe.wait_ge(adj_normed_rows, val(j + 1))
                    if j >= 2:
                        pe.wait_ge(nadjT_ready, val(j - 1))
                    nc.tensor.transpose(pT[j % 2][:, 0:P], A[:, g, k, :], ident[:, :]).then_inc(adj_transposed, 1)
                pe.wait_ge(nadjT_ready, NG * GT)
                pe.wait_ge(weights_loaded, 80)
                for g in range(NG):
                    for c in range(DC):
                        if g:
                            pe.wait_ge(xaT_ready, val((g - 1) * DC + c + 1))
                        for k in range(GT):
                            ins = nc.tensor.matmul(pX[c][:, k * P:(k + 1) * P], x0[:, k, c * P:(c + 1) * P],
                                                   nadjT[:, g, k, :], start=True, stop=True)
                        ins.then_inc(xa_multiplied, 1)
                    pe.wait_ge(xaT_ready, val((g + 1) * DC))
                    for e in range(HC):
                        if g * HC + e >= 2:
                            pe.wait_ge(hT_ready, val(g * HC + e - 1))
                        for c in range(DC):
                            ins = nc.tensor.matmul(pH[e % 2][:, 0:B * width(g)], w1[:, g, c, e * P:(e + 1) * P],
                                                   xaT[:, c, 0:B * width(g)], start=c == 0, stop=c == DC - 1)
                        ins.then_inc(h_multiplied, 1)
                    pe.wait_ge(hT_ready, val((g + 1) * HC))
                    for k in range(GT):
                        if g * GT + k >= 2:
                            pe.wait_ge(sup2_ready, val(g * GT + k - 1))
                        for e in range(HC):
                            ins = nc.tensor.matmul(pS[k % 2][:, 0:D], hT[:, e, k * P:(k + 1) * P], w2[:, g, e, :],
                                                   start=e == 0, stop=e == HC - 1)
                        ins.then_inc(sup2_multiplied, 1)
                    for k in range(GT):
                        pe.wait_ge(sup2_ready, val(g * GT + k + 1))
                        if g * GT + k >= 2:
                            pe.wait_ge(out_read, val(g * GT + k - 1))
                        nc.tensor.matmul(pT[k % 2][:, 0:D], nadjT[:, g, k, :], sup2[:, k, :],
                                         start=True, stop=True).then_inc(out_multiplied, 1)


def conv_stage(nc, t, co):
    with ExitStack() as ctx:
        m = Space(nc, ctx, f"c{co}")
        prepares = co == 0
        PAIRS = B // 2
        whi = m.sb("whi", [P, DC, 3, 4, 3, P], F32R)
        wlo = m.sb("wlo", [P, DC, 3, 4, 3, P], F32R)
        h4 = m.sb("h4", [P, 2, 2 * DC, 4, HQ])
        bn = m.sb("bn", [P, 2, 4, DC])
        bnp = m.sb("bnp", [P, 2, DC])
        scale = m.sb("scale", [P, 2, DC])
        shift = m.sb("shift", [P, 2, DC])
        half = m.sb("half", [P, NT])
        M0 = m.sb("M0", [P, 2, H2])
        Y0 = m.sb("Y0", [P, 2, H2])
        y = m.sb("y", [P, 2, N])
        with ExitStack() as staging:
            ms = Space(nc, staging, f"c{co}")
            kept = ms if prepares else m
            raw = kept.sb("raw", [P, DC, 18, P])
            tap = kept.sb("tap", [P, 2, DC, 3, P])
            pairs = ms.sb("pairs", [P, DC, 9, P])
            if prepares:
                w1stage = ms.sb("w1stage", [P, DC, D])
        Pt = m.sb("Pt", [P, 2 * DC, 2, PQ])
        Dt = m.sb("Dt", [P, 2, 2 * DC, 2, PQ])
        Dhi = m.sb("Dhi", [P, 2, 2 * DC, 2, PQ], F32R)
        Dlo = m.sb("Dlo", [P, 2, 2 * DC, 2, PQ], F32R)
        if prepares:
            ident = m.sb("ident", [P, P])
            w1hi = m.sb("w1hi", [P, DC, D], F32R)
            w1lo = m.sb("w1lo", [P, DC, D], F32R)
            xin = m.sb("xin", [P, NT, D])
            fus = m.sb("fus", [GN, D])
            stats = m.sb("stats", [P, NT, 6])
            mv = m.sb("mv", [P, NT, 2])
            mark = m.sb("mark", [P, 1])
            veps = m.sb("veps", [P, NT])
            rstd = m.sb("rstd", [P, NT])
            negmean = m.sb("negmean", [P, NT])
            offset = m.sb("offset", [P, NT])
            xT = m.sb("xT", [P, DC, H2])
            xhi = m.sb("xhi", [P, DC, H2], F32R)
            xlo = m.sb("xlo", [P, DC, H2], F32R)

        pY = [m.bank(f"pY{k}") for k in range(4)]
        pT = [m.bank(f"pT{k}") for k in range(2)]
        pH = [m.bank(f"pH{k}") for k in range(2)]

        bn_loaded = m.sem("bn_loaded")
        taps_loaded = m.sem("taps_loaded")
        pairs_summed = m.sem("pairs_summed")
        tap_sums = m.sem("tap_sums")
        taps_ready = m.sem("taps_ready")
        tap_hi_ready = m.sem("tap_hi_ready")
        tap_lo_ready = m.sem("tap_lo_ready")
        dve_setup_chain = m.sem("dve_setup_chain")
        bn_powered = m.sem("bn_powered")
        half_set = m.sem("half_set")
        pads_zeroed = m.sem("pads_zeroed")
        y_loaded = m.sem("y_loaded")
        y_stored = m.sem("y_stored")
        P_ready = m.sem("P_ready")
        D_ready = m.sem("D_ready")
        D_hi_ready = m.sem("D_hi_ready")
        D_lo_ready = m.sem("D_lo_ready")
        conv2_chunk0_multiplied = m.sem("conv2_chunk0_multiplied")
        conv2_multiplied = m.sem("conv2_multiplied")
        M_first_ready = m.sem("M_first_ready")
        sums_ready = m.sem("sums_ready")
        y_added = m.sem("y_added")
        y_ready = m.sem("y_ready")

        if prepares:
            constants_loaded = m.sem("constants_loaded")
            conv1_weights_split = m.sem("conv1_weights_split")
            x_loaded = m.sem("x_loaded")
            x1_stored = m.sem("x1_stored")
            x1T_stored = m.sem("x1T_stored")
            h_stored = [m.sem(f"h_stored{k}") for k in range(2)]
            fused_added = m.sem("fused_added")
            bn_stats_done = m.sem("bn_stats_done")
            mean_var_done = m.sem("mean_var_done")
            var_eps_done = m.sem("var_eps_done")
            rstd_done = m.sem("rstd_done")
            x1_ready = m.sem("x1_ready")
            x1_transposed = m.sem("x1_transposed")
            x1T_ready = m.sem("x1T_ready")
            x1T_hi_ready = m.sem("x1T_hi_ready")
            x1T_lo_ready = m.sem("x1T_lo_ready")
            conv1_multiplied = m.sem("conv1_multiplied")
            h_ready = m.sem("h_ready")
        else:
            h_loaded = [m.sem(f"h_loaded{k}") for k in range(2)]

        first = lambda j: isinstance(j, int) and j == 0

        PS = (1, 0, 2)
        SUMS = [(c, j, 3 * a + max(0, k - 1), k) for a, c in enumerate(PS) for k, j in enumerate((0, 3, 1, 2))]
        NS, ND = len(SUMS), 9
        ADDS = {0: (0,), 3: (1,), 1: (0, 1), 2: (0, 1)}
        OPS = [(n, odd) for n, sm in enumerate(SUMS) if n > 1 for odd in ADDS[sm[1]]]
        SOPS = len(OPS)
        SUM_END = [sum(o[0] <= n for o in OPS) for n in range(NS)]
        START = {j: [(0, 0), (1, 1), (0, 3)] for j in (0, 1, 2)} | {3: [(1, 0), (0, 2), (1, 3)]}
        LAST_USE = [max(n for n, sm in enumerate(SUMS) if sm[2] == k) for k in range(ND)]
        DW = PQ - 1

        def schedule(body, eng):
            body(0, 0, True)
            with eng.Fori(0, PAIRS // 2 - 1) as turn:
                i = Turn(turn)
                for k in range(2):
                    body(2 * i + k + 1, 1 - k, True)
            body(PAIRS - 1, 1, False)

        def units(u):
            return [(e, e // 2, e % 2, 4 * u + e) for e in range(4)]

        def multiplied(u, k):
            return NS * (u if k >= 0 else u - 1) + LAST_USE[k % ND] + 1

        with nc.Block() as block:
            @block.sync
            def _(sp):
                def load_x(j):
                    if not first(j):
                        sp.wait_ge(x1_stored, val(16 * j))
                        sp.wait_ge(x1_transposed, val(4 * j))
                    sp.dma_start(xin[:, :, :], t["x"][val(j)]).then_inc(x_loaded, 16)
                    sp.dma_start(fus[:, :], t["fused"][val(j)]).then_inc(x_loaded, 16)

                def store_x1(j):
                    sp.wait_ge(x1_ready, val(NT * j + NT))
                    sp.dma_start(t["x1"][val(j)], xin[:, :, :]).then_inc(x1_stored, 16)

                def store_x1T(j, nh):
                    sp.wait_ge(x1T_ready, val(2 * (2 * j + nh) + 2))
                    sp.dma_start(t["x1T"][val(j)][:, :, nh * H2:(nh + 1) * H2], xT[:]).then_inc(x1T_stored, 16)

                def store_h(u, s):
                    sp.wait_ge(h_ready, val(8 * u + 8))
                    sp.dma_start(t["h4"][val(u)], h4[:, s]).then_inc(h_stored[s], 16)

                def load_h(u, s):
                    if not (isinstance(u, int) and u < 2):
                        sp.wait_ge(D_ready, val(ND * u - ND))
                    sp.dma_start(h4[:, s], t["h4"][val(u)]).then_inc(h_loaded[s], 16)

                def x1T_in_dram(u, nxt):
                    if prepares:
                        sp.wait_ge(x1T_stored, val(64 * u + 64 + 32 * nxt))

                def store_y(u, q):
                    sp.dma_start(t["xcT"][val(2 * u + q)][:, co, :], y[:, q, :]).then_inc(y_stored, 16)

                def turn_y(u, nxt):
                    if first(u):
                        x1T_in_dram(u, nxt)
                    else:
                        sp.wait_ge(y_ready, val(u))
                        store_y(u - 1, 0)
                        x1T_in_dram(u, nxt)
                        store_y(u - 1, 1)
                        sp.wait_ge(y_stored, val(32 * u))
                    for q in range(2):
                        sp.dma_start(y[:, q, :], t["x1T"][val(2 * u + q)][:, co, :]).then_inc(y_loaded, 16)

                def body(u, s, nxt):
                    if not (nxt and prepares):
                        if prepares:
                            store_h(u, s)
                        elif nxt:
                            load_h(u + 1, 1 - s)
                        turn_y(u, nxt)
                        return
                    j = 2 * (u + 1)
                    load_x(j)
                    store_h(u, s)
                    store_x1(j)
                    store_x1T(j, 0)
                    store_x1T(j, 1)
                    load_x(j + 1)
                    turn_y(u, nxt)
                    store_x1(j + 1)
                    store_x1T(j + 1, 0)
                    store_x1T(j + 1, 1)

                def load_taps():
                    for i in range(DC):
                        sp.dma_start(raw[:, i, 0:TAPS, :], t["conv2_w"][:, i, :, co * P:(co + 1) * P]).then_inc(taps_loaded, 16)

                if prepares:
                    load_x(0)
                    sp.dma_start(bn[:], t["bn"]).then_inc(bn_loaded, 16)
                    sp.dma_start(ident[:], t["ident"]).then_inc(constants_loaded, 16)
                    sp.dma_start(w1stage[:], t["conv1_w"]).then_inc(constants_loaded, 16)
                    load_taps()
                    for j in range(2):
                        store_x1(j)
                        store_x1T(j, 0)
                        if j == 0:
                            load_x(1)
                        store_x1T(j, 1)
                else:
                    load_taps()
                    sp.dma_start(bn[:], t["bn"]).then_inc(bn_loaded, 16)
                    load_h(0, 0)
                schedule(body, sp)
                sp.wait_ge(y_ready, PAIRS)
                for q in range(2):
                    store_y(PAIRS - 1, q)
                sp.wait_ge(y_stored, 32 * PAIRS)
                if prepares:
                    sp.wait_ge(x1_stored, 16 * B)
                    sp.wait_ge(x1T_stored, 32 * B)
                    for s in range(2):
                        sp.wait_ge(h_stored[s], 8 * PAIRS)

            @block.gpsimd
            def _(pool):
                nc.gpsimd.memset(half[:, :], -0.5).then_inc(half_set, 1)
                nc.gpsimd.memset(raw[:, :, TAPS, :], 0.0).then_inc(pads_zeroed, 1)
                if prepares:
                    for s in range(2):
                        nc.gpsimd.memset(h4[:, s, :, :, 0:PAD // 4], 0.0).then_inc(pads_zeroed, 1)
                        nc.gpsimd.memset(h4[:, s, :, :, (PAD + N) // 4:HQ], 0.0).then_inc(pads_zeroed, 1)
                pool.wait_ge(half_set, 1)

                def rstd_of(j):
                    pool.wait_ge(var_eps_done, val(2 * j + 2))
                    nc.gpsimd.tensor_tensor(rstd[:, :], veps[:, :], half[:, :], ALU.pow).then_inc(rstd_done, 1)
                    pool.wait_ge(rstd_done, val(2 * j + 1))
                    nc.gpsimd.tensor_tensor(offset[:, :], negmean[:, :], rstd[:, :], ALU.mult).then_inc(rstd_done, 1)

                def low_d(u, s, k):
                    a = (s + k) % 2
                    for i in range(DC):
                        pool.wait_ge(D_hi_ready, val(DC * (ND * u + k) + i + 1))
                        ch = slice(2 * i, 2 * i + 2)
                        nc.gpsimd.tensor_tensor(Dlo[:, a, ch, :, 0:DW], Dt[:, a, ch, :, 0:DW],
                                                Dhi[:, a, ch, :, 0:DW].bitcast(F32), ALU.subtract).then_inc(D_lo_ready, 1)

                def body(u, s, nxt):
                    for k in range(ND):
                        if nxt and prepares and k in (0, 5):
                            rstd_of(2 * (u + 1) + k // 5)
                        low_d(u, s, k)

                if prepares:
                    rstd_of(0)
                pool.wait_ge(dve_setup_chain, 1)
                nc.gpsimd.tensor_tensor(bnp[:].rearrange("p a c -> p (a c)"), scale[:].rearrange("p a c -> p (a c)"),
                                        half[:, 0:2 * DC], ALU.pow).then_inc(bn_powered, 1)
                if prepares:
                    rstd_of(1)
                schedule(body, pool)

            @block.scalar
            def _(act):
                def taps_high(a):
                    for k, w in enumerate(taps_of(raw, pairs, tap, PS[a])):
                        if a == 0 and k == 0:
                            act.wait_ge(pairs_summed, 1)
                        if k == 2:
                            act.wait_ge(taps_ready, a + 1)
                        nc.scalar.copy(whi[:, :, PS[a], SUMS[k][1]], w).then_inc(tap_hi_ready, 1)

                def scale_x(j):
                    act.wait_ge(rstd_done, val(2 * j + 2))
                    for k in range(NT):
                        nc.scalar.activation(xin[:, k, :], xin[:, k, :], ACT.Identity, scale=rstd[:, k:k + 1],
                                             bias=offset[:, k:k + 1]).then_inc(x1_ready, 1)

                def parts_x(u, e, q, nh, n):
                    for ci in range(DC):
                        act.wait_ge(x1_transposed, val(2 * n + ci + 1))
                        if ci == 0 and not first(n):
                            act.wait_ge(x1T_stored, val(16 * n))
                            act.wait_ge(x1T_lo_ready, val(n))
                            act.wait_ge(conv1_multiplied, val(2 * n))
                        nc.scalar.copy(xT[:, ci, :], pT[ci][:, :]).then_inc(x1T_ready, 1)
                        nc.scalar.copy(xhi[:, ci, :], pT[ci][:, :]).then_inc(x1T_hi_ready, 1)

                def relu_h(u, s, e, q, nh, n):
                    for c in range(DC):
                        act.wait_ge(conv1_multiplied, val(2 * n + c + 1))
                        if e == 0 and c == 0 and not (isinstance(u, int) and u < 2):
                            act.wait_ge(D_ready, val(ND * u - ND))
                            act.wait_ge(h_stored[s], val(8 * u - 8 * s))
                        at = PAD // 4 + nh * (H2 // 4)
                        nc.scalar.activation(h4[:, s, 2 * c + q, :, at:at + H2 // 4],
                                             pH[c][:, :].rearrange("p (w r) -> p r w", r=4), ACT.Relu,
                                             scale=scale[:, 0, c:c + 1], bias=shift[:, 0, c:c + 1]).then_inc(h_ready, 1)

                def high_d(u, s, k):
                    a = (s + k) % 2
                    act.wait_ge(D_ready, val(ND * u + k + 1))
                    for i in range(DC):
                        if not (first(u) and k < 2):
                            act.wait_ge(conv2_chunk0_multiplied if i == 0 else conv2_multiplied, val(multiplied(u, k - 2)))
                        ch = slice(2 * i, 2 * i + 2)
                        nc.scalar.copy(Dhi[:, a, ch, :, 0:DW], Dt[:, a, ch, :, 0:DW]).then_inc(D_hi_ready, 1)

                def first_sums(u):
                    for k in range(2):
                        act.wait_ge(conv2_multiplied, val(NS * u + k + 1))
                        if not first(u) and k == 0:
                            act.wait_ge(y_added, val(4 * u))
                        nc.scalar.activation(M0[:, k, :], pY[k][:, :], ACT.Copy, scale=1.0 - 2 * k).then_inc(M_first_ready, 1)

                def finish(u):
                    act.wait_ge(y_added, val(4 * u + 4))
                    nc.scalar.activation(y[:], y[:], ACT.Relu, bias=shift[:, 1, co:co + 1]).then_inc(y_ready, 1)

                def body(u, s, nxt):
                    unit = lambda e: units(u + 1)[e]
                    more = nxt and prepares
                    for k in range(ND):
                        high_d(u, s, k)
                        if k < 2 and first(u) and not prepares:
                            taps_high(k + 1)
                        if k == 1 and more:
                            scale_x(2 * (u + 1))
                        if k == 2:
                            first_sums(u)
                            if more:
                                parts_x(u + 1, *unit(0))
                        if k == 3 and more:
                            relu_h(u + 1, 1 - s, *unit(0))
                            parts_x(u + 1, *unit(1))
                        if k == 4:
                            if not first(u):
                                finish(u - 1)
                            if more:
                                relu_h(u + 1, 1 - s, *unit(1))
                        if k == 5 and more:
                            scale_x(2 * (u + 1) + 1)
                        if k == 6 and more:
                            parts_x(u + 1, *unit(2))
                        if k == 7 and more:
                            relu_h(u + 1, 1 - s, *unit(2))
                            parts_x(u + 1, *unit(3))
                            relu_h(u + 1, 1 - s, *unit(3))

                if prepares:
                    scale_x(0)
                    act.wait_ge(constants_loaded, 32)
                    nc.scalar.copy(w1hi[:], w1stage[:]).then_inc(conv1_weights_split, 1)
                    act.wait_ge(dve_setup_chain, 4)
                    for e, q, nh, n in units(0):
                        if e:
                            taps_high(e - 1)
                        parts_x(0, e, q, nh, n)
                        relu_h(0, 0, e, q, nh, n)
                        if e == 1:
                            scale_x(1)
                else:
                    taps_high(0)
                    act.wait_ge(dve_setup_chain, 4)
                schedule(body, act)
                finish(PAIRS - 1)

            @block.vector
            def _(v):
                def bn_coefficients():
                    v.wait_ge(bn_loaded, 16)
                    nc.vector.tensor_scalar(scale[:, :, :], bn[:, :, 3, :], EPS, None, ALU.add).then_inc(dve_setup_chain, 1)
                    v.wait_ge(bn_powered, 1)
                    nc.vector.tensor_tensor(scale[:, :, :], bn[:, :, 0, :], bnp[:, :, :], ALU.mult).then_inc(dve_setup_chain, 1)
                    v.wait_ge(dve_setup_chain, 2)
                    nc.vector.tensor_tensor(shift[:, :, :], bn[:, :, 2, :], scale[:, :, :], ALU.mult).then_inc(dve_setup_chain, 1)
                    v.wait_ge(dve_setup_chain, 3)
                    nc.vector.tensor_tensor(shift[:, :, :], bn[:, :, 1, :], shift[:, :, :], ALU.subtract).then_inc(dve_setup_chain, 1)

                def norm(j):
                    v.wait_ge(x_loaded, val(32 * j + 32))
                    nc.vector.tensor_tensor(xin[0:GN, 0, :], xin[0:GN, 0, :], fus[:, :], ALU.add).then_inc(fused_added, 1)
                    v.wait_ge(fused_added, val(j + 1))
                    for k in range(NT):
                        nc.vector.bn_stats(stats[:, k, :], xin[:, k, :]).then_inc(bn_stats_done, 1)
                    v.wait_ge(bn_stats_done, val(NT * j + NT))
                    nc.vector.memset(mark[:, :], 0.0)
                    for k in range(NT):
                        nc.vector.bn_aggr(mv[:, k, :], stats[:, k, :]).then_inc(mean_var_done, 1)
                    v.wait_ge(mean_var_done, val(NT * j + NT))
                    nc.vector.tensor_scalar(veps[:, :], mv[:, :, 1], EPS, None, ALU.add).then_inc(var_eps_done, 1)
                    nc.vector.tensor_scalar(negmean[:, :], mv[:, :, 0], -1.0, None, ALU.mult).then_inc(var_eps_done, 1)

                def low_x(n):
                    v.wait_ge(x1T_hi_ready, val(2 * n + 2))
                    if not first(n):
                        v.wait_ge(conv1_multiplied, val(2 * n))
                    nc.vector.tensor_tensor(xlo[:], xT[:], xhi[:].bitcast(F32), ALU.subtract).then_inc(x1T_lo_ready, 1)

                def pair_taps():
                    v.wait_ge(taps_loaded, 16 * DC)
                    v.wait_ge(pads_zeroed, 1)
                    nc.vector.tensor_tensor(pairs[:], raw[:, :, 0:18:2, :], raw[:, :, 1:18:2, :], ALU.add).then_inc(pairs_summed, 1)
                    v.wait_ge(pairs_summed, 1)

                def taps_low(a):
                    g = blocks_of(raw, pairs, PS[a])
                    if a:
                        v.wait_ge(tap_lo_ready, 4 * a)
                    nc.vector.tensor_tensor(tap[:, 0], g[:, :, :, 0], g[:, :, :, 2], ALU.add).then_inc(tap_sums, 1)
                    outer, total = [tap[:, j].rearrange("p c l n -> p (c l) n") for j in range(2)]
                    middle = pairs[:].rearrange("p c k n -> p (c k) n")[:, 1::3, :] if PS[a] == 1 else \
                        raw[:].rearrange("p c k n -> p (c k) n")[:, PS[a] // 2 + 2::6, :]
                    nc.vector.tensor_scalar(middle, middle, 0.5, None, ALU.mult).then_inc(tap_sums, 1)
                    v.wait_ge(tap_sums, 3 * a + 2)
                    nc.vector.scalar_tensor_tensor(total, outer, 0.5, middle, ALU.mult, ALU.add).then_inc(tap_sums, 1)
                    v.wait_ge(tap_sums, 3 * a + 3)
                    nc.vector.scalar_tensor_tensor(outer, outer, 0.5, middle, ALU.mult, ALU.subtract).then_inc(taps_ready, 1)
                    v.wait_ge(taps_ready, a + 1)
                    for k, w in enumerate(taps_of(raw, pairs, tap, PS[a])):
                        v.wait_ge(tap_hi_ready, 4 * a + k + 1)
                        nc.vector.tensor_tensor(wlo[:, :, PS[a], SUMS[k][1]], w, whi[:, :, PS[a], SUMS[k][1]].bitcast(F32),
                                                ALU.subtract).then_inc(tap_lo_ready, 1)

                def stream(u, s, k):
                    c, j, a = PS[k // 3], k % 3, (s + k) % 2
                    X, to = h4[:, s], Dt[:, a]
                    if k == 0:
                        if prepares:
                            v.wait_ge(h_ready, val(8 * u + 8))
                            if first(u):
                                v.wait_ge(pads_zeroed, 5)
                        else:
                            v.wait_ge(h_loaded[s], val(8 * u - 8 * s + 16))
                    if j == 0 and c == 0:
                        nc.vector.tensor_tensor(Pt[:, :, :, :], X[:, :, 0::2, 0:PQ], X[:, :, 1::2, 0:PQ], ALU.subtract).then_inc(P_ready, 1)
                        v.wait_ge(P_ready, val(3 * u + 1))
                    if j == 0 and c == 2:
                        v.wait_ge(D_ready, val(ND * u + 6))
                        nc.vector.tensor_tensor(Pt[:, :, 0, :], X[:, :, 2, 0:PQ], X[:, :, 1, 0:PQ], ALU.subtract).then_inc(P_ready, 1)
                        nc.vector.tensor_tensor(Pt[:, :, 1, :], X[:, :, 0, 1:PQ + 1], X[:, :, 3, 0:PQ], ALU.subtract).then_inc(P_ready, 1)
                        v.wait_ge(P_ready, val(3 * u + 3))
                    S = X[:, :, 1::2, :] if c == 1 else Pt[:, :, :, :]
                    lo, hi = slice(0, DW), slice(1, DW + 1)
                    if not (first(u) and k < 2):
                        v.wait_ge(D_lo_ready, val(DC * (ND * u + k - 1)))
                    if j == 0:
                        nc.vector.tensor_tensor(to[:, :, :, lo], S[:, :, :, lo], S[:, :, :, hi], ALU.subtract).then_inc(D_ready, 1)
                    elif j == 1:
                        nc.vector.tensor_tensor(to[:, :, 0, lo], S[:, :, 1, lo], S[:, :, 0, hi], ALU.add)
                        nc.vector.tensor_tensor(to[:, :, 1, lo], S[:, :, 0, hi], S[:, :, 1, hi], ALU.add).then_inc(D_ready, 1)
                    else:
                        nc.vector.tensor_tensor(to[:, :, 0, lo], S[:, :, 0, hi], S[:, :, 1, lo], ALU.subtract)
                        nc.vector.tensor_tensor(to[:, :, 1, lo], S[:, :, 1, hi], S[:, :, 0, hi], ALU.subtract).then_inc(D_ready, 1)

                def sums(u, n):
                    c, j, _k, _o = SUMS[n]
                    if n == 2:
                        v.wait_ge(M_first_ready, val(2 * u + 2))
                    v.wait_ge(conv2_multiplied, val(NS * u + n + 1))
                    to = Y0 if c == 0 else M0
                    for odd in ADDS[j]:
                        op = ALU.subtract if (j == 3 or (j == 2 and odd)) else ALU.add
                        so_far = M0 if c == 0 and j in (0, 3) else to
                        v.wait_ge(sums_ready, val(SOPS * u + OPS.index((n, odd))))
                        nc.vector.tensor_tensor(to[:, odd, :], so_far[:, odd, :], pY[n % 4][:, :], op).then_inc(sums_ready, 1)

                def add_up(u):
                    v.wait_ge(y_loaded, val(32 * u + 32))
                    v.wait_ge(sums_ready, val(SOPS * u + SOPS))
                    for p, src in enumerate((Y0, M0)):
                        for odd in range(2):
                            view = y[:].rearrange("p b (w r) -> p b w r", r=4)[:, :, :, 2 * odd + p]
                            nc.vector.scalar_tensor_tensor(view, src[:, odd, :].rearrange("p (b w) -> p b w", b=2),
                                                           scale[:, 1, co:co + 1], view, ALU.mult, ALU.add).then_inc(y_added, 1)

                def body(u, s, nxt):
                    more = nxt and prepares
                    if more:
                        norm(2 * (u + 1))
                    for k in range(ND):
                        stream(u, s, k)
                        if k < 2 and first(u) and not prepares:
                            taps_low(k + 1)
                        if not first(u):
                            for n in {0: (8,), 1: (9, 10), 2: (11,)}.get(k, ()):
                                sums(u - 1, n)
                            if k == 2:
                                add_up(u - 1)
                        if k == 3 and more:
                            low_x(4 * (u + 1))
                        if k == 7 and more:
                            low_x(4 * (u + 1) + 2)
                        for n in {4: (2,), 5: (3,), 6: (4,), 7: (5, 6), 8: (7,)}.get(k, ()):
                            sums(u, n)
                        if k == 5 and more:
                            low_x(4 * (u + 1) + 1)
                            norm(2 * (u + 1) + 1)
                        if k == 8 and more:
                            low_x(4 * (u + 1) + 3)

                if prepares:
                    norm(0)
                    bn_coefficients()
                    v.wait_ge(conv1_weights_split, 1)
                    nc.vector.tensor_tensor(w1lo[:], w1stage[:], w1hi[:].bitcast(F32), ALU.subtract).then_inc(conv1_weights_split, 1)
                    pair_taps()
                    for e in range(4):
                        if e:
                            taps_low(e - 1)
                        low_x(e)
                        if e == 1:
                            norm(1)
                    v.wait_ge(tap_lo_ready, 12)
                    v.wait_ge(conv1_weights_split, 2)
                else:
                    pair_taps()
                    taps_low(0)
                    bn_coefficients()
                schedule(body, v)
                for n in range(8, NS):
                    sums(PAIRS - 1, n)
                add_up(PAIRS - 1)

            @block.tensor
            def _(pe):
                def transposes(u, e, q, nh, n):
                    for ci in range(DC):
                        pe.wait_ge(x1_ready, val(NT * (2 * u + q) + 4 * nh + 4))
                        if not first(n):
                            pe.wait_ge(x1T_hi_ready, val(2 * n + ci - 1))
                        for k in range(4):
                            ins = nc.tensor.transpose(pT[ci][:, k * P:(k + 1) * P],
                                                      xin[:, 4 * nh + k, ci * P:(ci + 1) * P], ident[:, :])
                        ins.then_inc(x1_transposed, 1)

                def conv1(u, e, q, nh, n):
                    pe.wait_ge(x1T_lo_ready, val(n + 1))
                    for c in range(DC):
                        if not first(n):
                            pe.wait_ge(h_ready, val(2 * n + c - 1))
                        cs = slice(c * P, (c + 1) * P)
                        products(nc, pH[c][:, :], [(w1hi[:, i, cs], w1lo[:, i, cs], xhi[:, i, :], xlo[:, i, :])
                                                   for i in range(DC)]).then_inc(conv1_multiplied, 1)

                def conv2(u, s, n):
                    c, j, k, o = SUMS[n]
                    a = (s + k) % 2
                    if first(u):
                        pe.wait_ge(tap_lo_ready, n + 1)
                    if n in (4, 5):
                        pe.wait_ge(M_first_ready, val(2 * u + n - 3))
                    elif not (first(u) and n < 4):
                        pe.wait_ge(sums_ready, val(SOPS * (u if n >= 4 else u - 1) + SUM_END[(n - 4) % NS]))
                    for ci in range(DC):
                        pe.wait_ge(D_lo_ready, val(DC * (ND * u + k) + ci + 1))
                        steps = []
                        for L in range(3):
                            if (c, j, L) == (2, 3, 2):
                                continue
                            par, at = START[j][L]
                            cols = [d[:, a, 2 * ci:2 * ci + 2, par, at:at + H2 // 2] for d in (Dhi, Dlo)]
                            steps.append((whi[:, ci, c, j, L, :], wlo[:, ci, c, j, L, :], cols[0], cols[1]))
                        products(nc, pY[n % 4][:, :].rearrange("p (b w) -> p b w", b=2), steps,
                                 start=ci == 0, stop=ci == DC - 1).then_inc(conv2_chunk0_multiplied if ci == 0 else conv2_multiplied, 1)

                def body(u, s, nxt):
                    turned, convolved = {1: 0, 2: 1, 6: 2, 7: 3}, {2: 0, 4: 1, 7: 2, 8: 3}
                    for n in range(NS):
                        conv2(u, s, n)
                        if nxt and prepares and n in turned:
                            transposes(u + 1, *units(u + 1)[turned[n]])
                        if nxt and prepares and n in convolved:
                            conv1(u + 1, *units(u + 1)[convolved[n]])

                if prepares:
                    pe.wait_ge(constants_loaded, 32)
                    for unit in units(0):
                        transposes(0, *unit)
                        if unit[0] == 0:
                            pe.wait_ge(conv1_weights_split, 2)
                        conv1(0, *unit)
                schedule(body, pe)


def blocks_of(raw, pairs, c):
    g = pairs[:] if c == 1 else raw[:, :, c // 2:18:2, :]
    return g.rearrange("p c (l i) n -> p c l i n", i=3)


def taps_of(raw, pairs, tap, c):
    g = blocks_of(raw, pairs, c)
    return g[:, :, :, 0], g[:, :, :, 2], tap[:, 1], tap[:, 0]


def nodes_stage(nc, t):
    with ExitStack() as ctx:
        m = Space(nc, ctx, "n")
        SR = 12
        LR = 16
        XK = 2 * DC
        wihh = m.sb("wihh", [P, XK, 3 * D], F32R)
        wihl = m.sb("wihl", [P, XK, 3 * D], F32R)
        whhh = m.sb("whhh", [P, DC, 3 * D], F32R)
        whhl = m.sb("whhl", [P, DC, 3 * D], F32R)
        wmh = m.sb("wmh", [P, DC, D], F32R)
        wml = m.sb("wml", [P, DC, D], F32R)
        wseh = m.sb("wseh", [P, DC, SR], F32R)
        wsel = m.sb("wsel", [P, DC, SR], F32R)
        wse = m.sb("wse", [P, DC, SR])
        bse = m.sb("bse", [SR, 1])
        sel = m.sb("sel", [SK, P])
        rows = m.sb("rows", [LR, 6])
        bih = m.sb("bih", [P, 3 * D])
        bn_ = m.sb("bn", [P, 2 * D])
        bmsg = m.sb("bmsg", [P, 2 * D])
        half = m.sb("half", [P, 1])

        xstg = m.sb("xstg", [P, DC, H2])
        cstg = m.sb("cstg", [P, DC, H2])
        xhi = m.sb("xhi", [P, 2, DC, N], F32R)
        xlo = m.sb("xlo", [P, 2, DC, N], F32R)
        chi = m.sb("chi", [P, 2, DC, H2], F32R)
        clo = m.sb("clo", [P, 2, DC, H2], F32R)
        mhi = m.sb("mhi", [P, 2, DC, H2], F32R)
        mlo = m.sb("mlo", [P, 2, DC, H2], F32R)
        ss = m.sb("ss", [SK, 2, H2])
        vhi = m.sb("vhi", [LR, H2])
        vlo = m.sb("vlo", [LR, H2])
        vt = m.sb("vt", [LR, 2, H2])
        Lr = m.sb("Lr", [LR, N], F32R)
        Rr = m.sb("Rr", [LR, N], F32R)
        mt_ = m.sb("mt", [P, 2, 2 * D])
        msgh = m.sb("msgh", [P, NT, D], F32R)
        msgl = m.sb("msgl", [P, NT, D], F32R)
        adj = m.sb("adj", [P, 4, H2])
        E = m.sb("E", [P, 2, H2])
        A32 = m.sb("A32", [P, 2, H2])
        Ahi = m.sb("Ahi", [P, 3, H2], F32R)
        Alo = m.sb("Alo", [P, 3, H2], F32R)
        x1 = m.sb("x1", [P, 2, D])
        rz = m.sb("rz", [P, 2 * D])
        th = m.sb("th", [P, 2 * D])
        gn = m.sb("gn", [P, 2 * D])
        t1 = m.sb("t1", [P, D])
        t2 = m.sb("t2", [P, D])
        nn = m.sb("nn", [P, D])
        dd = m.sb("dd", [P, D])
        ee, ff = t1, t2
        res = m.sb("res", [P, D])
        stats = m.sb("stats", [P, 6])
        mv = m.sb("mv", [P, 2])
        mark = m.sb("mark", [P, 1])
        veps = m.sb("veps", [P, 1])
        rstd = m.sb("rstd", [P, 1])
        outt = m.sb("outt", [P, 2, D])

        pN = [m.bank(f"pN{k}") for k in range(2)]
        pD = [m.bank(f"pD{k}") for k in range(2)]
        pRZ = m.bank("pRZ")
        pG = m.bank("pG")
        pP = [m.bank(f"pP{k}") for k in range(2)]

        constants_loaded = m.sem("constants_loaded")
        weights_hi = m.sem("weights_hi")
        weights_lo = m.sem("weights_lo")
        biases_summed = m.sem("biases_summed")
        constants_set = m.sem("constants_set")
        x1T_loaded = m.sem("x1T_loaded")
        xcT_loaded = m.sem("xcT_loaded")
        x1T_hi_ready = m.sem("x1T_hi_ready")
        x1T_lo_ready = m.sem("x1T_lo_ready")
        xcT_hi_ready = m.sem("xcT_hi_ready")
        xcT_lo_ready = m.sem("xcT_lo_ready")
        s_multiplied = m.sem("s_multiplied")
        s_ready = m.sem("s_ready")
        s_squared = m.sem("s_squared")
        rows_multiplied = m.sem("rows_multiplied")
        rows_hi = m.sem("rows_hi")
        rows_lo = m.sem("rows_lo")
        rows_partial = m.sem("rows_partial")
        LR_ready = m.sem("LR_ready")
        msg_multiplied = m.sem("msg_multiplied")
        msg_biased = m.sem("msg_biased")
        msg_hi_ready = m.sem("msg_hi_ready")
        msg_lo_ready = m.sem("msg_lo_ready")
        adj_loaded = [m.sem(f"adj_loaded{k}") for k in range(4)]
        dist_multiplied = m.sem("dist_multiplied")
        E_ready = m.sem("E_ready")
        A_ready = m.sem("A_ready")
        A_hi_ready = m.sem("A_hi_ready")
        A_lo_ready = m.sem("A_lo_ready")
        A_multiplied = m.sem("A_multiplied")
        nmp_hi_ready = m.sem("nmp_hi_ready")
        nmp_lo_ready = m.sem("nmp_lo_ready")
        x1_loaded = [m.sem(f"x1_loaded{k}") for k in range(2)]
        rz_multiplied = m.sem("rz_multiplied")
        n_multiplied = m.sem("n_multiplied")
        rz_biased = m.sem("rz_biased")
        n_biased = m.sem("n_biased")
        rz_tanh = m.sem("rz_tanh")
        r_gh_n = m.sem("r_gh_n")
        n_argument = m.sem("n_argument")
        n_ready = m.sem("n_ready")
        x_minus_n = m.sem("x_minus_n")
        z_scaled = m.sem("z_scaled")
        update_ready = m.sem("update_ready")
        residual_ready = m.sem("residual_ready")
        stats_ready = m.sem("stats_ready")
        mean_var_ready = m.sem("mean_var_ready")
        var_eps_ready = m.sem("var_eps_ready")
        rstd_ready = m.sem("rstd_ready")
        out_ready = m.sem("out_ready")
        out_stored = [m.sem(f"out_stored{k}") for k in range(2)]

        flat = lambda x: x.rearrange("p a b -> p (a b)")
        W3 = 3 * D
        places = [flat(adj[:, 0:2])[:, 0:W3], flat(adj[:, 2:4])[:, 0:W3], flat(cstg[:])[:, 0:W3], flat(E[:])[:, 0:W3],
                  flat(A32[:])[:, 0:W3], flat(mt_[:])[:, 0:W3]]
        gate_weights = ([(t["w_ih"][:, k, :], wihh[:, k, :], wihl[:, k, :]) for k in range(XK)]
                        + [(t["w_hh"][:, k, :], whhh[:, k, :], whhl[:, k, :]) for k in range(DC)])
        WTS = ([(t["w_se"], wse[:], wseh[:], wsel[:])]
               + [(t["w_msg"][:, k, :], (rz, th)[k][:, 0:D], wmh[:, k, :], wml[:, k, :]) for k in range(DC)]
               + [(src, place, hi, lo) for (src, hi, lo), place in zip(gate_weights, places)])
        NW, NM = len(WTS), 1 + DC
        weights_staged = [m.sem(f"weights_staged{n}") for n in range(NW)]
        first = lambda j: isinstance(j, int) and j == 0

        STEPS = 2 * NT

        def schedule(body, eng):
            body(0, 0, False, True)
            with eng.Fori(0, B // 2 - 1) as turn:
                i = Turn(turn)
                for k in range(2):
                    body(2 * i + k + 1, 1 - k, True, True)
            body(B - 1, 1, True, False)

        def gate_tile(b, p, back=0):
            k = p - back - DC * 2
            return (b, k) if k >= 0 else (b - 1, k + NT)

        def has_gates(gates, p):
            return gates or p >= NT // 2


        with nc.Block() as block:
            @block.sync
            def _(sp):
                def stage(n):
                    src, place, _h, _l = WTS[n]
                    sp.dma_start(place, src).then_inc(weights_staged[n], 16)

                def load_xT(b, h):
                    if not (first(b) and h == 0):
                        sp.wait_ge(x1T_lo_ready, val(2 * b + h))
                    sp.dma_start(xstg[:], t["x1T"][val(b)][:, :, h * H2:(h + 1) * H2]).then_inc(x1T_loaded, 16)

                def load_xc(b, h):
                    if not (first(b) and h == 0):
                        sp.wait_ge(xcT_lo_ready, val(2 * b + h))
                    sp.dma_start(cstg[:], t["xcT"][val(b)][:, :, h * H2:(h + 1) * H2]).then_inc(xcT_loaded, 16)

                def load_adj(b, n):
                    h, k = divmod(n, NT)
                    if not (first(b) and n < 4):
                        sp.wait_ge(A_ready, val(STEPS * b + n - 3))
                    sp.dma_start(adj[:, n % 4, :], t["adjT"][val(b)][:, k, h * H2:(h + 1) * H2]).then_inc(adj_loaded[n % 4], 16)

                def load_x1(g_b, g_k):
                    if not (first(g_b) and g_k < 2):
                        sp.wait_ge(residual_ready, val(NT * g_b + g_k - 1))
                    sp.dma_start(x1[:, g_k % 2, :], t["x1"][val(g_b)][:, g_k, :]).then_inc(x1_loaded[g_k % 2], 16)

                def store(g_b, g_k):
                    sp.wait_ge(out_ready, val(NT * g_b + g_k + 1))
                    sp.dma_start(t["out"][val(g_b)][:, g_k, :], outt[:, g_k % 2, :]).then_inc(out_stored[g_k % 2], 16)

                def body(b, s, gates, nxt):
                    for n in range(STEPS):
                        p = n // 2
                        if n + 2 < STEPS:
                            load_adj(b, n + 2)
                        elif nxt:
                            load_adj(b + 1, n + 2 - STEPS)
                        if n % NT == 0:
                            load_xc(b, n // NT)
                        if nxt and n in (7, 9):
                            load_xT(b + 1, (n - 7) // 2)
                        if n % 2 == 0 and has_gates(gates, p):
                            load_x1(*gate_tile(b, p))
                        if n % 2 == 1 and (gates or p >= NT // 2 + 2):
                            store(*gate_tile(b, p, 2))

                for n in range(NM):
                    stage(n)
                for dst, src in ((bse[:], t["b_se"]), (sel[:], t["sel"]),
                                 (rows[:], t["rows"]), (bih[:], t["b_ih"]), (places[-1], t["b_hh"]),
                                 (bmsg[:, 0:D], t["b_msg"]), (bmsg[:, D:2 * D], t["b_msg"])):
                    sp.dma_start(dst, src).then_inc(constants_loaded, 16)
                load_xT(0, 0)
                for n in range(NM, NW - 1):
                    stage(n)
                sp.wait_ge(biases_summed, 3)
                stage(NW - 1)
                load_xT(0, 1)
                sp.wait_ge(weights_lo, NM + 3)
                for n in range(2):
                    load_adj(0, n)
                schedule(body, sp)
                for k in range(2, NT):
                    if k >= 4:
                        load_x1(B - 1, k)
                    store(B - 1, k)
                for k in range(2):
                    sp.wait_ge(out_stored[k], 16 * B * NT // 2)

            @block.gpsimd
            def _(pool):
                nc.gpsimd.memset(half[:, :], -0.5).then_inc(constants_set, 1)
                nc.gpsimd.memset(ss[:, :, :], 0.0).then_inc(constants_set, 1)
                pool.wait_ge(constants_set, 2)

                def split_x(b, s, h):
                    pool.wait_ge(x1T_hi_ready, val(2 * b + h + 1))
                    nc.gpsimd.tensor_tensor(xlo[:, s, :, h * H2:(h + 1) * H2], xstg[:],
                                            xhi[:, s, :, h * H2:(h + 1) * H2].bitcast(F32), ALU.subtract).then_inc(x1T_lo_ready, 1)

                def split_c(b, h):
                    pool.wait_ge(xcT_hi_ready, val(2 * b + h + 1))
                    nc.gpsimd.tensor_tensor(clo[:, h], cstg[:], chi[:, h].bitcast(F32), ALU.subtract).then_inc(xcT_lo_ready, 1)

                def low_A(b, n):
                    pool.wait_ge(A_hi_ready, val(STEPS * b + n + 1))
                    a = n % 3
                    nc.gpsimd.tensor_tensor(Alo[:, a], A32[:, n % 2], Ahi[:, a].bitcast(F32),
                                            ALU.subtract).then_inc(A_lo_ready, 1)

                def rstd_of(g_b, g_k):
                    pool.wait_ge(var_eps_ready, val(NT * g_b + g_k + 1))
                    nc.gpsimd.tensor_tensor(rstd[:, :], veps[:, :], half[:, :], ALU.pow).then_inc(rstd_ready, 1)

                def body(b, s, gates, nxt):
                    for n in range(STEPS):
                        p = n // 2
                        low_A(b, n)
                        if n % NT == 3:
                            split_c(b, n // NT)
                        if nxt and n in (9, 11):
                            split_x(b + 1, 1 - s, (n - 9) // 2)
                        if n % 2 == 1 and has_gates(gates, p - 1):
                            rstd_of(*gate_tile(b, p, 1))

                for h in range(2):
                    split_x(0, 0, h)
                schedule(body, pool)
                for k in range(3, NT):
                    rstd_of(B - 1, k)

            @block.scalar
            def _(act):
                def weights_high(n):
                    _s, place, hi, _l = WTS[n]
                    act.wait_ge(weights_staged[n], 16)
                    nc.scalar.copy(hi, place).then_inc(weights_hi, 1)

                def split_x(b, s, h):
                    act.wait_ge(x1T_loaded, val(32 * b + 16 * h + 16))
                    if h == 0 and not (isinstance(b, int) and b < 2):
                        act.wait_ge(n_multiplied, val(8 * b - 8))
                    nc.scalar.copy(xhi[:, s, :, h * H2:(h + 1) * H2], xstg[:]).then_inc(x1T_hi_ready, 1)

                def bias_s(b):
                    for h in range(2):
                        act.wait_ge(s_multiplied, val(2 * b + h + 1))
                        if not first(b):
                            act.wait_ge(rows_multiplied, val(2 * b - 1 + h))
                        nc.scalar.activation(ss[0:SR, h, :], pP[h][0:SR, :], ACT.Identity, bias=bse[:, :]).then_inc(s_ready, 1)

                def hi_rows(b, h):
                    act.wait_ge(rows_multiplied, val(2 * b + h + 1))
                    if not (first(b) and h == 0):
                        act.wait_ge(LR_ready, val(4 * b + 2 * h))
                    nc.scalar.copy(vhi[:, :].bitcast(F32R), pP[h][0:LR, :]).then_inc(rows_hi, 1)

                def hi_msg(b):
                    for k in range(NT // 2):
                        act.wait_ge(msg_biased, val(4 * b + k + 1))
                        high = msgh[:, 2 * k:2 * k + 2, :].rearrange("p a b -> p (a b)")
                        nc.scalar.activation(high, mt_[:, k % 2, :], ACT.Relu).then_inc(msg_hi_ready, 1)

                def exps(b, n):
                    act.wait_ge(dist_multiplied, val(STEPS * b + n + 1))
                    if not (first(b) and n < 2):
                        act.wait_ge(A_ready, val(STEPS * b + n - 1))
                    nc.scalar.activation(E[:, n % 2], pD[n % 2][:, :], ACT.Exp).then_inc(E_ready, 1)

                def hi_A(b, n):
                    act.wait_ge(A_ready, val(STEPS * b + n + 1))
                    if n >= 3:
                        act.wait_ge(A_multiplied, val(STEPS * b + n - 2))
                    elif not first(b):
                        act.wait_ge(A_multiplied, val(STEPS * b))
                    nc.scalar.copy(Ahi[:, n % 3], A32[:, n % 2]).then_inc(A_hi_ready, 1)

                def hi_c(b, h):
                    act.wait_ge(xcT_loaded, val(32 * b + 16 * h + 16))
                    if not first(b):
                        act.wait_ge(n_multiplied, val(8 * b - 8 + 4 * h + 4))
                    nc.scalar.copy(chi[:, h], cstg[:]).then_inc(xcT_hi_ready, 1)

                def hi_n(b, h):
                    act.wait_ge(A_multiplied, val(16 * b + 8 * h + 8))
                    if not first(b):
                        act.wait_ge(n_multiplied, val(8 * b - 8 + 4 * h + 4))
                    for c in range(DC):
                        nc.scalar.copy(mhi[:, h, c, :], pN[c][:, :]).then_inc(nmp_hi_ready, 1)

                def tanh_rz(g_b, g_k):
                    g = NT * g_b + g_k
                    act.wait_ge(rz_biased, val(g + 1))
                    if not (first(g_b) and g_k == 0):
                        act.wait_ge(z_scaled, val(g))
                    nc.scalar.activation(th[:, :], rz[:, :], ACT.Tanh, scale=0.5).then_inc(rz_tanh, 1)

                def tanh_n(g_b, g_k):
                    g = NT * g_b + g_k
                    act.wait_ge(n_argument, val(g + 1))
                    if not (first(g_b) and g_k == 0):
                        act.wait_ge(update_ready, val(g))
                    nc.scalar.activation(nn[:, :], t2[:, :], ACT.Tanh).then_inc(n_ready, 1)

                def body(b, s, gates, nxt):
                    hi_A(b, 0)
                    for n in range(STEPS):
                        p = n // 2
                        if n + 2 < STEPS:
                            exps(b, n + 2)
                        if n + 1 < STEPS:
                            hi_A(b, n + 1)
                        if n % NT == 2:
                            hi_c(b, n // NT)
                        if nxt and n in (8, 10):
                            split_x(b + 1, 1 - s, (n - 8) // 2)
                        if n == NT - 1:
                            hi_n(b, 0)
                        if nxt and n == 12:
                            bias_s(b + 1)
                        if nxt and n in (13, 14):
                            hi_rows(b + 1, n - 13)
                        if has_gates(gates, p):
                            (tanh_n if n % 2 else tanh_rz)(*gate_tile(b, p))
                    hi_n(b, 1)
                    if nxt:
                        exps(b + 1, 0)
                        exps(b + 1, 1)
                        hi_msg(b + 1)

                for n in range(NM):
                    weights_high(n)
                split_x(0, 0, 0)
                for n in range(NM, NW):
                    weights_high(n)
                split_x(0, 0, 1)
                act.wait_ge(constants_loaded, 112)
                act.wait_ge(weights_lo, NW)
                act.wait_ge(constants_set, 2)
                bias_s(0)
                hi_rows(0, 0)
                hi_rows(0, 1)
                exps(0, 0)
                exps(0, 1)
                hi_msg(0)
                schedule(body, act)
                for k in range(4, NT):
                    tanh_rz(B - 1, k)
                    tanh_n(B - 1, k)

            @block.vector
            def _(v):
                def weights_low(n):
                    _s, place, hi, lo = WTS[n]
                    v.wait_ge(weights_hi, n + 1)
                    nc.vector.tensor_tensor(lo, place, hi.bitcast(F32), ALU.subtract).then_inc(weights_lo, 1)

                for n in range(NM):
                    weights_low(n)
                v.wait_ge(constants_loaded, 112)
                nc.vector.tensor_tensor(bih[:, 0:2 * D], bih[:, 0:2 * D], places[-1][:, 0:2 * D], ALU.add).then_inc(biases_summed, 1)
                nc.vector.tensor_copy(bn_[:, D:2 * D], places[-1][:, 2 * D:3 * D]).then_inc(biases_summed, 1)
                nc.vector.tensor_copy(bn_[:, 0:D], bih[:, 2 * D:3 * D]).then_inc(biases_summed, 1)
                v.wait_ge(biases_summed, 3)
                for n in range(NM, NW):
                    weights_low(n)

                def operands(b, h):
                    sl = slice(h * H2, (h + 1) * H2)
                    v.wait_ge(rows_hi, val(2 * b + h + 1))
                    nc.vector.tensor_tensor(vlo[:, :], pP[h][0:LR, :], vhi[:, :], ALU.subtract).then_inc(rows_lo, 1)
                    nc.vector.tensor_scalar(vt[:, 0, :], vhi[:, :], rows[:, 0:1], rows[:, 2:3], ALU.mult, ALU.add).then_inc(rows_partial, 1)
                    nc.vector.tensor_scalar(vt[:, 1, :], vhi[:, :], rows[:, 3:4], rows[:, 5:6], ALU.mult, ALU.add).then_inc(rows_partial, 1)
                    v.wait_ge(rows_lo, val(2 * b + h + 1))
                    v.wait_ge(rows_partial, val(4 * b + 2 * h + 2))
                    if not first(b):
                        v.wait_ge(dist_multiplied, val(16 * b))
                    nc.vector.scalar_tensor_tensor(Lr[:, sl], vlo[:, :], rows[:, 1:2], vt[:, 0, :], ALU.mult, ALU.add).then_inc(LR_ready, 1)
                    nc.vector.scalar_tensor_tensor(Rr[:, sl], vlo[:, :], rows[:, 4:5], vt[:, 1, :], ALU.mult, ALU.add).then_inc(LR_ready, 1)
                    v.wait_ge(LR_ready, val(4 * b + 2 * h + 2))

                def square_s(b):
                    for h in range(2):
                        v.wait_ge(s_ready, val(2 * b + h + 1))
                        if not first(b):
                            v.wait_ge(rows_multiplied, val(2 * b - 1 + h))
                        nc.vector.tensor_tensor(ss[SQ:SQ + SR, h, :], ss[0:SR, h, :], ss[0:SR, h, :], ALU.mult).then_inc(s_squared, 1)

                def low_msg(b, between=lambda: None):
                    for k in range(NT // 2 + 1):
                        if k == 1:
                            between()
                        if k < NT // 2:
                            v.wait_ge(msg_multiplied, val(4 * b + k + 1))
                            if not (first(b) and k < 2):
                                v.wait_ge(msg_lo_ready, val(4 * b + k - 1))
                            nc.vector.tensor_tensor(mt_[:, k % 2, :], pP[k % 2][:, :], bmsg[:, :], ALU.add).then_inc(msg_biased, 1)
                        if k:
                            v.wait_ge(msg_hi_ready, val(4 * b + k))
                            low = msgl[:, 2 * k - 2:2 * k, :].rearrange("p a b -> p (a b)")
                            high = msgh[:, 2 * k - 2:2 * k, :].rearrange("p a b -> p (a b)").bitcast(F32)
                            nc.vector.scalar_tensor_tensor(low, mt_[:, (k - 1) % 2, :], 0.0, high,
                                                           ALU.max, ALU.subtract).then_inc(msg_lo_ready, 1)
                        if k in (1, 2):
                            mask(b, k - 1)

                def mask(b, n):
                    v.wait_ge(E_ready, val(STEPS * b + n + 1))
                    v.wait_ge(adj_loaded[n % 4], val(64 * b + 16 * (n // 4) + 16))
                    if not (first(b) and n < 2):
                        v.wait_ge(A_lo_ready, val(STEPS * b + n - 1))
                    nc.vector.tensor_tensor(A32[:, n % 2], E[:, n % 2], adj[:, n % 4], ALU.mult).then_inc(A_ready, 1)

                def low_n(b, h):
                    for c in range(DC):
                        v.wait_ge(nmp_hi_ready, val(4 * b + 2 * h + c + 1))
                        nc.vector.tensor_tensor(mlo[:, h, c, :], pN[c][:, :], mhi[:, h, c, :].bitcast(F32), ALU.subtract).then_inc(nmp_lo_ready, 1)

                def bias_rz(g_b, g_k):
                    g = NT * g_b + g_k
                    v.wait_ge(rz_multiplied, val(g + 1))
                    if not (first(g_b) and g_k == 0):
                        v.wait_ge(rz_tanh, val(g))
                    nc.vector.tensor_tensor(rz[:, :], pRZ[:, :], bih[:, 0:2 * D], ALU.add).then_inc(rz_biased, 1)

                def n_arg(g_b, g_k):
                    g = NT * g_b + g_k
                    v.wait_ge(n_multiplied, val(g + 1))
                    nc.vector.tensor_tensor(gn[:, :], pG[:, :], bn_[:, :], ALU.add).then_inc(n_biased, 1)
                    v.wait_ge(n_biased, val(g + 1))
                    v.wait_ge(rz_tanh, val(g + 1))
                    nc.vector.scalar_tensor_tensor(t1[:, :], th[:, 0:D], 1.0, gn[:, D:2 * D], ALU.add, ALU.mult).then_inc(r_gh_n, 1)
                    v.wait_ge(r_gh_n, val(g + 1))
                    nc.vector.scalar_tensor_tensor(t2[:, :], t1[:, :], 0.5, gn[:, 0:D], ALU.mult, ALU.add).then_inc(n_argument, 1)

                def update(g_b, g_k):
                    g = 8 * g_b + g_k
                    v.wait_ge(n_ready, val(g + 1))
                    v.wait_ge(x1_loaded[g_k % 2], val(64 * g_b + 16 * (g_k // 2) + 16))
                    nc.vector.tensor_tensor(dd[:, :], x1[:, g_k % 2, :], nn[:, :], ALU.subtract).then_inc(x_minus_n, 1)
                    v.wait_ge(x_minus_n, val(g + 1))
                    nc.vector.scalar_tensor_tensor(ee[:, :], th[:, D:2 * D], 1.0, dd[:, :], ALU.add, ALU.mult).then_inc(z_scaled, 1)
                    v.wait_ge(z_scaled, val(g + 1))
                    nc.vector.scalar_tensor_tensor(ff[:, :], ee[:, :], 0.5, nn[:, :], ALU.mult, ALU.add).then_inc(update_ready, 1)
                    v.wait_ge(update_ready, val(g + 1))
                    nc.vector.tensor_tensor(res[:, :], ff[:, :], x1[:, g_k % 2, :], ALU.add).then_inc(residual_ready, 1)
                    v.wait_ge(residual_ready, val(g + 1))
                    nc.vector.bn_stats(stats[:, :], res[:, :]).then_inc(stats_ready, 1)
                    v.wait_ge(stats_ready, val(g + 1))
                    nc.vector.memset(mark[:, :], 0.0)
                    nc.vector.bn_aggr(mv[:, :], stats[:, :]).then_inc(mean_var_ready, 1)
                    v.wait_ge(mean_var_ready, val(g + 1))
                    nc.vector.tensor_scalar(veps[:, :], mv[:, 1:2], EPS, None, ALU.add).then_inc(var_eps_ready, 1)

                def norm(g_b, g_k):
                    g = 8 * g_b + g_k
                    v.wait_ge(rstd_ready, val(g + 1))
                    if not (first(g_b) and g_k < 2):
                        v.wait_ge(out_stored[g_k % 2], val(64 * g_b + 16 * (g_k // 2)))
                    nc.vector.tensor_scalar(outt[:, g_k % 2, :], res[:, :], mv[:, 0:1], rstd[:, :],
                                            ALU.subtract, ALU.mult).then_inc(out_ready, 1)

                def body(b, s, gates, nxt):
                    for n in range(STEPS):
                        p = n // 2
                        if n + 2 < STEPS:
                            mask(b, n + 2)
                        if nxt and n == 12:
                            square_s(b + 1)
                        if has_gates(gates, p - 1):
                            (norm if n % 2 else update)(*gate_tile(b, p, 1))
                        if n == NT - 1:
                            low_n(b, 0)
                        if nxt and n == 14:
                            operands(b + 1, 1)
                        if has_gates(gates, p):
                            (n_arg if n % 2 else bias_rz)(*gate_tile(b, p))
                        if nxt and n == 13:
                            operands(b + 1, 0)
                    if nxt:
                        low_msg(b + 1, lambda: low_n(b, 1))
                    else:
                        low_n(b, 1)

                square_s(0)
                operands(0, 0)
                operands(0, 1)
                low_msg(0)
                schedule(body, v)
                update(B - 1, 3)
                norm(B - 1, 3)
                for k in range(4, NT):
                    bias_rz(B - 1, k)
                    n_arg(B - 1, k)
                    update(B - 1, k)
                    norm(B - 1, k)

            @block.tensor
            def _(pe):
                pe.wait_ge(weights_lo, NM)
                pe.wait_ge(constants_loaded, 112)

                def multiply_s(b, s):
                    for h in range(2):
                        sl = slice(h * H2, (h + 1) * H2)
                        pe.wait_ge(x1T_lo_ready, val(2 * b + h + 1))
                        if h == 0 and not first(b):
                            pe.wait_ge(msg_biased, val(4 * b))
                        products(nc, pP[h][0:SR, :], [(wseh[:, c, :], wsel[:, c, :], xhi[:, s, c, sl], xlo[:, s, c, sl])
                                                      for c in range(DC)]).then_inc(s_multiplied, 1)

                def multiply_rows(b):
                    for h in range(2):
                        pe.wait_ge(s_ready, val(2 * b + h + 1))
                        pe.wait_ge(s_squared, val(2 * b + h + 1))
                        nc.tensor.matmul(pP[h][:, :], sel[:, :], ss[:, h, :], start=True, stop=True).then_inc(rows_multiplied, 1)

                def multiply_msg(b, s):
                    for k in range(NT):
                        pair, half = k // 2, slice(k % 2 * D, (k % 2 + 1) * D)
                        if k in (0, 2):
                            pe.wait_ge(rows_lo, val(2 * b + pair + 1))
                        elif k % 2 == 0:
                            pe.wait_ge(msg_biased, val(4 * b + pair - 1))
                        ins = products(nc, pP[pair % 2][:, half], [
                            (xhi[:, s, c, k * P:(k + 1) * P], xlo[:, s, c, k * P:(k + 1) * P], wmh[:, c, :], wml[:, c, :])
                            for c in range(DC)])
                        if k % 2:
                            ins.then_inc(msg_multiplied, 1)

                def dist(b, n):
                    h, k = divmod(n, NT)
                    if n == 0:
                        pe.wait_ge(LR_ready, val(4 * b + 4))
                    if not (first(b) and n < 2):
                        pe.wait_ge(E_ready, val(STEPS * b + n - 1))
                    nc.tensor.matmul(pD[n % 2][:, :], Lr[:, k * P:(k + 1) * P], Rr[:, h * H2:(h + 1) * H2],
                                     start=True, stop=True).then_inc(dist_multiplied, 1)

                def gather(b, n):
                    h, k = divmod(n, NT)
                    pe.wait_ge(A_lo_ready, val(STEPS * b + n + 1))
                    if h == 0:
                        pe.wait_ge(msg_lo_ready, val(4 * b + k // 2 + 1))
                    if k == 0 and not (first(b) and h == 0):
                        pe.wait_ge(nmp_lo_ready, val(4 * b + 2 * h))
                    a = n % 3
                    for c in range(DC):
                        cs = slice(c * P, (c + 1) * P)
                        ins = products(nc, pN[c][:, :], [(msgh[:, k, cs], msgl[:, k, cs], Ahi[:, a], Alo[:, a])],
                                       start=k == 0, stop=k == NT - 1)
                    ins.then_inc(A_multiplied, 1)

                def operands(g_b, s, g_k):
                    h, k = divmod(g_k, NT // 2)
                    cs, ns = slice(k * P, (k + 1) * P), slice(g_k * P, (g_k + 1) * P)
                    return ([(xhi[:, s, c, ns], xlo[:, s, c, ns]) for c in range(DC)],
                            [(chi[:, h, c, cs], clo[:, h, c, cs]) for c in range(DC)]
                            + [(mhi[:, h, c, cs], mlo[:, h, c, cs]) for c in range(DC)])

                def gate_rz(g_b, s, g_k):
                    h, k = divmod(g_k, NT // 2)
                    xs, xin = operands(g_b, s, g_k)
                    cols = slice(0, 2 * D)
                    if first(g_b) and g_k == 0:
                        pe.wait_ge(weights_lo, NW)
                    if k == 0:
                        pe.wait_ge(xcT_lo_ready, val(2 * g_b + h + 1))
                    if not (first(g_b) and g_k == 0):
                        pe.wait_ge(rz_biased, val(NT * g_b + g_k))
                    parts = ([(a, l, whhh[:, c, cols], whhl[:, c, cols]) for c, (a, l) in enumerate(xs)]
                             + [(a, l, wihh[:, c, cols], wihl[:, c, cols]) for c, (a, l) in enumerate(xin)])
                    products(nc, pRZ[:, :], parts[:2 * DC], stop=False)
                    if k == 0:
                        pe.wait_ge(nmp_lo_ready, val(4 * g_b + 2 * h + 2))
                    products(nc, pRZ[:, :], parts[2 * DC:], start=False).then_inc(rz_multiplied, 1)

                def gate_n(g_b, s, g_k):
                    xs, xin = operands(g_b, s, g_k)
                    cols = slice(2 * D, 3 * D)
                    if not (first(g_b) and g_k == 0):
                        pe.wait_ge(n_biased, val(NT * g_b + g_k))
                    products(nc, pG[:, 0:D], [(a, l, wihh[:, c, cols], wihl[:, c, cols]) for c, (a, l) in enumerate(xin)])
                    products(nc, pG[:, D:2 * D], [(a, l, whhh[:, c, cols], whhl[:, c, cols])
                                                  for c, (a, l) in enumerate(xs)]).then_inc(n_multiplied, 1)

                def body(b, s, gates, nxt):
                    for n in range(STEPS):
                        p = n // 2
                        if n + 2 < STEPS:
                            dist(b, n + 2)
                        if has_gates(gates, p):
                            g_b, g_k = gate_tile(b, p)
                            (gate_n if n % 2 else gate_rz)(g_b, s if p >= NT // 2 else 1 - s, g_k)
                        gather(b, n)
                        if nxt and n == 11:
                            multiply_s(b + 1, 1 - s)
                        if nxt and n == 12:
                            multiply_rows(b + 1)
                    if nxt:
                        dist(b + 1, 0)
                        dist(b + 1, 1)
                        multiply_msg(b + 1, 1 - s)

                multiply_s(0, 0)
                multiply_rows(0)
                dist(0, 0)
                dist(0, 1)
                multiply_msg(0, 0)
                schedule(body, pe)
                for k in range(4, NT):
                    gate_rz(B - 1, 1, k)
                    gate_n(B - 1, 1, k)


INPUTS = ["x", "adjT", "l0_x", "l0_adj", "l0_gmask", "l0_geye", "l0_member", "l0_fw", "ident", "l0_w1", "l0_b1",
          "l0_w2", "l0_b2", "conv1_w", "conv2_w", "bn", "w_ih", "w_hh", "w_msg", "w_se", "b_se", "sel",
          "rows", "b_ih", "b_hh", "b_msg"]


def build(nc, t):
    t["fused"] = nc.dram_tensor("fused_scratch", (B, GN, D), F32, kind="Internal").ap()
    t["x1"] = nc.dram_tensor("x1_scratch", (B, P, NT, D), F32, kind="Internal").ap()
    t["x1T"] = nc.dram_tensor("x1T_scratch", (B, P, DC, N), F32, kind="Internal").ap()
    t["h4"] = nc.dram_tensor("h_scratch", (B // 2, P, 2 * DC, 4, HQ), F32, kind="Internal").ap()
    t["xcT"] = nc.dram_tensor("xcT_scratch", (B, P, DC, N), F32, kind="Internal").ap()
    groups_stage(nc, t)
    for co in range(DC):
        conv_stage(nc, t, co)
    nodes_stage(nc, t)


def constants():
    gmask = np.zeros((P, NG, P), np.float32)
    geye = np.zeros((P, NG, P), np.float32)
    member = np.zeros((P, NG), np.float32)
    for g, idx in enumerate(GROUPS):
        for q in range(GB):
            rows = GP * q + np.array(idx)
            gmask[np.ix_(rows, [g], rows)] = 1
            geye[rows, g, rows] = 1
            member[rows, g] = 1
    sel = np.zeros((SK, P), np.float32)
    sel[np.arange(12), np.arange(12)] = 1
    sel[SQ:SQ + 3, 12:16] = -1
    rows = np.zeros((16, 6), np.float32)
    rows[0:6, 0] = 1
    rows[6:12, 1] = 1
    rows[12:14, 2] = 1
    rows[14, 0] = rows[15, 1] = 1
    rows[[0, 1, 2, 6, 7, 8], 3] = 2
    rows[[3, 4, 5, 9, 10, 11], 4] = 2
    rows[12, 3] = rows[13, 4] = 1
    rows[14:16, 5] = 1
    return {"l0_gmask": gmask, "l0_geye": geye, "l0_member": member, "ident": np.eye(P, dtype=np.float32),
            "sel": sel, "rows": rows}


def layout(i):
    def parts(w):
        return np.ascontiguousarray(w.reshape(-1, P, w.shape[-1]).transpose(1, 0, 2))

    def rep(v):
        return np.ascontiguousarray(np.broadcast_to(v, (P,) + v.shape))

    x, adj = i["x"], i["adj"]
    l0_x = np.zeros((GT, GB, GP, D), np.float32)
    l0_x[:, :, :GN] = x[:, :GN].reshape(GT, GB, GN, D)
    l0_adj = np.zeros((GT, GB, GP, GB, GP), np.float32)
    for q in range(GB):
        l0_adj[:, q, :GN, q, :GN] = adj[:, :GN, :GN].reshape(GT, GB, GN, GN)[:, q]
    bn = np.stack([np.stack([i[f"L1_gnn_bn{k}_{f}"].reshape(DC, P) for f in "gbmv"]) for k in (1, 2)])
    w_se = np.concatenate([i["L1_gnn_w_se"].T] * 4, axis=1)
    b_se = np.concatenate([i["L1_gnn_b_se"]] * 4)
    return {
        "x": np.ascontiguousarray(x.reshape(B, NT, P, D).transpose(0, 2, 1, 3)),
        "adjT": np.ascontiguousarray(adj.transpose(0, 2, 1).reshape(B, NT, P, N).transpose(0, 2, 1, 3)),
        "l0_x": np.ascontiguousarray(l0_x.reshape(GT, P, D).transpose(1, 0, 2)),
        "l0_adj": np.ascontiguousarray(l0_adj.reshape(GT, P, P).transpose(1, 0, 2)),
        "l0_fw": rep(i["L0_gnn_fusion_w"]),
        "l0_w1": np.ascontiguousarray(i["L0_gnn_W1"].reshape(NG, DC, P, DH).transpose(2, 0, 1, 3)),
        "l0_w2": np.ascontiguousarray(i["L0_gnn_W2"].reshape(NG, HC, P, D).transpose(2, 0, 1, 3)),
        "l0_b1": np.ascontiguousarray(i["L0_gnn_b1"].reshape(NG, HC, P).transpose(2, 0, 1)),
        "l0_b2": rep(i["L0_gnn_b2"]),
        "conv1_w": parts(i["L1_gnn_conv1_w"][:, :, 0].T),
        "conv2_w": np.ascontiguousarray(i["L1_gnn_conv2_w"].transpose(1, 2, 0).reshape(DC, P, TAPS, D).transpose(1, 0, 2, 3)),
        "bn": np.ascontiguousarray(bn.transpose(3, 0, 1, 2)),
        "w_ih": parts(i["L1_gnn_w_ih"].T), "w_hh": parts(i["L1_gnn_w_hh"].T), "w_msg": parts(i["L1_gnn_w_msg"].T),
        "w_se": parts(w_se), "b_se": b_se.reshape(-1, 1),
        "b_ih": rep(i["L1_gnn_b_ih"]), "b_hh": rep(i["L1_gnn_b_hh"]), "b_msg": rep(i["L1_gnn_b_msg"]),
    }


def kernel(**inputs):
    import concourse.bacc as bacc
    from concourse.bass_utils import run_bass_kernel_spmd

    inputs = {k: np.asarray(v) for k, v in inputs.items()}
    arrays = {**layout(inputs), **constants()}
    arrays = {f"in_{k}": np.ascontiguousarray(arrays[k]) for k in INPUTS}
    nc = bacc.Bacc("TRN2", target_bir_lowering=False, num_devices=1)
    t = {k: nc.dram_tensor(f"in_{k}", arrays[f"in_{k}"].shape, F32, kind="ExternalInput").ap() for k in INPUTS}
    t["out"] = nc.dram_tensor("out", (B, P, NT, D), F32, kind="ExternalOutput").ap()
    build(nc, t)
    r = run_bass_kernel_spmd(nc, [arrays], core_ids=[0])
    out = r.results[0]["out"]
    return np.ascontiguousarray(out.transpose(0, 2, 1, 3).reshape(B, N, D))
```
